# Optimizing a Trainium2 kernel written in Bass

```python
import numpy as np
import jax
import jax.numpy as jnp

def _softmax(x, axis=-1):
    return jax.nn.softmax(x, axis=axis)

def _gelu(x):
    return jax.nn.gelu(x, approximate=True)

def _silu(x):
    return jax.nn.silu(x)

def _sigmoid(x):
    return jax.nn.sigmoid(x)

def _layernorm(x, axis=-1, eps=1e-05):
    m = jnp.mean(x, axis=axis, keepdims=True)
    v = jnp.var(x, axis=axis, keepdims=True)
    return (x - m) / jnp.sqrt(v + eps)

def _scatter_add(tgt, idx, src, axis=0):
    return tgt.at[idx].add(src)

def _segment_sum(src, seg, n):
    return jax.ops.segment_sum(src, seg, n)
kernel_name = 'mk_decoder_postln_d2_seqx_r8_aaef60'

def setup_inputs(seed: int=0):
    np.random.seed(seed)
    _w = jnp.asarray

    def _rec_inputs():
        import jax
        import jax.numpy as jnp
        _rk = jax.random.key(seed)
        x = -0.000125 + 0.9999 * jax.random.normal(jax.random.fold_in(_rk, 1), (8, 256, 128), jnp.float32)
        _lenS = 256 - jax.random.randint(jax.random.fold_in(_rk, 7), (8,), 0, max(1, 256 // 4) + 1, jnp.int32)
        _lenS2 = 64 - jax.random.randint(jax.random.fold_in(_rk, 8), (8,), 0, max(1, 64 // 4) + 1, jnp.int32)
        _ctx_1024P = jax.random.normal(jax.random.fold_in(_rk, 11), (8, 16, 128), jnp.float32)
        _ctx_1024c = jax.random.dirichlet(jax.random.fold_in(_rk, 511), 0.3 * jnp.ones((16,), jnp.float32), (8, 64))
        _ctx_1024t = jnp.einsum('bsk,bkd->bsd', _ctx_1024c, _ctx_1024P)
        _ctx_1024t = _ctx_1024t * jax.lax.rsqrt(jnp.mean(jnp.square(_ctx_1024t)) + 1e-12) * 0.953939
        ctx_1024 = -1.52775e-05 + 0.999936 * (_ctx_1024t + 0.3 * jax.random.normal(jax.random.fold_in(_rk, 611), (8, 64, 128), jnp.float32))
        return (x, ctx_1024)
    x, ctx_1024 = _rec_inputs()

    def _L0_attn_setup():
        import jax, jax.numpy as jnp
        import numpy as np
        BATCH, SEQ, D_EMBED, N_HEADS, D_HEAD = (1, 256, 128, 16, 64)
        MASK_VAL = 10000000000.0
        key = jax.random.key(seed)
        ks = jax.random.split(key, 5)
        s = 1.0 / np.sqrt(D_EMBED).astype(np.float32)
        return {'x': jax.random.normal(ks[0], (BATCH, SEQ, D_EMBED), jnp.float32), 'W_Q': jax.random.normal(ks[1], (N_HEADS, D_HEAD, D_EMBED), jnp.float32) * s, 'W_K': jax.random.normal(ks[2], (N_HEADS, D_HEAD, D_EMBED), jnp.float32) * s, 'W_V': jax.random.normal(ks[3], (N_HEADS, D_HEAD, D_EMBED), jnp.float32) * s, 'W_O': jax.random.normal(ks[4], (N_HEADS, D_EMBED, D_HEAD), jnp.float32) * s}
    _L0_attn_all = _L0_attn_setup()
    _L0_attn_in = {k: v for k, v in _L0_attn_all.items() if k in ('W_Q', 'W_K', 'W_V', 'W_O')}
    del _L0_attn_all

    def _L0_xattn_setup():
        import jax, jax.numpy as jnp
        import numpy as np
        HEAD = 16
        EMB = 128
        B, S = (8, 512)

        def _proj_heads(x, W, b, H, d):
            Bx, Sx, _ = x.shape
            y = x @ W.T + b
            return y.reshape(Bx, Sx, H, d).transpose(0, 2, 1, 3)
        key = jax.random.key(seed)
        ks = jax.random.split(key, 11)
        scale = 1.0 / np.sqrt(EMB).astype(np.float32)
        inp = {'query': jax.random.normal(ks[0], (B, S, EMB), jnp.float32), 'key': jax.random.normal(ks[1], (B, S, EMB), jnp.float32), 'value': jax.random.normal(ks[2], (B, S, EMB), jnp.float32), 'Wq': jax.random.normal(ks[3], (EMB, EMB), jnp.float32) * scale, 'bq': jnp.zeros((EMB,), jnp.float32), 'Wk': jax.random.normal(ks[4], (EMB, EMB), jnp.float32) * scale, 'bk': jnp.zeros((EMB,), jnp.float32), 'Wv': jax.random.normal(ks[5], (EMB, EMB), jnp.float32) * scale, 'bv': jnp.zeros((EMB,), jnp.float32), 'Wo': jax.random.normal(ks[6], (EMB, EMB), jnp.float32) * scale, 'bo': jnp.zeros((EMB,), jnp.float32)}
        return inp
    _L0_xattn_all = _L0_xattn_setup()
    _L0_xattn_in = {k: v for k, v in _L0_xattn_all.items() if k in ('Wq', 'bq', 'Wk', 'bk', 'Wv', 'bv', 'Wo', 'bo')}
    del _L0_xattn_all

    def _L0_ffn_setup():
        import jax, jax.numpy as jnp
        import numpy as np
        D_MODEL = 128
        HIDDEN = 256
        E_ROUTED = 14
        E_SHARED = 2
        TOP_K = 2
        EPS = 1e-09
        RMS_EPS = 1.1920929e-07

        def _ffn(xn, rw, W1, W2):
            ms = jnp.mean(xn * xn, axis=-1, keepdims=True)
            h = xn * jax.lax.rsqrt(ms + RMS_EPS) * rw
            return jax.nn.silu(h @ W1) @ W2
        key = jax.random.key(seed)
        ks = jax.random.split(key, 9)
        B, T = (2, 128)
        x = jax.random.normal(ks[0], (B, T, D_MODEL), dtype=jnp.float32)
        router_w = jax.random.normal(ks[1], (D_MODEL, E_ROUTED), dtype=jnp.float32) * 0.006
        rms_w = jnp.ones((E_ROUTED, D_MODEL), dtype=jnp.float32)
        w1 = jax.random.normal(ks[2], (E_ROUTED, D_MODEL, HIDDEN), dtype=jnp.float32) * 0.02
        w2 = jax.random.normal(ks[3], (E_ROUTED, HIDDEN, D_MODEL), dtype=jnp.float32) * 0.02
        rms_w_s = jnp.ones((E_SHARED, D_MODEL), dtype=jnp.float32)
        w1_s = jax.random.normal(ks[4], (E_SHARED, D_MODEL, HIDDEN), dtype=jnp.float32) * 0.02
        w2_s = jax.random.normal(ks[5], (E_SHARED, HIDDEN, D_MODEL), dtype=jnp.float32) * 0.02
        return {'x': x, 'router_w': router_w, 'rms_w': rms_w, 'w1': w1, 'w2': w2, 'rms_w_s': rms_w_s, 'w1_s': w1_s, 'w2_s': w2_s}
    _L0_ffn_all = _L0_ffn_setup()
    _L0_ffn_in = {k: v for k, v in _L0_ffn_all.items() if k in ('router_w', 'rms_w', 'w1', 'w2', 'rms_w_s', 'w1_s', 'w2_s')}
    del _L0_ffn_all

    def _L1_attn_setup():
        import jax, jax.numpy as jnp
        import numpy as np
        import math
        B, S, D, H, DH = (4, 256, 128, 8, 64)
        SCALE = 1.0 / math.sqrt(DH)
        EPS = 1e-08

        def _xavier(key, shape, gain):
            std = gain * np.sqrt(2.0 / (shape[0] + shape[1]))
            return (jax.random.normal(key, shape, jnp.float32) * std).astype(jnp.float32)

        def _stable_lse(a, b):
            m = jnp.maximum(a, b)
            return m + jnp.log1p(jnp.exp(-jnp.abs(a - b)))
        key = jax.random.key(seed)
        ks = jax.random.split(key, 7)
        return {'x': jax.random.normal(ks[0], (B, S, D), jnp.float32), 'W_q': _xavier(ks[1], (H * DH, D), 0.1), 'W_k': _xavier(ks[2], (H * DH, D), 0.1), 'W_v': _xavier(ks[3], (D, D), 1.0), 'W_alpha_w': jax.random.normal(ks[4], (H * DH, D), jnp.float32) * 0.01, 'W_alpha_b': jnp.ones((H * DH,), jnp.float32), 'W_o': _xavier(ks[5], (D, D), 0.1)}
    _L1_attn_all = _L1_attn_setup()
    _L1_attn_in = {k: v for k, v in _L1_attn_all.items() if k in ('W_q', 'W_k', 'W_v', 'W_alpha_w', 'W_alpha_b', 'W_o')}
    del _L1_attn_all

    def _L1_xattn_setup():
        import jax, jax.numpy as jnp
        import numpy as np
        B, L, D = (8, 256, 128)
        key = jax.random.key(seed)
        k1, k2, k3 = jax.random.split(key, 3)
        enc_outputs = jax.random.normal(k1, (B, L, D), dtype=jnp.float32)
        x = jax.random.normal(k2, (B, L, D), dtype=jnp.float32)
        Wq = jax.random.normal(k3, (D, D), dtype=jnp.float32) * (1.0 / np.sqrt(D))
        return {'enc_outputs': enc_outputs, 'x': x, 'Wq': Wq}
    _L1_xattn_all = _L1_xattn_setup()
    _L1_xattn_in = {k: v for k, v in _L1_xattn_all.items() if k in ('Wq',)}
    del _L1_xattn_all

    def _L1_ffn_setup():
        import jax, jax.numpy as jnp
        import numpy as np
        H = 128
        I = 64
        E = 64
        G = 8
        TOPK_GROUP = 4
        K = 8
        I_SH = 128
        SCALE = 2.5

        def _route(x, router_w, e_bias):
            T = x.shape[0]
            scores = jax.nn.sigmoid(x.astype(jnp.float32) @ router_w.T.astype(jnp.float32))
            sfc = jax.lax.stop_gradient(scores) + e_bias[None, :]
            group_scores = jax.lax.top_k(sfc.reshape(T, G, E // G), 2)[0].sum(-1)
            _, gidx = jax.lax.top_k(group_scores, TOPK_GROUP)
            gmask = jax.nn.one_hot(gidx, G, dtype=sfc.dtype).sum(1)
            smask = jnp.repeat(gmask, E // G, axis=1)
            masked = jnp.where(smask > 0, sfc, 0.0)
            _, topk_idx = jax.lax.top_k(masked, K)
            w = jnp.take_along_axis(scores, topk_idx, axis=1)
            w = w / (w.sum(-1, keepdims=True) + 1e-20)
            return (topk_idx, w * SCALE)
        key = jax.random.key(seed)
        ks = jax.random.split(key, 9)
        s = 0.02
        return {'hidden_states': jax.random.normal(ks[0], (2, 128, H), jnp.float32), 'router_w': jax.random.normal(ks[1], (E, H), jnp.float32) * s, 'e_bias': jnp.zeros((E,), jnp.float32), 'Wg': jax.random.normal(ks[2], (E, H, I), jnp.float32) * s, 'Wu': jax.random.normal(ks[3], (E, H, I), jnp.float32) * s, 'Wd': jax.random.normal(ks[4], (E, I, H), jnp.float32) * s, 'SWg': jax.random.normal(ks[5], (H, I_SH), jnp.float32) * s, 'SWu': jax.random.normal(ks[6], (H, I_SH), jnp.float32) * s, 'SWd': jax.random.normal(ks[7], (I_SH, H), jnp.float32) * s}
    _L1_ffn_all = _L1_ffn_setup()
    _L1_ffn_in = {k: v for k, v in _L1_ffn_all.items() if k in ('router_w', 'e_bias', 'Wg', 'Wu', 'Wd', 'SWg', 'SWu', 'SWd')}
    del _L1_ffn_all
    return {'x': x, 'ctx_1024': ctx_1024, 'L0_attn_W_Q': _L0_attn_in['W_Q'], 'L0_attn_W_K': _L0_attn_in['W_K'], 'L0_attn_W_V': _L0_attn_in['W_V'], 'L0_attn_W_O': _L0_attn_in['W_O'], 'L0_xattn_Wq': _L0_xattn_in['Wq'], 'L0_xattn_bq': _L0_xattn_in['bq'], 'L0_xattn_Wk': _L0_xattn_in['Wk'], 'L0_xattn_bk': _L0_xattn_in['bk'], 'L0_xattn_Wv': _L0_xattn_in['Wv'], 'L0_xattn_bv': _L0_xattn_in['bv'], 'L0_xattn_Wo': _L0_xattn_in['Wo'], 'L0_xattn_bo': _L0_xattn_in['bo'], 'L0_ffn_router_w': _L0_ffn_in['router_w'], 'L0_ffn_rms_w': _L0_ffn_in['rms_w'], 'L0_ffn_w1': _L0_ffn_in['w1'], 'L0_ffn_w2': _L0_ffn_in['w2'], 'L0_ffn_rms_w_s': _L0_ffn_in['rms_w_s'], 'L0_ffn_w1_s': _L0_ffn_in['w1_s'], 'L0_ffn_w2_s': _L0_ffn_in['w2_s'], 'L1_attn_W_q': _L1_attn_in['W_q'], 'L1_attn_W_k': _L1_attn_in['W_k'], 'L1_attn_W_v': _L1_attn_in['W_v'], 'L1_attn_W_alpha_w': _L1_attn_in['W_alpha_w'], 'L1_attn_W_alpha_b': _L1_attn_in['W_alpha_b'], 'L1_attn_W_o': _L1_attn_in['W_o'], 'L1_xattn_Wq': _L1_xattn_in['Wq'], 'L1_ffn_router_w': _L1_ffn_in['router_w'], 'L1_ffn_e_bias': _L1_ffn_in['e_bias'], 'L1_ffn_Wg': _L1_ffn_in['Wg'], 'L1_ffn_Wu': _L1_ffn_in['Wu'], 'L1_ffn_Wd': _L1_ffn_in['Wd'], 'L1_ffn_SWg': _L1_ffn_in['SWg'], 'L1_ffn_SWu': _L1_ffn_in['SWu'], 'L1_ffn_SWd': _L1_ffn_in['SWd']}

def reference(x, ctx_1024, L0_attn_W_Q, L0_attn_W_K, L0_attn_W_V, L0_attn_W_O, L0_xattn_Wq, L0_xattn_bq, L0_xattn_Wk, L0_xattn_bk, L0_xattn_Wv, L0_xattn_bv, L0_xattn_Wo, L0_xattn_bo, L0_ffn_router_w, L0_ffn_rms_w, L0_ffn_w1, L0_ffn_w2, L0_ffn_rms_w_s, L0_ffn_w1_s, L0_ffn_w2_s, L1_attn_W_q, L1_attn_W_k, L1_attn_W_v, L1_attn_W_alpha_w, L1_attn_W_alpha_b, L1_attn_W_o, L1_xattn_Wq, L1_ffn_router_w, L1_ffn_e_bias, L1_ffn_Wg, L1_ffn_Wu, L1_ffn_Wd, L1_ffn_SWg, L1_ffn_SWu, L1_ffn_SWd):
    import jax
    import jax.numpy as jnp

    def _L0_attn_ref(x, W_Q, W_K, W_V, W_O):
        import jax, jax.numpy as jnp
        import numpy as np
        BATCH, SEQ, D_EMBED, N_HEADS, D_HEAD = (1, 256, 128, 16, 64)
        MASK_VAL = 10000000000.0
        q = jnp.einsum('ahe,bce->bach', W_Q, x)
        k = jnp.einsum('ahe,bce->bach', W_K, x)
        v = jnp.einsum('ahe,bce->bach', W_V, x)
        n = x.shape[1]
        scores = jnp.einsum('bach,baCh->bacC', k, q)
        causal = jnp.tril(jnp.ones((n, n), dtype=bool))
        masked = jnp.where(causal, scores, jnp.float32(-MASK_VAL))
        attn = jax.nn.softmax(masked / np.float32(np.sqrt(D_HEAD)), axis=-1)
        z = jnp.einsum('bacC,baCh->bach', attn, v)
        out = jnp.einsum('aeh,bach->bce', W_O, z)
        return out

    def _L0_xattn_ref(query, key, value, Wq, bq, Wk, bk, Wv, bv, Wo, bo):
        import jax, jax.numpy as jnp
        import numpy as np
        HEAD = 16
        EMB = 128
        B, S = (8, 512)

        def _proj_heads(x, W, b, H, d):
            Bx, Sx, _ = x.shape
            y = x @ W.T + b
            return y.reshape(Bx, Sx, H, d).transpose(0, 2, 1, 3)
        Bx, Sx, E = query.shape
        H = HEAD
        d = E // H
        q = jax.nn.elu(_proj_heads(query, Wq, bq, H, d))
        k = jax.nn.elu(_proj_heads(key, Wk, bk, H, d))
        v = _proj_heads(value, Wv, bv, H, d)
        sqrt_S = jnp.asarray(np.sqrt(Sx), jnp.float32)
        k = k / (jnp.linalg.norm(k, axis=2, keepdims=True) * sqrt_S)
        sqrt_d = jnp.asarray(np.sqrt(d), jnp.float32)
        q = q / (jnp.linalg.norm(q, axis=3, keepdims=True) * sqrt_d)
        scores = jnp.einsum('bhsd,bhse->bhde', k, v)
        x = jnp.einsum('bhsd,bhde->bhse', q, scores)
        x = x.transpose(0, 2, 1, 3).reshape(Bx, Sx, E)
        return x @ Wo.T + bo

    def _L0_ffn_ref(x, router_w, rms_w, w1, w2, rms_w_s, w1_s, w2_s):
        import jax, jax.numpy as jnp
        import numpy as np
        D_MODEL = 128
        HIDDEN = 256
        E_ROUTED = 14
        E_SHARED = 2
        TOP_K = 2
        EPS = 1e-09
        RMS_EPS = 1.1920929e-07

        def _ffn(xn, rw, W1, W2):
            ms = jnp.mean(xn * xn, axis=-1, keepdims=True)
            h = xn * jax.lax.rsqrt(ms + RMS_EPS) * rw
            return jax.nn.silu(h @ W1) @ W2
        B, T, D = x.shape
        N = B * T
        xf = x.reshape(N, D)
        gates = jax.nn.softmax(xf @ router_w, axis=-1)
        top_v, top_i = jax.lax.top_k(gates, TOP_K)
        masked = jnp.zeros_like(gates).at[jnp.arange(N)[:, None], top_i].set(top_v)
        masked = masked / (masked.sum(axis=-1, keepdims=True) + EPS)
        routed = jax.vmap(lambda rw_, W1_, W2_: _ffn(xf, rw_, W1_, W2_))(rms_w, w1, w2)
        routed_out = jnp.einsum('end,ne->nd', routed, masked)
        shared = jax.vmap(lambda rw_, W1_, W2_: _ffn(xf, rw_, W1_, W2_))(rms_w_s, w1_s, w2_s).sum(0)
        return (routed_out + shared).reshape(B, T, D)

    def _L1_attn_ref(x, W_q, W_k, W_v, W_alpha_w, W_alpha_b, W_o):
        import jax, jax.numpy as jnp
        import numpy as np
        import math
        B, S, D, H, DH = (4, 256, 128, 8, 64)
        SCALE = 1.0 / math.sqrt(DH)
        EPS = 1e-08

        def _xavier(key, shape, gain):
            std = gain * np.sqrt(2.0 / (shape[0] + shape[1]))
            return (jax.random.normal(key, shape, jnp.float32) * std).astype(jnp.float32)

        def _stable_lse(a, b):
            m = jnp.maximum(a, b)
            return m + jnp.log1p(jnp.exp(-jnp.abs(a - b)))
        Bx, Sx, _ = x.shape
        q = (x @ W_q.T).reshape(Bx, Sx, H, DH)
        k = (x @ W_k.T).reshape(Bx, Sx, H, DH)
        v = x @ W_v.T
        b = (q * k).sum(-1) * SCALE
        alpha = (x @ W_alpha_w.T + W_alpha_b).reshape(Bx, Sx, H, DH)
        a = -jax.nn.softplus(alpha).sum(-1)
        vs = jnp.sign(v)
        vs = jnp.where(vs == 0, jnp.ones_like(vs), vs)
        vl = jnp.log(jnp.abs(v) + EPS)
        ln0 = b[:, 0]
        nm0 = b[:, 0, :, None] + vl[:, 0, None, :]
        sg0 = jnp.broadcast_to(vs[:, 0, None, :], nm0.shape)
        y0 = (sg0 * jnp.exp(nm0 - ln0[..., None])).sum(-2)

        def step(carry, inp):
            ln, nm, sg = carry
            a_t, b_t, vl_t, vs_t = inp
            ln = _stable_lse(a_t + ln, b_t)
            dec = a_t[..., None] + nm
            new = b_t[..., None] + vl_t[:, None, :]
            m = jnp.maximum(dec, new)
            ssum = sg * jnp.exp(dec - m) + vs_t[:, None, :] * jnp.exp(new - m)
            nsg = jnp.sign(ssum)
            nsg = jnp.where(nsg == 0, jnp.ones_like(nsg), nsg)
            nm = m + jnp.log(jnp.abs(ssum) + EPS)
            y = (nsg * jnp.exp(nm - ln[..., None])).sum(-2)
            return ((ln, nm, nsg), y)
        xs = (jnp.moveaxis(a[:, 1:], 1, 0), jnp.moveaxis(b[:, 1:], 1, 0), jnp.moveaxis(vl[:, 1:], 1, 0), jnp.moveaxis(vs[:, 1:], 1, 0))
        _, ys = jax.lax.scan(step, (ln0, nm0, sg0), xs)
        y = jnp.concatenate([y0[:, None, :], jnp.moveaxis(ys, 0, 1)], axis=1)
        return y @ W_o.T

    def _L1_xattn_ref(enc_outputs, x, Wq):
        import jax, jax.numpy as jnp
        import numpy as np
        B, L, D = (8, 256, 128)
        d_k = x.shape[-1]
        q = jnp.einsum('bld,hd->blh', x, Wq)
        k = jnp.einsum('bld,hd->blh', enc_outputs, Wq)
        v = k
        scores = jnp.einsum('bqh,bkh->bqk', q, k) / jnp.sqrt(jnp.float32(d_k))
        Lq, Lk = (scores.shape[1], scores.shape[2])
        causal = jnp.tril(jnp.ones((Lq, Lk), dtype=bool))
        scores = jnp.where(causal, scores, -jnp.inf)
        attn = jax.nn.softmax(scores, axis=-1)
        return jnp.einsum('bqk,bkh->bqh', attn, v)

    def _L1_ffn_ref(hidden_states, router_w, e_bias, Wg, Wu, Wd, SWg, SWu, SWd):
        import jax, jax.numpy as jnp
        import numpy as np
        H = 128
        I = 64
        E = 64
        G = 8
        TOPK_GROUP = 4
        K = 8
        I_SH = 128
        SCALE = 2.5

        def _route(x, router_w, e_bias):
            T = x.shape[0]
            scores = jax.nn.sigmoid(x.astype(jnp.float32) @ router_w.T.astype(jnp.float32))
            sfc = jax.lax.stop_gradient(scores) + e_bias[None, :]
            group_scores = jax.lax.top_k(sfc.reshape(T, G, E // G), 2)[0].sum(-1)
            _, gidx = jax.lax.top_k(group_scores, TOPK_GROUP)
            gmask = jax.nn.one_hot(gidx, G, dtype=sfc.dtype).sum(1)
            smask = jnp.repeat(gmask, E // G, axis=1)
            masked = jnp.where(smask > 0, sfc, 0.0)
            _, topk_idx = jax.lax.top_k(masked, K)
            w = jnp.take_along_axis(scores, topk_idx, axis=1)
            w = w / (w.sum(-1, keepdims=True) + 1e-20)
            return (topk_idx, w * SCALE)
        orig_shape = hidden_states.shape
        x = hidden_states.reshape(-1, orig_shape[-1])
        T = x.shape[0]
        topk_idx, topk_w = _route(x, router_w, e_bias)
        coef = jnp.zeros((T, E), topk_w.dtype).at[jnp.arange(T)[:, None], topk_idx].add(topk_w)
        g = jnp.einsum('th,ehi->tei', x, Wg)
        u = jnp.einsum('th,ehi->tei', x, Wu)
        h = jax.nn.silu(g) * u * coef[:, :, None]
        moe_out = jnp.einsum('tei,eih->th', h, Wd)
        shared = jax.nn.silu(x @ SWg) * (x @ SWu) @ SWd
        return (moe_out + shared).reshape(orig_shape)
    x = _layernorm(x + _L0_attn_ref(x, L0_attn_W_Q, L0_attn_W_K, L0_attn_W_V, L0_attn_W_O), axis=-1)
    x = _layernorm(x + _L0_xattn_ref(x, ctx_1024, ctx_1024, L0_xattn_Wq, L0_xattn_bq, L0_xattn_Wk, L0_xattn_bk, L0_xattn_Wv, L0_xattn_bv, L0_xattn_Wo, L0_xattn_bo), axis=-1)
    x = _layernorm(x + _L0_ffn_ref(x, L0_ffn_router_w, L0_ffn_rms_w, L0_ffn_w1, L0_ffn_w2, L0_ffn_rms_w_s, L0_ffn_w1_s, L0_ffn_w2_s), axis=-1)
    x = _layernorm(x + _L1_attn_ref(x, L1_attn_W_q, L1_attn_W_k, L1_attn_W_v, L1_attn_W_alpha_w, L1_attn_W_alpha_b, L1_attn_W_o), axis=-1)
    x = _layernorm(x + _L1_xattn_ref(ctx_1024, x, L1_xattn_Wq), axis=-1)
    x = _layernorm(x + _L1_ffn_ref(x, L1_ffn_router_w, L1_ffn_e_bias, L1_ffn_Wg, L1_ffn_Wu, L1_ffn_Wd, L1_ffn_SWg, L1_ffn_SWu, L1_ffn_SWd), axis=-1)
    return x

_drawn_inputs = setup_inputs


def setup_inputs(seed=0):
    import zlib

    import numpy as np

    out = dict(_drawn_inputs(seed))
    spreads = {'L0_xattn_bq': (0.0, 0.8),
     'L0_xattn_bk': (0.0, 0.8),
     'L0_xattn_bv': (0.0, 0.8),
     'L0_xattn_bo': (0.0, 0.1),
     'L0_ffn_rms_w': (1.0, 0.6),
     'L0_ffn_rms_w_s': (1.0, 0.6),
     'L1_attn_W_alpha_b': (1.0, 0.6),
     'L1_ffn_e_bias': (0.0, 0.8)}
    factors = {'L1_attn_W_q': 200.0,
     'L1_attn_W_k': 200.0,
     'L1_ffn_router_w': 8.0,
     'L1_ffn_Wg': 8.0,
     'L1_ffn_Wu': 8.0,
     'L1_ffn_Wd': 8.0,
     'L1_ffn_SWg': 8.0,
     'L1_ffn_SWu': 8.0,
     'L1_ffn_SWd': 8.0,
     'L1_attn_W_alpha_w': 8.0}
    for name, (base, spread) in spreads.items():
        noise = np.random.default_rng([zlib.crc32(name.encode()), seed]).standard_normal(out[name].shape)
        drawn = base * np.exp(spread * noise) if base else spread * noise
        out[name] = jnp.asarray(drawn.astype(out[name].dtype))
    for name, factor in factors.items():
        out[name] = (out[name] * factor).astype(out[name].dtype)
    return out
```

```python
import math
from contextlib import ExitStack

import numpy as np
import concourse.bass as bass
from concourse import mybir
from concourse.alu_op_type import AluOpType as ALU

ACT = mybir.ActivationFunctionType
AX = mybir.AxisListType
F32 = mybir.dt.float32
F32R = mybir.dt.float32r
ds = bass.ds

B, S, D = 8, 256, 128
N = B * S
T = N // 128
SC = 64
CH = 512
NC_ = N // CH
H0, DH = 16, 64
PAIRS = H0 // 2
HX, DX = 16, 8
E0, E0R, HID = 16, 14, 256
H1 = 8
E1, I1, K1 = 64, 64, 8
LN_EPS, RMS_EPS, EPS = 1e-5, 1.1920929e-07, 1e-8
BIG = 1e30


def decoder_program(nc, a, out):
    CTX_PE = {"ck_ready": 1, "cv_ready": 2, "kn_ready": 3, "gt_ready": 4, "g2_ready": 5, "ke_ready": 6, "ve_ready": 7, "kk_ready": 8}
    CTX_ACT = {"ck_exp": 1, "cv_done": 2, "wq_hi": 3, "g2_done": 11, "ke_done": 12, "ve_done": 13, "kk_done": 14}
    CTX_DVE = {"ck_pos": 1, "ck_done": 2, "kn_sum": 3, "gbt_done": 4, "wq_lo": 5, "wr_split": 7}
    CTX_POOL = {"ck_neg": 1, "ck_sq": 2, "kn_done": 3}
    ctx = ExitStack()
    sems = {}

    def sem(name):
        if name not in sems:
            sems[name] = ctx.enter_context(nc.semaphore(name))
        return sems[name]

    def sb(name, shape, dt=F32, scope=ctx):
        return scope.enter_context(nc.sbuf_tensor(name, shape, dt))

    with ctx:
        PS = ctx.enter_context(nc.psum_tensor("PS", [128, 8 * CH], F32))

        def bank(n, w=CH, k=1):
            return PS[:, n * CH:n * CH + (k - 1) * CH + w]

        Xp = sb("Xp", [128, (B + 1) * S])
        X = Xp[:, S:].rearrange("p (t d) -> p t d", d=D)
        XTh = sb("XTh", [128, N], F32R)
        XTl = sb("XTl", [128, N], F32R)
        ident = sb("ident", [128, 128])
        blockones = sb("blockones", [128, 128])
        sel2 = sb("sel2", [128, 72], F32R)
        cmask = sb("cmask", [128, 2 * 128])
        ones = sb("ones", [128, 128])
        scratch = sb("scratch", [128, 16])
        st = sb("st", [128, T, 6])
        mv = sb("mv", [128, T, 2])
        rs = sb("rs", [128, T])
        rs2 = sb("rs2", [128, T])
        ms = sb("ms", [128, T])
        neghalf = sb("neghalf", [128, T])
        ctxT = sb("ctxT", [128, B * SC])

        halfones = sb("halfones", [128, 2])
        wx = sb("wx", [128, 4, 128])
        bq = sb("bq", [128, 1])
        brow = sb("brow", [1, 3 * 128])
        G2 = sb("G2", [128, B, 128])
        wqh = sb("wqh", [128, 128], F32R)
        wql = sb("wql", [128, 128], F32R)
        wrh = sb("wrh", [128, 128], F32R)
        wrl = sb("wrl", [128, 128], F32R)
        wr_in = sb("wr_in", [128, E0R])

        wd_in = sb("wd_in", [128, 3 * CH + 128])
        wdh = sb("wdh", [128, 3 * CH + 128], F32R)
        wdl = sb("wdl", [128, 3 * CH + 128], F32R)
        abias = sb("abias", [1, CH])
        abr = sb("abr", [33, CH], F32R)
        onesr = sb("onesr", [33, 128], F32R)
        wo1 = sb("wo1", [128, 128])
        wqe = sb("wqe", [128, 2, 128])
        KK = sb("KK", [128, B * SC])
        vE = sb("vE", [64, B, 128])
        wr1_in = sb("wr1_in", [128, E1])
        wr1h = sb("wr1h", [128, 128], F32R)
        wr1l = sb("wr1l", [128, 128], F32R)
        ebias = sb("ebias", [128, E1])
        wsh = sb("wsh", [128, 384])
        wshh = sb("wshh", [128, 384], F32R)
        wshl = sb("wshl", [128, 384], F32R)
        tiny = sb("tiny", [128, 1])
        wo1e = sb("wo1e", [128, 128])

        sa = ExitStack()
        Mh = sb("Mh", [128, H0 * 128], F32R, sa)
        Ml = sb("Ml", [128, H0 * 128], F32R, sa)
        NVh = sb("NVh", [128, H0 * 128], F32R, sa)
        NVl = sb("NVl", [128, H0 * 128], F32R, sa)
        xall = sb("xall", [128, (B + 1) * S], F32, sa)
        xh = [sb(f"xh{k}", [128, S], F32R, sa) for k in range(2)]
        xl = [sb(f"xl{k}", [128, S], F32R, sa) for k in range(2)]
        VO = sb("VO", [128, 2, H0, 128], F32, sa)
        P = sb("P", [128, 4, 768], F32, sa)
        PT = sb("PT", [128, 2, 2, 384], F32, sa)
        Uh = sb("Uh", [128, CH], F32R, sa)
        Ul = sb("Ul", [128, CH], F32R, sa)
        mn = sb("mn", [128, 2, 4], F32, sa)
        ls = sb("ls", [128, 2, 4], F32, sa)
        rl = sb("rl", [128, 2, 4], F32, sa)
        wraw = ExitStack()
        w64 = {n: sb("w64" + n, [64, H0, 128], F32, wraw) for n in "qkvo"}
        cx = ExitStack()
        ce = sb("ce", [128, 4, 128], F32, cx)
        ck = sb("ck", [128, 4, 128], F32, cx)
        cv = sb("cv", [128, 4, 128], F32, cx)
        csq = sb("csq", [128, 4, 128], F32, cx)
        GBT = sb("GBT", [128, B, 128], F32, cx)
        kn = sb("kn", [128, B], F32, cx)
        kTe = sb("kTe", [128, B * SC], F32, cx)
        cx.close()
        wraw.close()
        sa.close()

        sbs = ExitStack()
        EQ = sb("EQ", [128, N], F32, sbs)
        RQ = sb("RQ", [128, N], F32, sbs)
        Q = sb("Q", [128, N], F32, sbs)
        SQ = sb("SQ", [128, N], F32, sbs)
        sbs.close()

        sc = ExitStack()
        XS = sb("XS", [128, T, 128], F32, sc)
        LT = sb("LT", [16, N], F32, sc)
        Lg = sb("Lg", [128, T, E0R], F32, sc)
        lm = sb("lm", [128, T], F32, sc)
        lz = sb("lz", [128, T], F32, sc)
        G20 = sb("G20", [128, T, 20], F32, sc)
        M8 = sb("M8", [128, T, 8], F32, sc)
        RPL = sb("RPL", [128, T, 8], F32, sc)
        RP = sb("RP", [128, T, 20], F32, sc)
        GI = sb("GI", [128, T, 128], F32R, sc)
        SELT = sb("SELT", [128, N], F32R, sc)
        rw = sb("rw", [128, E0], F32, sc)
        W0 = [sb(f"W0_{k}", [128, 2 * HID], F32, sc) for k in range(2)]
        W0h = [sb(f"W0h{k}", [128, 2 * HID], F32R, sc) for k in range(2)]
        W0l = [sb(f"W0l{k}", [128, 2 * HID], F32R, sc) for k in range(2)]
        esel = [sb(f"esel{k}", [128, 128], F32R, sc) for k in range(2)]
        SG = sb("SG", [128, 2, CH], F32, sc)
        Hf = sb("Hf", [128, 4, CH], F32, sc)
        HH = sb("HH", [128, 4, CH], F32R, sc)
        HL = sb("HL", [128, 4, CH], F32R, sc)
        OT = sb("OT", [128, N], F32, sc)
        sc.close()

        sd = ExitStack()
        VP = sb("VP", [128, N], F32, sd)
        AB64 = sb("AB64", [64, 2, S], F32, sd)
        mb = sb("mb", [64, S + 1], F32, sd)
        db = sb("db", [64, S + 1], F32, sd)
        ea = sb("ea", [64, S], F32, sd)
        eb = sb("eb", [64, S], F32, sd)
        rd = sb("rd", [64, S], F32, sd)
        wu = sb("wu", [64, 2, S], F32, sd)
        WUr = sb("WUr", [128, 2, S], F32R, sd)
        dsel = [sb(f"dsel{k}", [128, H1, 128], F32R, sd) for k in range(2)]
        sd1 = ExitStack()
        QS = sb("QS", [128, 2, CH], F32, sd1)
        PR = sb("PR", [128, 2, CH], F32, sd1)
        ZA = sb("ZA", [128, T, CH], F32, sd1)
        ZR = sb("ZR", [128, T, CH], F32, sd1)
        ABs = sb("ABs", [128, 2, T, H1], F32, sd1)
        ABt = sb("ABt", [128, 2, 2, H1, B], F32, sd1)
        VS = sb("VS", [128, N], F32, sd1)
        sd1.close()
        R = H1 * S
        Wb = [sb(f"Wb{k}", [128, R], F32, sd) for k in range(2)]
        qb = sb("qb", [128, R], F32, sd)
        r0b = [sb(f"r0b{k}", [128, R], F32, sd) for k in range(2)]
        dfb = [sb(f"dfb{k}", [128, R], F32, sd) for k in range(2)]
        sgb = sb("sgb", [128, R], F32, sd)
        gb = [sb(f"gb{k}", [128, R], F32, sd) for k in range(2)]
        rb = [sb(f"rb{k}", [128, R], F32, sd) for k in range(2)]
        sd.close()

        se = ExitStack()
        XTf = sb("XTf", [128, N], F32, se)
        SE = sb("SE", [128, T, SC], F32, se)
        PE_T = sb("PE_T", [64, N], F32, se)
        em = sb("em", [128, T], F32, se)
        el = sb("el", [128, T], F32, se)
        se.close()

        sf = ExitStack()
        FL = sb("FL", [64, N], F32, sf)
        SCo = sb("SCo", [128, T, E1], F32, sf)
        SF = sb("SF", [128, T, E1], F32, sf)
        h1 = sb("h1", [128, T * 8, 4], F32, sf)
        l1 = sb("l1", [128, T * 8, 4], F32, sf)
        h2 = sb("h2", [128, T * 8, 2], F32, sf)
        l2 = sb("l2", [128, T * 8, 2], F32, sf)
        t2 = sb("t2", [128, T * 8, 2], F32, sf)
        h3 = sb("h3", [128, T * 8, 1], F32, sf)
        l3 = sb("l3", [128, T * 8, 1], F32, sf)
        t3 = sb("t3", [128, T * 8, 1], F32, sf)
        GS = sb("GS", [128, T, 12], F32, sf)
        F8 = sb("F8", [128, T, 8], F32, sf)
        FR = sb("FR", [128, T, 8], F32, sf)
        GR = sb("GR", [128, T, 12], F32, sf)
        gm = sb("gm", [128, T, 8], F32, sf)
        FM = sb("FM", [128, T, E1], F32, sf)
        FRP = sb("FRP", [128, T, E1], F32, sf)
        fs = sb("fs", [128, T], F32, sf)
        fi = sb("fi", [128, T], F32, sf)
        GI1 = sb("GI1", [128, T, 128], F32R, sf)
        SELT1 = sb("SELT1", [128, N], F32R, sf)
        W3 = [sb(f"W3_{k}", [128, 384], F32, sf) for k in range(2)]
        W3h = [sb(f"W3h{k}", [128, 384], F32R, sf) for k in range(2)]
        W3l = [sb(f"W3l{k}", [128, 384], F32R, sf) for k in range(2)]
        fsel = [sb(f"fsel{k}", [128, 2, 64], F32R, sf) for k in range(2)]
        FG = sb("FG", [128, 2, CH], F32, sf)
        FU = sb("FU", [128, 2, CH], F32, sf)
        FH = sb("FH", [128, 4, CH], F32, sf)
        FHH = sb("FHH", [128, 4, CH], F32R, sf)
        FHL = sb("FHL", [128, 4, CH], F32R, sf)
        OT1 = sb("OT1", [128, N], F32, sf)
        sf.close()
        NEG = -3e38
        SP_GROUPS = ((0, 6), (6, 12), (12, 16))

        block = ctx.enter_context(nc.Block())

        def piece(q):
            r, h = q // 2, q % 2
            return (h * 128, 128) if r == 0 else (256 + h * 256, 256)

        def scores(par, q):
            r, h = q // 2, q % 2
            c = (2 * par + r) * CH + h * (128 if r == 0 else 256)
            return PS[:, c:c + (128 if r == 0 else 256)]

        PTP = bank(4, CH, 2).rearrange("p (a c) -> p a c", a=2)[:, :, 0:384]
        UB, OB = bank(6), bank(7)
        STEPS = 2 * PAIRS

        def ln_pool(pool, n):
            pool.wait_ge(sem("ln_mv"), T * (n + 1))
            pool.tensor_scalar(ms[:, :], mv[:, :, 1], LN_EPS, None, ALU.add).then_inc(sem("ln_ms"), 1)
            pool.wait_ge(sem("ln_ms"), n + 1)
            pool.tensor_tensor(rs[:, :], ms[:, :], neghalf[:, :], ALU.pow).then_inc(sem("ln_rs"), 1)

        def ln_vector(dve, n, src=None):
            src = src or (lambda t: X[:, t, :])
            for t in range(T):
                dve.bn_stats(st[:, t, :], src(t)).then_inc(sem("ln_st"), 1)
            for t in range(T):
                dve.wait_ge(sem("ln_st"), T * n + t + 1)
                dve.bn_aggr(mv[:, t, :], st[:, t, :]).then_inc(sem("ln_mv"), 1)
            dve.wait_ge(sem("ln_rs"), n + 1)
            for t in range(T):
                dve.tensor_scalar(X[:, t, :], src(t), mv[:, t, 0:1], rs[:, t:t + 1],
                                  ALU.subtract, ALU.mult).then_inc(sem("ln_x"), 1)

        def ln_lo(dve, n):
            with dve.Fori(0, NC_) as c:
                dve.wait_ge(sem("ln_hi"), NC_ * n + c + 1)
                dve.tensor_tensor(XTl[:, ds(c * CH, CH)], PS[:, ds(c * CH, CH)],
                                  XTh[:, ds(c * CH, CH)].bitcast(F32), ALU.subtract).then_inc(sem("ln_lo"), 1)

        def ln_tensor(pe, n, src=None, ready=None):
            for t in range(T):
                if ready:
                    pe.wait_ge(sem(ready), t + 1)
                else:
                    pe.wait_ge(sem("ln_x"), T * n + t + 1)
                r = pe.transpose(bank(t // 4)[:, t % 4 * 128:t % 4 * 128 + 128], (src or X)[:, t, :], ident[:, :])
                if t % 4 == 3:
                    r.then_inc(sem("ln_T"), 1)

        def ln_hi(act, n):
            with act.Fori(0, NC_) as c:
                act.wait_ge(sem("ln_T"), NC_ * n + c + 1)
                act.activation(XTh[:, ds(c * CH, CH)], PS[:, ds(c * CH, CH)], ACT.Copy).then_inc(sem("ln_hi"), 1)

        @block.sync
        def _(sp):
            sp.dma_start(ctxT[:, :], a["ctxT"]).then_inc(sem("ctx_in"), 16)
            sp.dma_start(wx[:, :, :], a["wx"]).then_inc(sem("ctx_in"), 16)
            sp.dma_start(brow[:, :], a["brow"]).then_inc(sem("ctx_in"), 16)
            sp.dma_start(bq[:, :], a["bq"]).then_inc(sem("ctx_in"), 16)
            for n in "qkvo":
                sp.dma_start(w64[n][:, :, :], a["w64" + n]).then_inc(sem("w64_in"), 16)
            sp.dma_start(xall[:, 0:N], a["xT"]).then_inc(sem("xT_in"), 16)
            sp.dma_start(X, a["x"]).then_inc(sem("x_in"), 16)
            sp.dma_start(wr_in[:, :], a["wr0"]).then_inc(sem("wr_in"), 16)
            for name, dst in (("wd", wd_in), ("abias", abias), ("wo1", wo1), ("wqe", wqe), ("wr1", wr1_in),
                              ("ebias", ebias), ("wsh", wsh)):
                sp.dma_start(dst[tuple([slice(None)] * len(dst.shape))], a[name]).then_inc(sem("l1_in"), 16)
            sp.wait_ge(sem("x_added"), NC_)
            sp.dma_start(rw[:, :], a["rw"]).then_inc(sem("rw_in"), 16)
            with sp.Fori(0, E0 // 2) as i:
                for s in range(2):
                    sp.wait_ge(sem("w_split"), i * 2 + s + 2)
                    sp.dma_start(W0[s][:, :], a["w12"][ds(i * 2 + s, 1), :, :].rearrange("o p n -> p (o n)")).then_inc(sem(f"w_in{s}"), 16)
            sp.wait_ge(sem("x_added"), 2 * NC_ + NC_)
            with sp.Fori(0, E1 // 4) as i:
                for s in range(2):
                    sp.wait_ge(sem("f_split"), i * 2 + s + 1)
                    sp.dma_start(W3[s][:, :], a["w3"][ds(i * 2 + s, 1), :, :].rearrange("o p n -> p (o n)")).then_inc(sem(f"w_in{s}"), 16)
            for c in range(NC_):
                sp.wait_ge(sem("ln_x"), 5 * T + 4 * c + 4)
                sp.dma_start(out[:, 4 * c:4 * c + 4, :], X[:, 4 * c:4 * c + 4, :]).then_inc(sem("out_done"), 16)
            sp.wait_ge(sem("out_done"), 16 * NC_)

        @block.gpsimd
        def _(pool):
            pool.memset(ident[:, :], 0.0).then_inc(sem("zeroed"), 1)
            pool.memset(blockones[:, :], 1.0).then_inc(sem("zeroed"), 1)
            pool.memset(cmask[:, :], 0.0).then_inc(sem("zeroed"), 1)
            pool.memset(ones[:, :], 1.0).then_inc(sem("consts"), 1)
            pool.memset(neghalf[:, :], -0.5).then_inc(sem("consts"), 1)
            pool.memset(wrh[:, :].bitcast(F32), 0.0).then_inc(sem("wr_zero"), 1)
            pool.memset(wrl[:, :].bitcast(F32), 0.0).then_inc(sem("wr_zero"), 1)
            pool.wait_ge(sem("zeroed"), 3)
            pool.affine_select(out=ident[:, :], in_=ident[:, :], compare_op=ALU.not_equal, fill=1.0,
                               base=0, pattern=[[-1, 128]], channel_multiplier=1).then_inc(sem("consts"), 1)
            pool.affine_select(out=cmask[:, 128:256], in_=cmask[:, 128:256], compare_op=ALU.is_ge, fill=BIG,
                               base=0, pattern=[[-1, 128]], channel_multiplier=1).then_inc(sem("consts"), 1)
            pool.affine_select(out=blockones[:, :], in_=blockones[:, :], compare_op=ALU.is_ge, fill=0.0,
                               base=0, pattern=[[-DX, HX], [0, DX]], channel_multiplier=1).then_inc(sem("zeroed"), 1)
            pool.wait_ge(sem("zeroed"), 4)
            pool.affine_select(out=blockones[:, :], in_=blockones[:, :], compare_op=ALU.is_ge, fill=0.0,
                               base=DX - 1, pattern=[[DX, HX], [0, DX]], channel_multiplier=-1).then_inc(sem("consts"), 1)
            pool.memset(xall[:, N:], 0.0).then_inc(sem("x_pad"), 1)
            pool.memset(P[:, 2, :], 0.0).then_inc(sem("norm_done"), 1)
            pool.memset(PT[:, 1, :, :], 0.0).then_inc(sem("pt_done"), 1)
            pool.memset(VO[:, :, :, :], 0.0).then_inc(sem("vo_done"), 1)

            pool.wait_ge(sem("ctx_act"), CTX_ACT["ck_exp"])
            pool.tensor_scalar(ce[:, :, :], ce[:, :, :], 1.0, -1.0, ALU.min, ALU.add).then_inc(sem("ctx_pool"), 1)
            pool.wait_ge(sem("ctx_dve"), CTX_DVE["ck_done"])
            pool.tensor_tensor(csq[:, :, :], ck[:, :, :], ck[:, :, :], ALU.mult).then_inc(sem("ctx_pool"), 1)
            pool.wait_ge(sem("ctx_dve"), CTX_DVE["kn_sum"])
            pool.tensor_tensor(kn[:, :], kn[:, :], neghalf[:, 0:B], ALU.pow).then_inc(sem("ctx_pool"), 1)

            def divide(g, k):
                slot, par = (k - 1) % 4, (k - 1) % 2
                pool.wait_ge(sem("rl_done"), g + 1)
                for r, w in ((0, 128), (1, 256)):
                    v = P[:, slot, 256 * r:256 * r + 2 * w].rearrange("p (h c) -> p h c", h=2)
                    f = rl[:, par, 2 * r:2 * r + 2].rearrange("p (h o) -> p h o", o=1).to_broadcast([128, 2, w])
                    last = pool.tensor_tensor(v, v, f, ALU.mult)
                last.then_inc(sem("norm_done"), 1)

            with pool.Fori(0, B // 2) as i:
                for k in range(STEPS):
                    divide(i * STEPS + k, k)
            divide(B * PAIRS, 0)
            ln_pool(pool, 0)

            for c in range(NC_):
                cc = slice(c * CH, c * CH + CH)
                pool.wait_ge(sem("q_exp"), c + 1)
                pool.tensor_scalar(EQ[:, cc], EQ[:, cc], 1.0, -1.0, ALU.min, ALU.add).then_inc(sem("q_neg"), 1)
            for c in range(NC_):
                cc = slice(c * CH, c * CH + CH)
                pool.wait_ge(sem("q_elu"), c + 1)
                pool.tensor_tensor(SQ[:, cc], Q[:, cc], Q[:, cc], ALU.mult).then_inc(sem("q_sq"), 1)
            ln_pool(pool, 1)
            pool.wait_ge(sem("ln_rs"), 2)
            pool.tensor_tensor(ms[:, :], mv[:, :, 1], rs[:, :], ALU.mult).then_inc(sem("rms"), 1)
            pool.wait_ge(sem("rms"), 1)
            pool.tensor_tensor(ms[:, :], ms[:, :], rs[:, :], ALU.mult).then_inc(sem("rms"), 1)
            pool.wait_ge(sem("rms"), 2)
            pool.tensor_scalar(ms[:, :], ms[:, :], RMS_EPS, None, ALU.add).then_inc(sem("rms"), 1)
            pool.wait_ge(sem("rms"), 3)
            pool.tensor_tensor(rs2[:, :], ms[:, :], neghalf[:, :], ALU.pow).then_inc(sem("rms"), 1)
            pool.memset(GI[:, :, :].bitcast(F32), 0.0).then_inc(sem("gi_zero"), 1)
            pool.memset(G20[:, :, :], -1.0).then_inc(sem("g20_init"), 1)
            pool.memset(RPL[:, :, :], -1.0).then_inc(sem("g20_init"), 1)
            pool.memset(Hf[:, 3, :], 0.0).then_inc(sem("h_done"), 2)
            pool.memset(HH[:, 1:3, :].bitcast(F32), 0.0).then_inc(sem("hl_done"), 1)
            pool.memset(HL[:, 1:3, :].bitcast(F32), 0.0).then_inc(sem("hl_done"), 1)
            pool.memset(W0h[1][:, :].bitcast(F32), 0.0).then_inc(sem("w2_zero"), 1)
            pool.memset(W0l[1][:, :].bitcast(F32), 0.0).then_inc(sem("w2_zero"), 1)
            pool.wait_ge(sem("gi_zero"), 1)
            pool.memset(GI[:, :, E0R:E0].bitcast(F32), 1.0).then_inc(sem("gi_zero"), 1)
            pool.memset(SG[:, 0, 0:1], 0.0).then_inc(sem("w_split"), 2)
            pool.memset(SG[:, 1, 0:1], 0.0).then_inc(sem("sg_done"), 2)
            pool.memset(esel[0][:, :].bitcast(F32), 0.0).then_inc(sem("down_done"), 16)
            pool.wait_ge(sem("rw_in"), 16)
            with pool.Fori(0, E0 // 2) as i:
                for s in range(2):
                    e = i * 2 + s
                    pool.wait_ge(sem(f"w_in{s}"), i * 16 + 16)
                    pool.tensor_tensor(W0[s][:, 0:HID], W0[s][:, 0:HID], rw[:, ds(e, 1)].to_broadcast([128, HID]),
                                       ALU.mult).then_inc(sem("w_scaled"), 1)
                    pool.wait_ge(sem("w_scaled"), e + 1)
                    pool.wait_ge(sem("down_done"), i * 16 + 11 + 8 * s)
                    pool.tensor_tensor(W0h[s][:, :], W0[s][:, :], ones[:, 0:1].to_broadcast([128, 2 * HID]),
                                       ALU.mult).then_inc(sem("w_rounded"), 1)
                    pool.tensor_copy(esel[s][:, :], sel2[:, ds(e, 1)].to_broadcast([128, 128]).bitcast(F32R)).then_inc(sem("w_sel"), 1)
                    pool.wait_ge(sem("w_rounded"), e + 1)
                    pool.tensor_tensor(W0l[s][:, :], W0[s][:, :], W0h[s][:, :].bitcast(F32), ALU.subtract).then_inc(sem("w_split"), 1)
            ln_pool(pool, 2)
            for t in range(T):
                pool.wait_ge(sem("z_ln"), t + 1)
                pool.wait_ge(sem("z_pos"), t + 1)
                pool.tensor_tensor(ZR[:, t, :], ZR[:, t, :], ZA[:, t, :], ALU.add).then_inc(sem("z_sp"), 1)
            pool.memset(mb[:, 0:1], -BIG).then_inc(sem("d_init"), 1)
            pool.memset(db[:, 0:1], 0.0).then_inc(sem("d_init"), 1)
            pool.wait_ge(sem("ab_placed"), 4)
            pool.wait_ge(sem("ab_T"), 1)
            pool.wait_ge(sem("vp_done"), 2 * NC_)
            for k in range(2):
                pool.memset(gb[k][:, :], 0.0).then_inc(sem("floor_done"), 1)
            pool.memset(Wb[1][:, :], 0.0).then_inc(sem("w_copied"), 2)
            pool.memset(r0b[1][:, :], 0.0).then_inc(sem("signed_done"), 1)
            pool.memset(rb[0][:, :], 0.0).then_inc(sem("scan2_done"), 1)
            pool.wait_ge(sem("floor_done"), 2)

            def floor_terms(g, par):
                pool.wait_ge(sem("sgn_done"), g + 1)
                pool.wait_ge(sem("abs_done"), g + 1)
                pool.tensor_tensor(dfb[par][:, :], dfb[par][:, :], sgb[:, :], ALU.mult).then_inc(sem("signed_done"), 1)
                pool.wait_ge(sem("signed_done"), g + 2)
                pool.wait_ge(sem("scan2_done"), g + 1)
                later = lambda x: x[:, :].rearrange("p (h t) -> p h t", h=H1)[:, :, 1:]
                pool.tensor_tensor(later(gb[par]), later(dfb[par]), later(r0b[par]), ALU.add).then_inc(sem("floor_done"), 1)

            with pool.Fori(0, B // 2) as i:
                for k in range(2):
                    floor_terms(i * 2 + k, k)
            ln_pool(pool, 3)
            pool.wait_ge(sem("es_step"), 5 + 1)
            pool.tensor_tensor(SE[:, :, :], SE[:, :, :], el[:, :].rearrange("p (t o) -> p t o", o=1).to_broadcast([128, T, SC]),
                               ALU.mult).then_inc(sem("e_prob"), 1)
            ln_pool(pool, 4)
            pool.wait_ge(sem("x_added"), 2 * NC_ + NC_)
            pool.memset(GS[:, :, :], NEG).then_inc(sem("f_init"), 1)
            pool.memset(FR[:, :, :], NEG).then_inc(sem("f_init"), 1)
            pool.memset(FH[:, 3, :], 0.0).then_inc(sem("fh_done"), 1)
            pool.memset(FHH[:, 2, :].bitcast(F32), 0.0).then_inc(sem("f_init"), 1)
            pool.memset(FHL[:, 2, :].bitcast(F32), 0.0).then_inc(sem("fhl_done"), 1)
            pool.memset(W3h[1][:, :].bitcast(F32), 0.0).then_inc(sem("f_init"), 1)
            pool.memset(W3l[1][:, :].bitcast(F32), 0.0).then_inc(sem("f_init"), 1)
            pool.memset(scratch[:, 1:2], 0.0).then_inc(sem("fg_done"), 2)
            pool.memset(scratch[:, 2:3], 0.0).then_inc(sem("ft_done"), 2)
            pool.memset(scratch[:, 3:4], 0.0).then_inc(sem("fdown_done"), 8)
            pool.memset(scratch[:, 4:5], 0.0).then_inc(sem("f_split"), 2)
            with pool.Fori(0, E1 // 4) as i:
                for s in range(2):
                    j = i * 2 + s
                    pool.wait_ge(sem(f"w_in{s}"), E0 // 2 * 16 + i * 16 + 16)
                    pool.wait_ge(sem("fdown_done"), i * 8 + 6 + 4 * s)
                    pool.tensor_tensor(W3h[s][:, :], W3[s][:, :], ones[:, 0:1].to_broadcast([128, 384]), ALU.mult).then_inc(sem("f_rounded"), 1)
                    pool.tensor_copy(fsel[s][:, :, :], sel2[:, ds(j * 2, 2)].rearrange("p (e o) -> p e o", o=1)
                                     .to_broadcast([128, 2, 64])).then_inc(sem("f_sel"), 1)
                    pool.wait_ge(sem("f_rounded"), j + 1)
                    pool.tensor_tensor(W3l[s][:, :], W3[s][:, :], W3h[s][:, :].bitcast(F32), ALU.subtract).then_inc(sem("f_split"), 1)
            ln_pool(pool, 5)

        @block.scalar
        def _(act):
            act.wait_ge(sem("ctx_pe"), CTX_PE["ck_ready"])
            act.activation(ce[:, :, :], bank(0).rearrange("p (a d) -> p a d", a=4), ACT.Exp).then_inc(sem("ctx_act"), 1)
            act.wait_ge(sem("ctx_pe"), CTX_PE["cv_ready"])
            act.activation(cv[:, :, :], bank(1).rearrange("p (a d) -> p a d", a=4), ACT.Copy).then_inc(sem("ctx_act"), 1)
            act.activation(wqh[:, :], wx[:, 3, :], ACT.Copy).then_inc(sem("ctx_act"), 1)
            act.wait_ge(sem("ctx_pool"), CTX_POOL["kn_done"])
            act.wait_ge(sem("ctx_pe"), CTX_PE["g2_ready"])
            for b in range(B):
                src = bank(5 + b % 2)[:, b // 2 * 128:b // 2 * 128 + 128]
                act.activation(G2[:, b, :], src, ACT.Copy, scale=kn[:, b:b + 1]).then_inc(sem("ctx_act"), 1)
            act.wait_ge(sem("ctx_pe"), CTX_PE["ke_ready"])
            act.activation(kTe[:, :], bank(0), ACT.Copy).then_inc(sem("ctx_act"), 1)
            act.wait_ge(sem("ctx_pe"), CTX_PE["ve_ready"])
            act.activation(vE[:, :, :], bank(1, CH, 2)[0:64, :].rearrange("p (b d) -> p b d", b=B), ACT.Copy).then_inc(sem("ctx_act"), 1)
            act.wait_ge(sem("ctx_pe"), CTX_PE["kk_ready"])
            act.activation(KK[:, :], bank(3), ACT.Copy, scale=1.0 / math.sqrt(D)).then_inc(sem("ctx_act"), 1)

            for n in range(8):
                act.wait_ge(sem("fold"), n + 1)
                dst = (NVh if n < 4 else Mh)[:, n % 4 * CH:n % 4 * CH + CH]
                act.activation(dst, bank(7 - n), ACT.Copy, scale=1.0 if n < 4 else -1.0 / math.sqrt(DH)).then_inc(sem("fold_hi"), 1)

            def split_x(b, slot):
                act.activation(xh[slot][:, :], xall[:, ds(b * S, S)] if not isinstance(b, int) else xall[:, b * S:b * S + S],
                               ACT.Copy).then_inc(sem("xh_done"), 1)

            act.wait_ge(sem("xT_in"), 16)
            act.wait_ge(sem("x_pad"), 1)
            split_x(0, 0)

            def exps(g, k):
                par, slot = (k - 1) % 2, (k - 1) % 4
                for q in range(4):
                    c, w = piece(q)
                    act.wait_ge(sem("masked"), g * 4 + q + 1)
                    last = act.activation(P[:, slot, c:c + w], P[:, slot, c:c + w], ACT.Exp, scale=-1.0,
                                          bias=mn[:, par, q:q + 1], accum_out=ls[:, par, q:q + 1])
                last.then_inc(sem("exp_done"), 1)

            with act.Fori(0, B // 2) as i:
                for k in range(STEPS):
                    g = i * STEPS + k
                    act.wait_ge(sem("u_ready"), g + 1)
                    act.activation(Uh[:, :], UB, ACT.Copy).then_inc(sem("u_hi"), 1)
                    exps(g, k)
                    act.wait_ge(sem("vo_ready"), g + 1)
                    t, q4 = k % 2, k % 8 // 2
                    act.activation(VO[:, t, 4 * q4:4 * q4 + 4, :], UB, ACT.Copy).then_inc(sem("vo_done"), 1)
                    if k in (4, 12):
                        split_x(i * 2 + (1 if k == 4 else 2), 1 if k == 4 else 0)
            exps(B * PAIRS, 0)
            ln_hi(act, 0)

            for c in range(NC_):
                act.wait_ge(sem("q_ready"), c + 1)
                act.activation(EQ[:, c * CH:c * CH + CH], bank(c), ACT.Exp, bias=bq[:, 0:1]).then_inc(sem("q_exp"), 1)
            for c in range(NC_):
                act.wait_ge(sem("q_norm"), c + 1)
                act.wait_ge(sem("q_neg"), NC_)
                act.wait_ge(sem("q_elu"), c + 1)
                act.activation(EQ[:, c * CH:c * CH + CH], bank(4 + c), ACT.Ln, scale=float(DX)).then_inc(sem("q_ln"), 1)
                act.wait_ge(sem("q_ln"), c + 1)
                act.activation(EQ[:, c * CH:c * CH + CH], EQ[:, c * CH:c * CH + CH], ACT.Exp, scale=-0.5).then_inc(sem("q_inv"), 1)
            act.wait_ge(sem("rms"), 4)
            for t in range(T):
                act.wait_ge(sem("ln_x"), T + t + 1)
                act.activation(XS[:, t, :], X[:, t, :], ACT.Copy, scale=rs2[:, t:t + 1]).then_inc(sem("xs_done"), 1)
            ln_hi(act, 1)
            for c in range(NC_):
                act.wait_ge(sem("router_T"), c + 1)
                act.activation(LT[:, c * CH:c * CH + CH], bank(4 + c)[0:16, :], ACT.Copy).then_inc(sem("router_out"), 1)
            act.wait_ge(sem("lg_sub"), 1)
            act.activation(Lg[:, :, :], Lg[:, :, :], ACT.Exp).then_inc(sem("lg_exp"), 1)
            for c in range(NC_):
                act.wait_ge(sem("gates_T"), c + 1)
                act.activation(SELT[:, c * CH:c * CH + CH], bank(4 + c), ACT.Copy).then_inc(sem("gates_out"), 1)

            def round_h(U, k):
                act.wait_ge(sem("h_done"), U + 2)
                act.activation(HH[:, (k - 1) % 4, :], Hf[:, (k - 1) % 4, :], ACT.Copy).then_inc(sem("hh_done"), 1)

            with act.Fori(0, E0 // 2) as i:
                for k in range(16):
                    U = i * 16 + k
                    act.wait_ge(sem("h_done"), U + 1)
                    act.wait_ge(sem("up_ready"), U + 1)
                    act.activation(SG[:, k % 2, :], bank(6 + k % 2), ACT.Silu).then_inc(sem("sg_done"), 1)
                    round_h(U, k)
            round_h(E0 * 8, 0)
            for c in range(NC_):
                act.wait_ge(sem("down_done"), E0 * 8 + 3 + 16)
                act.activation(OT[:, c * CH:c * CH + CH], bank(c), ACT.Copy).then_inc(sem("experts_out"), 1)
            ln_hi(act, 2)
            for first, end in SP_GROUPS:
                for t in range(first, end):
                    act.wait_ge(sem("dq_ready"), t + 1)
                    if t >= 2:
                        act.wait_ge(sem("pr_done"), t - 1)
                    act.activation(QS[:, t % 2, :], bank(4 + t % 2), ACT.Copy).then_inc(sem("qs_done"), 1)
                    act.wait_ge(sem("dz_ready"), t + 1)
                    act.activation(ZA[:, t, :], bank(6 + t % 2), ACT.Abs).then_inc(sem("z_abs"), 1)
                    act.wait_ge(sem("z_abs"), t + 1)
                    act.activation(ZA[:, t, :], ZA[:, t, :], ACT.Exp, scale=-1.0).then_inc(sem("z_exp"), 1)
                for t in range(first, end):
                    act.wait_ge(sem("z_exp"), t + 1)
                    act.activation(ZA[:, t, :], ZA[:, t, :], ACT.Ln, bias=1.0).then_inc(sem("z_ln"), 1)
            act.wait_ge(sem("ea_arg"), 1)
            act.activation(ea[:, :], ea[:, :], ACT.Exp).then_inc(sem("e_ab"), 1)
            act.activation(eb[:, :], eb[:, :], ACT.Exp).then_inc(sem("e_ab"), 1)

            def head_selector(b, slot):
                src = (sel2[:, ds(b, 64)] if not isinstance(b, int) else sel2[:, b:b + 64]).bitcast(F32)
                act.activation(dsel[slot][:, :, :], src.rearrange("p (h k) -> p h k", k=B)[:, :, 0:1].to_broadcast([128, H1, 128]),
                               ACT.Copy).then_inc(sem("dsel_done"), 1)

            head_selector(0, 0)
            act.wait_ge(sem("w_copied"), 2)
            with act.Fori(0, B // 2) as i:
                for k in range(2):
                    g = i * 2 + k
                    act.wait_ge(sem("scan2_done"), g + 1)
                    for r in range(4):
                        act.wait_ge(sem("w_bc"), g * 4 + r + 1)
                        act.activation(Wb[k][:, r * CH:r * CH + CH], bank(r % 2), ACT.Copy).then_inc(sem("w_copied"), 1)
                    act.wait_ge(sem("u_bc"), g * 4 + 1)
                    head_selector(g + 1, 1 - k)
                    act.wait_ge(sem("signed_done"), g + 1)
                    act.wait_ge(sem("scan1_done"), g + 2)
                    act.activation(sgb[:, :], r0b[k][:, :], ACT.Sign, bias=tiny[:, 0:1]).then_inc(sem("sgn_done"), 1)
                    act.wait_ge(sem("diff_done"), g + 2)
                    act.activation(dfb[k][:, :], dfb[k][:, :], ACT.Abs).then_inc(sem("abs_done"), 1)
            for c in range(NC_):
                act.wait_ge(sem("ln_T"), 3 * NC_ + c + 1)
                act.activation(XTf[:, c * CH:c * CH + CH], bank(c), ACT.Copy).then_inc(sem("ln_hi"), 1)
            act.wait_ge(sem("es_step"), 3 + 1)
            act.activation(SE[:, :, :], SE[:, :, :], ACT.Exp).then_inc(sem("e_exp"), 1)
            for c in range(NC_):
                act.wait_ge(sem("e_T"), c + 1)
                act.activation(PE_T[:, c * CH:c * CH + CH], bank(c)[0:64, :], ACT.Copy).then_inc(sem("e_pt"), 1)
            ln_hi(act, 4)
            for c in range(NC_):
                act.wait_ge(sem("router_T"), NC_ + c + 1)
                act.activation(FL[:, c * CH:c * CH + CH], bank(4 + c)[0:64, :], ACT.Copy).then_inc(sem("router_out"), 1)
            act.wait_ge(sem("logits_T"), 1 + 1)
            act.activation(SCo[:, :, :], bank(4, CH, 2).rearrange("p (t e) -> p t e", e=E1), ACT.Exp, scale=-1.0).then_inc(sem("f_exp"), 1)
            for c in range(NC_):
                act.wait_ge(sem("sh_g"), c + 1)
                if c >= 2:
                    act.wait_ge(sem("sh_h"), c - 1)
                act.activation(FG[:, c % 2, :], bank(6), ACT.Silu).then_inc(sem("sh_sg"), 1)
                act.wait_ge(sem("sh_h"), c + 1)
                act.activation(FHH[:, c % 2, :], FH[:, c % 2, :], ACT.Copy).then_inc(sem("sh_hh"), 1)
            for c in range(NC_):
                act.wait_ge(sem("gates_T"), NC_ + c + 1)
                act.activation(SELT1[:, c * CH:c * CH + CH], bank(4 + c), ACT.Copy).then_inc(sem("gates_out"), 1)

            def round_f(U, k):
                act.wait_ge(sem("fh_done"), U + 1)
                act.activation(FHH[:, (k - 1) % 4, :], FH[:, (k - 1) % 4, :], ACT.Copy).then_inc(sem("fhh_done"), 1)

            act.wait_ge(sem("sh_down"), NC_)
            with act.Fori(0, E1 // 4) as i:
                for k in range(8):
                    U = i * 8 + k
                    act.wait_ge(sem("ft_done"), U + 1)
                    act.wait_ge(sem("g_ready"), U + 1)
                    act.activation(FG[:, k % 2, :], bank(4 + k % 2), ACT.Silu).then_inc(sem("fg_done"), 1)
                    round_f(U, k)
            round_f(E1 * 2, 0)
            act.wait_ge(sem("fdown_done"), E1 * 2 + 2 + 8)
            for c in range(NC_):
                act.activation(OT1[:, c * CH:c * CH + CH], bank(c), ACT.Copy).then_inc(sem("experts_out"), 1)

        @block.vector
        def _(dve):
            dve.wait_ge(sem("consts"), 5)
            dve.memset(sel2[:, 64:72].bitcast(F32), 0.0)
            dve.tensor_tensor(sel2[:, 0:64], ident[:, 0:64], ident[:, 64:128], ALU.add).then_inc(sem("sel2_done"), 1)
            dve.tensor_reduce(halfones[:, :], ident[:, :].rearrange("p (a c) -> p a c", a=2), AX.X, ALU.add).then_inc(sem("halves"), 1)
            dve.wait_ge(sem("ctx_act"), CTX_ACT["ck_exp"])
            dve.tensor_scalar(ck[:, :, :], bank(0).rearrange("p (a d) -> p a d", a=4), 0.0, None, ALU.max).then_inc(sem("ctx_dve"), 1)
            dve.wait_ge(sem("ctx_pool"), CTX_POOL["ck_neg"])
            dve.wait_ge(sem("ctx_dve"), CTX_DVE["ck_pos"])
            dve.tensor_tensor(ck[:, :, :], ck[:, :, :], ce[:, :, :], ALU.add).then_inc(sem("ctx_dve"), 1)
            dve.wait_ge(sem("ctx_pe"), CTX_PE["kn_ready"])
            dve.tensor_scalar(kn[:, :], bank(2, B), float(S), None, ALU.mult).then_inc(sem("ctx_dve"), 1)
            dve.wait_ge(sem("ctx_pe"), CTX_PE["gt_ready"])
            dve.tensor_tensor(GBT[:, :, :], bank(3, CH, 2).rearrange("p (b d) -> p b d", b=B),
                              blockones[:, :].rearrange("p (o d) -> p o d", o=1).to_broadcast([128, B, 128]),
                              ALU.mult).then_inc(sem("ctx_dve"), 1)
            dve.wait_ge(sem("ctx_act"), CTX_ACT["wq_hi"])
            dve.tensor_tensor(wql[:, :], wx[:, 3, :], wqh[:, :].bitcast(F32), ALU.subtract).then_inc(sem("ctx_dve"), 1)
            dve.wait_ge(sem("wr_in"), 16)
            dve.wait_ge(sem("wr_zero"), 2)
            dve.tensor_copy(wrh[:, 0:E0R], wr_in[:, :]).then_inc(sem("ctx_dve"), 1)
            dve.wait_ge(sem("ctx_dve"), CTX_DVE["wr_split"] - 1)
            dve.tensor_tensor(wrl[:, 0:E0R], wr_in[:, :], wrh[:, 0:E0R].bitcast(F32), ALU.subtract).then_inc(sem("ctx_dve"), 1)

            dve.memset(tiny[:, :], 1e-37)
            dve.memset(abr[:, :].bitcast(F32), 0.0).then_inc(sem("abr_zero"), 1)
            dve.memset(onesr[:, :].bitcast(F32), 1.0).then_inc(sem("l1_split"), 1)
            dve.wait_ge(sem("l1_in"), 16 * 7)
            dve.memset(wr1h[:, :].bitcast(F32), 0.0).then_inc(sem("wr1"), 1)
            dve.memset(wr1l[:, :].bitcast(F32), 0.0).then_inc(sem("wr1"), 1)
            dve.wait_ge(sem("wr1"), 2)
            dve.tensor_copy(wr1h[:, 0:E1], wr1_in[:, :]).then_inc(sem("wr1"), 1)
            dve.tensor_copy(wdh[:, :], wd_in[:, :]).then_inc(sem("wr1"), 1)
            dve.tensor_copy(wshh[:, :], wsh[:, :]).then_inc(sem("wr1"), 1)
            dve.wait_ge(sem("abr_zero"), 1)
            dve.tensor_copy(abr[0:1, :], abias[:, :]).then_inc(sem("wr1"), 1)
            dve.wait_ge(sem("wr1"), 6)
            dve.tensor_tensor(abr[32:33, :], abias[:, :], abr[0:1, :].bitcast(F32), ALU.subtract).then_inc(sem("l1_split"), 1)
            dve.tensor_tensor(wr1l[:, 0:E1], wr1_in[:, :], wr1h[:, 0:E1].bitcast(F32), ALU.subtract).then_inc(sem("l1_split"), 1)
            dve.tensor_tensor(wdl[:, :], wd_in[:, :], wdh[:, :].bitcast(F32), ALU.subtract).then_inc(sem("l1_split"), 1)
            dve.tensor_scalar(wo1e[:, :], wo1[:, :], EPS / 2, None, ALU.mult)
            dve.tensor_tensor(wshl[:, :], wsh[:, :], wshh[:, :].bitcast(F32), ALU.subtract).then_inc(sem("l1_split"), 1)

            for n in range(8):
                dve.wait_ge(sem("fold_hi"), n + 1)
                cols = slice(n % 4 * CH, n % 4 * CH + CH)
                hi, lo = (NVh, NVl) if n < 4 else (Mh, Ml)
                dve.scalar_tensor_tensor(lo[:, cols], bank(7 - n), 1.0 if n < 4 else -1.0 / math.sqrt(DH),
                                         hi[:, cols].bitcast(F32), ALU.mult, ALU.subtract).then_inc(sem("fold_lo"), 1)

            def split_x(b, slot):
                dve.tensor_tensor(xl[slot][:, :], xall[:, ds(b * S, S)] if not isinstance(b, int) else xall[:, b * S:b * S + S],
                                  xh[slot][:, :].bitcast(F32), ALU.subtract).then_inc(sem("xl_done"), 1)

            dve.wait_ge(sem("xh_done"), 1)
            split_x(0, 0)
            dve.wait_ge(sem("fold_hi"), 8)
            dve.wait_ge(sem("fold_lo"), 8)
            dve.memset(bank(2, CH, 2), 0.0).then_inc(sem("s_ready"), 1)
            dve.memset(bank(7), 0.0).then_inc(sem("acc_free"), 1)
            dve.memset(Xp[:, 0:S], 0.0)
            dve.wait_ge(sem("x_in"), 16)

            def mask_and_max(g, k):
                par, slot = (k - 1) % 2, (k - 1) % 4
                dve.wait_ge(sem("s_ready"), g + 1)
                dve.memset(scratch[:, 5:6], 0.0)
                for q in range(4):
                    c, w = piece(q)
                    dve.tensor_tensor_reduce(out=P[:, slot, c:c + w], in0=scores(par, q), in1=cmask[:, 256 - w:256],
                                             scale=1.0, scalar=3e38, op0=ALU.add, op1=ALU.min,
                                             accum_out=mn[:, par, q:q + 1]).then_inc(sem("masked"), 1)

            def invert(g, k):
                par = (k - 1) % 2
                dve.wait_ge(sem("exp_done"), g + 1)
                dve.reciprocal(rl[:, par, :], ls[:, par, :]).then_inc(sem("rl_done"), 1)

            def copy_pt(g, k):
                dve.wait_ge(sem("t_ready"), g + 1)
                dve.tensor_copy(PT[:, k % 2, :, :], PTP).then_inc(sem("pt_done"), 1)

            def add_out(b, g):
                dve.wait_ge(sem("pv_done"), g + 1)
                x = Xp[:, ds(b * S, S)] if not isinstance(b, int) else Xp[:, b * S:b * S + S]
                dve.tensor_tensor(x, x, OB[:, 0:256], ALU.add).then_inc(sem("acc_free"), 1)

            with dve.Fori(0, B // 2) as i:
                for k in range(STEPS):
                    g = i * STEPS + k
                    mask_and_max(g, k)
                    dve.wait_ge(sem("u_hi"), g + 1)
                    dve.tensor_tensor(Ul[:, :], UB, Uh[:, :].bitcast(F32), ALU.subtract).then_inc(sem("u_lo"), 1)
                    copy_pt(g, k)
                    if k in (2, 10):
                        add_out(i * 2 + k // 8, g)
                    invert(g, k)
                    if k in (4, 12):
                        dve.wait_ge(sem("xh_done"), i * 2 + (2 if k == 4 else 3))
                        split_x(i * 2 + (1 if k == 4 else 2), 1 if k == 4 else 0)
            G = B * PAIRS
            mask_and_max(G, 0)
            copy_pt(G, 0)
            invert(G, 0)
            copy_pt(G + 1, 1)
            add_out(B, G + 2)
            dve.wait_ge(sem("acc_free"), B + 2)
            ln_vector(dve, 0)
            ln_lo(dve, 0)

            for c in range(NC_):
                dve.wait_ge(sem("q_exp"), c + 1)
                dve.tensor_scalar(RQ[:, c * CH:c * CH + CH], bank(c), bq[:, 0:1], 0.0, ALU.add, ALU.max).then_inc(sem("q_pos"), 1)
            for c in range(NC_):
                cc = slice(c * CH, c * CH + CH)
                dve.wait_ge(sem("q_pos"), c + 1)
                dve.wait_ge(sem("q_neg"), c + 1)
                dve.tensor_tensor(Q[:, cc], EQ[:, cc], RQ[:, cc], ALU.add).then_inc(sem("q_elu"), 1)
            for c in range(NC_):
                cc = slice(c * CH, c * CH + CH)
                dve.wait_ge(sem("q_sq"), c + 1)
                dve.wait_ge(sem("q_inv"), c + 1)
                dve.tensor_tensor(Q[:, cc], Q[:, cc], EQ[:, cc], ALU.mult).then_inc(sem("q_done"), 1)
            for c in range(NC_):
                dve.wait_ge(sem("b_out"), c + 1)
                x = Xp[:, S + c * CH:S + c * CH + CH]
                dve.tensor_tensor(x, x, bank(c), ALU.add).then_inc(sem("x_added"), 1)
            dve.wait_ge(sem("x_added"), NC_)
            ln_vector(dve, 1)
            ln_lo(dve, 1)
            dve.wait_ge(sem("rms"), 4)
            dve.reciprocal(lm[:, :], rs2[:, :]).then_inc(sem("g_step"), 1)
            dve.wait_ge(sem("g_step"), 1)
            dve.wait_ge(sem("logits_T"), 1)
            bc = lambda v, w: v.rearrange("p (t o) -> p t o", o=1).to_broadcast([128, T, w])
            dve.tensor_tensor(Lg[:, :, :], bank(0, 256).rearrange("p (t e) -> p t e", e=16)[:, :, 0:E0R],
                              bc(lm[:, :], E0R), ALU.mult).then_inc(sem("g_step"), 1)
            dve.wait_ge(sem("g_step"), 2)
            dve.tensor_reduce(lz[:, :], Lg[:, :, :], AX.X, ALU.max).then_inc(sem("g_step"), 1)
            dve.wait_ge(sem("g_step"), 3)
            dve.tensor_tensor(Lg[:, :, :], Lg[:, :, :], bc(lz[:, :], E0R), ALU.subtract).then_inc(sem("lg_sub"), 1)
            dve.wait_ge(sem("lg_exp"), 1)
            dve.tensor_reduce(lm[:, :], Lg[:, :, :], AX.X, ALU.add).then_inc(sem("g_step"), 1)
            dve.wait_ge(sem("g_step"), 4)
            dve.reciprocal(lz[:, :], lm[:, :]).then_inc(sem("g_step"), 1)
            dve.wait_ge(sem("g_step"), 5)
            dve.wait_ge(sem("g20_init"), 2)
            dve.tensor_tensor(G20[:, :, 0:E0R], Lg[:, :, :], bc(lz[:, :], E0R), ALU.mult).then_inc(sem("g_step"), 1)
            dve.wait_ge(sem("g_step"), 6)
            for t in range(T):
                last = dve.max(M8[:, t, :], G20[:, t, :])
            last.then_inc(sem("g_step"), 1)
            dve.wait_ge(sem("g_step"), 7)
            dve.tensor_copy(RPL[:, :, 0:2], M8[:, :, 0:2]).then_inc(sem("g_step"), 1)
            dve.wait_ge(sem("g_step"), 8)
            for t in range(T):
                last = dve.match_replace(RP[:, t, :], RPL[:, t, :], G20[:, t, :], -5.0)
            last.then_inc(sem("g_step"), 1)
            dve.wait_ge(sem("g_step"), 9)
            dve.scalar_tensor_tensor(Lg[:, :, :], RP[:, :, 0:E0R], -4.0, G20[:, :, 0:E0R], ALU.is_lt, ALU.mult).then_inc(sem("g_step"), 1)
            dve.wait_ge(sem("g_step"), 10)
            dve.tensor_reduce(lm[:, :], Lg[:, :, :], AX.X, ALU.add).then_inc(sem("g_step"), 1)
            dve.wait_ge(sem("g_step"), 11)
            dve.tensor_scalar(lm[:, :], lm[:, :], 1e-9, None, ALU.add).then_inc(sem("g_step"), 1)
            dve.wait_ge(sem("g_step"), 12)
            dve.reciprocal(lz[:, :], lm[:, :]).then_inc(sem("g_step"), 1)
            dve.wait_ge(sem("g_step"), 13)
            dve.tensor_tensor(Lg[:, :, :], Lg[:, :, :], bc(lz[:, :], E0R), ALU.mult).then_inc(sem("g_step"), 1)
            dve.wait_ge(sem("g_step"), 14)
            dve.wait_ge(sem("gi_zero"), 2)
            dve.tensor_copy(GI[:, :, 0:E0R], Lg[:, :, :]).then_inc(sem("g_step"), 1)
            dve.wait_ge(sem("g_step"), 15)
            dve.tensor_tensor(GI[:, :, 64:64 + E0R], Lg[:, :, :], GI[:, :, 0:E0R].bitcast(F32), ALU.subtract).then_inc(sem("gates_split"), 1)

            def rest_h(U, k):
                dve.wait_ge(sem("hh_done"), U + 1)
                dve.tensor_tensor(HL[:, (k - 1) % 4, :], Hf[:, (k - 1) % 4, :], HH[:, (k - 1) % 4, :].bitcast(F32),
                                  ALU.subtract).then_inc(sem("hl_done"), 1)

            with dve.Fori(0, E0 // 2) as i:
                for k in range(16):
                    U = i * 16 + k
                    if k % 2 == 0:
                        dve.wait_ge(sem("gb_ready"), i * 8 + k // 2 + 1)
                    dve.wait_ge(sem("sg_done"), U + 3)
                    dve.tensor_tensor(Hf[:, k % 4, :], SG[:, k % 2, :], bank(4 + k // 2 % 2), ALU.mult).then_inc(sem("h_done"), 1)
                    rest_h(U, k)
            rest_h(E0 * 8, 0)
            dve.wait_ge(sem("experts_T"), NC_)
            ln_vector(dve, 2, lambda t: bank(4 + t // 4)[:, t % 4 * 128:t % 4 * 128 + 128])
            ln_lo(dve, 2)
            def softplus_sums(first, end):
                dve.wait_ge(sem("z_sp"), end)
                dve.tensor_reduce(ABs[:, 0, first:end, :].rearrange("p t h -> p (t h)"),
                                  ZR[:, first:end, :].rearrange("p t (h d) -> p (t h) d", h=H1), AX.X, ALU.add).then_inc(sem("ab_sums"), 1)

            def signed_values(c):
                cc = slice(c * CH, c * CH + CH)
                dve.wait_ge(sem("dv_ready"), c + 1)
                dve.tensor_scalar(VS[:, cc], bank(c % 2), 0.0, 2 * EPS, ALU.is_ge, ALU.mult).then_inc(sem("vp_done"), 1)
                dve.wait_ge(sem("vp_done"), 2 * c + 1)
                dve.scalar_tensor_tensor(VP[:, cc], bank(c % 2), EPS, VS[:, cc], ALU.subtract, ALU.add).then_inc(sem("vp_done"), 1)

            for t in range(T):
                p = t % 2
                dve.wait_ge(sem("qs_done"), t + 1)
                dve.wait_ge(sem("dk_ready"), t + 1)
                dve.tensor_tensor(PR[:, p, :], bank(2 + p), QS[:, p, :], ALU.mult).then_inc(sem("pr_done"), 1)
                dve.wait_ge(sem("z_abs"), t + 1)
                dve.tensor_scalar(ZR[:, t, :], bank(6 + p), 0.0, None, ALU.max).then_inc(sem("z_pos"), 1)
                dve.wait_ge(sem("pr_done"), t + 1)
                dve.tensor_reduce(ABs[:, 1, t, :], PR[:, p, :].rearrange("p (h d) -> p h d", h=H1), AX.X, ALU.add).then_inc(sem("b_sum"), 1)
                if t % 4 == 3:
                    signed_values(t // 4)
                for first, end in SP_GROUPS:
                    if t == end + 1:
                        softplus_sums(first, end)
            softplus_sums(*SP_GROUPS[-1])
            dve.wait_ge(sem("b_sum"), T)
            dve.wait_ge(sem("ab_sums"), len(SP_GROUPS))
            for n, scale in ((1, 1.0 / math.sqrt(64)), (0, -1.0)):
                src = ABs[:, n, :, :].rearrange("p (b r) h -> p r h b", r=2)
                for r in range(2):
                    dve.tensor_scalar(ABt[:, r, n, :, :], src[:, r, :, :], scale, None, ALU.mult).then_inc(sem("ab_placed"), 1)
            dve.wait_ge(sem("ab_T"), 1)
            dve.tensor_copy(AB64[:, :, :], bank(2)[0:64, :].rearrange("p (n t) -> p n t", n=2)).then_inc(sem("ab_in"), 1)
            dve.wait_ge(sem("ab_in"), 1)
            dve.wait_ge(sem("d_init"), 2)
            av, bv = AB64[:, 0, :], AB64[:, 1, :]
            dve.tensor_tensor_scan(mb[:, 1:], av, bv, -BIG, ALU.add, ALU.max).then_inc(sem("r_step"), 1)
            dve.wait_ge(sem("r_step"), 1)
            dve.tensor_tensor(ea[:, :], av, mb[:, 0:S], ALU.add).then_inc(sem("r_step"), 1)
            dve.tensor_tensor(eb[:, :], bv, mb[:, 1:], ALU.subtract).then_inc(sem("r_step"), 1)
            dve.wait_ge(sem("r_step"), 3)
            dve.tensor_tensor(ea[:, :], ea[:, :], mb[:, 1:], ALU.subtract).then_inc(sem("ea_arg"), 1)
            dve.wait_ge(sem("e_ab"), 2)
            dve.tensor_tensor_scan(db[:, 1:], ea[:, :], eb[:, :], 0.0, ALU.mult, ALU.add).then_inc(sem("r_step"), 1)
            dve.wait_ge(sem("r_step"), 4)
            dve.reciprocal(rd[:, :], db[:, 1:]).then_inc(sem("r_step"), 1)
            dve.tensor_tensor(ea[:, :], ea[:, :], db[:, 0:S], ALU.mult).then_inc(sem("r_step"), 1)
            dve.wait_ge(sem("r_step"), 6)
            dve.tensor_tensor(wu[:, 0, :], ea[:, :], rd[:, :], ALU.mult).then_inc(sem("r_step"), 1)
            dve.tensor_tensor(wu[:, 1, :], eb[:, :], rd[:, :], ALU.mult).then_inc(sem("r_step"), 1)
            dve.wait_ge(sem("r_step"), 8)
            dve.tensor_copy(WUr[0:64, :, :], wu[:, :, :]).then_inc(sem("r_step"), 1)
            dve.wait_ge(sem("r_step"), 9)
            dve.tensor_tensor(WUr[64:128, :, :], wu[:, :, :], WUr[0:64, :, :].bitcast(F32), ALU.subtract).then_inc(sem("wu_done"), 1)
            dve.memset(scratch[:, 6:7], 0.0).then_inc(sem("qr_done"), 1)
            dve.memset(scratch[:, 7:8], 0.0).then_inc(sem("u_bc"), 1)
            dve.memset(bank(3), 0.0).then_inc(sem("scan1_done"), 1)
            dve.memset(scratch[:, 10:11], 0.0).then_inc(sem("diff_done"), 1)
            dve.memset(scratch[:, 8:9], 0.0).then_inc(sem("y0_done"), 1)
            dve.memset(scratch[:, 9:10], 0.0).then_inc(sem("y1_done"), 1)

            def last_scan(g, par):
                dve.wait_ge(sem("floor_done"), g + 2)
                dve.wait_ge(sem("y1_done"), g + 1)
                dve.tensor_tensor_scan(rb[1 - par][:, :], Wb[1 - par][:, :], gb[1 - par][:, :], 0.0, ALU.mult, ALU.add).then_inc(sem("scan2_done"), 1)

            dve.wait_ge(sem("w_copied"), 2)
            dve.wait_ge(sem("signed_done"), 1)
            with dve.Fori(0, B // 2) as i:
                for k in range(2):
                    g = i * 2 + k
                    dve.wait_ge(sem("diff_done"), g + 1)
                    for r in range(4):
                        dve.wait_ge(sem("u_bc"), g * 4 + r + 2)
                        v = VP[:, ds(g * S, S)].rearrange("p (o t) -> p o t", o=1).to_broadcast([128, 2, S])
                        dve.tensor_tensor(qb[:, r * CH:r * CH + CH].rearrange("p (h t) -> p h t", h=2),
                                          bank(2).rearrange("p (h t) -> p h t", h=2), v, ALU.mult).then_inc(sem("qr_done"), 1)
                    dve.wait_ge(sem("qr_done"), g * 4 + 5)
                    dve.wait_ge(sem("w_copied"), g * 4 + 6)
                    dve.wait_ge(sem("y0_done"), g + 1)
                    dve.wait_ge(sem("floor_done"), g + 1)
                    dve.tensor_tensor_scan(r0b[k][:, :], Wb[k][:, :], qb[:, :], 0.0, ALU.mult, ALU.add).then_inc(sem("scan1_done"), 1)
                    dve.wait_ge(sem("scan1_done"), g + 2)
                    dve.scalar_tensor_tensor(dfb[k][:, :], qb[:, :], -2.0, r0b[k][:, :], ALU.mult, ALU.add).then_inc(sem("diff_done"), 1)
                    last_scan(g, k)
            last_scan(B, 0)
            dve.wait_ge(sem("y1_done"), B + 3)
            for c in range(NC_):
                x = Xp[:, S + c * CH:S + c * CH + CH]
                dve.tensor_tensor(x, x, bank(4 + c), ALU.add).then_inc(sem("x_added"), 1)
            dve.wait_ge(sem("x_added"), NC_ + NC_)
            ln_vector(dve, 3)
            dve.wait_ge(sem("es_ready"), 1)
            sc_ = bank(4, CH, 2).rearrange("p (b r s) -> p b r s", b=B, r=2)
            sev = SE[:, :, :].rearrange("p (b r) s -> p b r s", r=2)
            dve.tensor_tensor(sev[:, :, 0, :], sc_[:, :, 0, :], cmask[:, 128:192].rearrange("p (o s) -> p o s", o=1)
                              .to_broadcast([128, B, SC]), ALU.subtract).then_inc(sem("es_step"), 1)
            dve.tensor_copy(sev[:, :, 1, :], sc_[:, :, 1, :]).then_inc(sem("es_step"), 1)
            dve.wait_ge(sem("es_step"), 2)
            dve.tensor_reduce(em[:, :], SE[:, :, :], AX.X, ALU.max).then_inc(sem("es_step"), 1)
            dve.wait_ge(sem("es_step"), 3)
            dve.tensor_tensor(SE[:, :, :], SE[:, :, :], bc(em[:, :], SC), ALU.subtract).then_inc(sem("es_step"), 1)
            dve.wait_ge(sem("e_exp"), 1)
            dve.tensor_reduce(em[:, :], SE[:, :, :], AX.X, ALU.add).then_inc(sem("es_step"), 1)
            dve.wait_ge(sem("es_step"), 5)
            dve.reciprocal(el[:, :], em[:, :]).then_inc(sem("es_step"), 1)
            for c in range(NC_):
                dve.wait_ge(sem("e_out"), c + 1)
                x = Xp[:, S + c * CH:S + c * CH + CH]
                dve.tensor_tensor(x, x, bank(4 + c), ALU.add).then_inc(sem("x_added"), 1)
            dve.wait_ge(sem("x_added"), 2 * NC_ + NC_)
            ln_vector(dve, 4)
            ln_lo(dve, 4)
            nf = [0]

            def link(ins):
                nf[0] += 1
                ins.then_inc(sem("f_step"), 1)
                dve.wait_ge(sem("f_step"), nf[0])

            dve.wait_ge(sem("f_exp"), 1)
            link(dve.tensor_scalar(SCo[:, :, :], SCo[:, :, :], 1.0, None, ALU.add))
            link(dve.reciprocal(SCo[:, :, :], SCo[:, :, :]))
            link(dve.tensor_tensor(SF[:, :, :], SCo[:, :, :], ebias[:, :].rearrange("p (o e) -> p o e", o=1)
                                   .to_broadcast([128, T, E1]), ALU.add))
            g8 = SF[:, :, :].rearrange("p t (g e) -> p (t g) e", e=8)
            dve.tensor_tensor(h1[:, :, :], g8[:, :, 0:4], g8[:, :, 4:8], ALU.max)
            link(dve.tensor_tensor(l1[:, :, :], g8[:, :, 0:4], g8[:, :, 4:8], ALU.min))
            dve.tensor_tensor(h2[:, :, :], h1[:, :, 0:2], h1[:, :, 2:4], ALU.max)
            dve.tensor_tensor(t2[:, :, :], h1[:, :, 0:2], h1[:, :, 2:4], ALU.min)
            link(dve.tensor_tensor(l2[:, :, :], l1[:, :, 0:2], l1[:, :, 2:4], ALU.max))
            link(dve.tensor_tensor(l2[:, :, :], l2[:, :, :], t2[:, :, :], ALU.max))
            dve.tensor_tensor(h3[:, :, :], h2[:, :, 0:1], h2[:, :, 1:2], ALU.max)
            dve.tensor_tensor(t3[:, :, :], h2[:, :, 0:1], h2[:, :, 1:2], ALU.min)
            link(dve.tensor_tensor(l3[:, :, :], l2[:, :, 0:1], l2[:, :, 1:2], ALU.max))
            link(dve.tensor_tensor(l3[:, :, :], l3[:, :, :], t3[:, :, :], ALU.max))
            dve.wait_ge(sem("f_init"), 5)
            tg = lambda x: x[:, :, :].rearrange("p (t g) o -> p t (g o)", g=8)
            link(dve.tensor_tensor(GS[:, :, 0:8], tg(h3), tg(l3), ALU.add))
            for t in range(T):
                last = dve.max(F8[:, t, :], GS[:, t, 0:8])
            link(last)
            link(dve.tensor_copy(FR[:, :, 0:4], F8[:, :, 0:4]))
            for t in range(T):
                last = dve.match_replace(GR[:, t, :], FR[:, t, :], GS[:, t, :], -NEG)
            link(last)
            link(dve.tensor_scalar(gm[:, :, :], GR[:, :, 0:8], 2.9e38, None, ALU.is_ge))
            link(dve.tensor_tensor(FM[:, :, :].rearrange("p t (g e) -> p (t g) e", e=8), g8,
                                   gm[:, :, :].rearrange("p t (g o) -> p (t g) o", o=1).to_broadcast([128, T * 8, 8]), ALU.mult))
            link(dve.tensor_scalar(FM[:, :, :], FM[:, :, :], 0.0, None, ALU.add))
            for t in range(T):
                last = dve.max(F8[:, t, :], FM[:, t, :])
            link(last)
            for t in range(T):
                last = dve.match_replace(FRP[:, t, :], F8[:, t, :], FM[:, t, :], NEG)
            link(last)
            link(dve.scalar_tensor_tensor(FM[:, :, :], FRP[:, :, :], -2.9e38, SCo[:, :, :], ALU.is_le, ALU.mult))
            link(dve.tensor_reduce(fs[:, :], FM[:, :, :], AX.X, ALU.add))
            link(dve.tensor_scalar(fs[:, :], fs[:, :], 1e-20, None, ALU.add))
            link(dve.reciprocal(fi[:, :], fs[:, :]))
            link(dve.tensor_scalar(fi[:, :], fi[:, :], 2.5, None, ALU.mult))
            link(dve.tensor_tensor(FM[:, :, :], FM[:, :, :], bc(fi[:, :], E1), ALU.mult))
            link(dve.tensor_copy(GI1[:, :, 0:64], FM[:, :, :]))
            dve.tensor_tensor(GI1[:, :, 64:128], FM[:, :, :], GI1[:, :, 0:64].bitcast(F32), ALU.subtract).then_inc(sem("gates_split"), 1)
            for c in range(NC_):
                dve.wait_ge(sem("sh_u"), c + 1)
                dve.wait_ge(sem("sh_sg"), c + 1)
                dve.tensor_tensor(FH[:, c % 2, :], FG[:, c % 2, :], bank(7), ALU.mult).then_inc(sem("sh_h"), 1)
                dve.wait_ge(sem("sh_hh"), c + 1)
                if c >= 2:
                    dve.wait_ge(sem("sh_down"), c - 1)
                dve.tensor_tensor(FHL[:, c % 2, :], FH[:, c % 2, :], FHH[:, c % 2, :].bitcast(F32), ALU.subtract).then_inc(sem("sh_hl"), 1)

            def rest_f(U, k):
                dve.wait_ge(sem("fhh_done"), U + 1)
                dve.tensor_tensor(FHL[:, (k - 1) % 4, :], FH[:, (k - 1) % 4, :], FHH[:, (k - 1) % 4, :].bitcast(F32),
                                  ALU.subtract).then_inc(sem("fhl_done"), 1)

            dve.wait_ge(sem("sh_hl"), NC_)
            dve.wait_ge(sem("sh_down"), NC_)
            with dve.Fori(0, E1 // 4) as i:
                for k in range(8):
                    U = i * 8 + k
                    dve.wait_ge(sem("fg_done"), U + 3)
                    dve.wait_ge(sem("fu_ready"), U + 1)
                    dve.tensor_tensor(FU[:, k % 2, :], FG[:, k % 2, :], bank(6), ALU.mult).then_inc(sem("ft_done"), 1)
                    rest_f(U, k)
                    dve.wait_ge(sem("ft_done"), U + 3)
                    dve.wait_ge(sem("fgb_ready"), U + 1)
                    dve.tensor_tensor(FH[:, k % 4, :], FU[:, k % 2, :], bank(7), ALU.mult).then_inc(sem("fh_done"), 1)
            rest_f(E1 * 2, 0)
            dve.wait_ge(sem("experts_T"), NC_ + NC_)
            ln_vector(dve, 5, lambda t: bank(4 + t // 4)[:, t % 4 * 128:t % 4 * 128 + 128])

        @block.tensor
        def _(pe):
            pe.wait_ge(sem("ctx_in"), 64)
            pe.wait_ge(sem("consts"), 5)
            for n in range(2):
                for p in range(4):
                    dst = bank(n)[:, p * 128:p * 128 + 128]
                    pe.matmul(dst, ctxT[:, p * 128:p * 128 + 128], wx[:, n, :], start=True, stop=False)
                    last = pe.matmul(dst, ones[0:1, :], brow[0:1, n * 128:n * 128 + 128], start=False, stop=True)
                last.then_inc(sem("ctx_pe"), 1)
            pe.wait_ge(sem("halves"), 1)
            pe.wait_ge(sem("ctx_pool"), CTX_POOL["ck_sq"])
            for p in range(4):
                last = pe.matmul(bank(2)[:, 2 * p:2 * p + 2], csq[:, p, :], halfones[:, :], start=True, stop=True)
            last.then_inc(sem("ctx_pe"), 1)
            pe.wait_ge(sem("ctx_dve"), CTX_DVE["ck_done"])
            pe.wait_ge(sem("ctx_act"), CTX_ACT["cv_done"])
            for b in range(B):
                r = slice(b % 2 * 64, b % 2 * 64 + 64)
                last = pe.matmul(bank(3 + b % 2)[:, b // 2 * 128:b // 2 * 128 + 128], cv[r, b // 2, :], ck[r, b // 2, :],
                                 start=True, stop=True)
            last.then_inc(sem("ctx_pe"), 1)
            pe.wait_ge(sem("ctx_dve"), CTX_DVE["gbt_done"])
            for b in range(B):
                last = pe.matmul(bank(5 + b % 2)[:, b // 2 * 128:b // 2 * 128 + 128], GBT[:, b % 2 * 4 + b // 2, :], wx[:, 2, :],
                                 start=True, stop=True)
            last.then_inc(sem("ctx_pe"), 1)
            pe.wait_ge(sem("ctx_act"), CTX_ACT["g2_done"])
            pe.wait_ge(sem("l1_in"), 16 * 7)
            pe.matmul(bank(0), wqe[:, 0, :], ctxT[:, :], start=True, stop=True).then_inc(sem("ctx_pe"), 1)
            for b in range(B):
                last = pe.matmul(bank(1 + b // 4)[0:64, b % 4 * 128:b % 4 * 128 + 128], ctxT[:, b * SC:b * SC + SC], wqe[:, 0, :],
                                 start=True, stop=True)
            last.then_inc(sem("ctx_pe"), 1)
            pe.wait_ge(sem("ctx_act"), CTX_ACT["ke_done"])
            pe.matmul(bank(3), wqe[:, 1, :], kTe[:, :], start=True, stop=True).then_inc(sem("ctx_pe"), 1)
            pe.wait_ge(sem("ctx_act"), CTX_ACT["kk_done"])

            pe.wait_ge(sem("w64_in"), 64)
            for n in range(8):
                l, r = (w64["v"], w64["o"]) if n < 4 else (w64["q"], w64["k"])
                for h in range(4):
                    last = pe.matmul(bank(7 - n)[:, h * 128:h * 128 + 128], l[:, n % 4 * 4 + h, :], r[:, n % 4 * 4 + h, :],
                                     start=True, stop=True)
                last.then_inc(sem("fold"), 1)

            def mm3(dst, l, r, start=True, stop=True, skip=False):
                pe.matmul(dst, l[0], r[0], start=start, stop=False, skip_group_check=skip)
                pe.matmul(dst, l[0], r[1], start=False, stop=False, skip_group_check=skip)
                return pe.matmul(dst, l[1], r[0], start=False, stop=stop, skip_group_check=skip)

            def project_u(g, k):
                b, p = k // PAIRS, k % PAIRS
                for h in range(2):
                    w = slice((2 * p + h) * 128, (2 * p + h) * 128 + 128)
                    last = mm3(UB[:, h * S:h * S + S], (Mh[:, w], Ml[:, w]), (xh[b][:, :], xl[b][:, :]))
                last.then_inc(sem("u_ready"), 1)

            def transposes(g, k):
                slot = (k - 2) % 4
                pe.wait_ge(sem("norm_done"), g + 1)
                pe.wait_ge(sem("pt_done"), g + 1)
                for h in range(2):
                    for j, c in enumerate((h * 128, 256 + h * 256, 384 + h * 256)):
                        last = pe.transpose(bank(4 + h)[:, j * 128:j * 128 + 128], P[:, slot, c:c + 128], ident[:, :])
                last.then_inc(sem("t_ready"), 1)

            def weighted_sums(g, k, turn=None):
                p, par = (k - 3) % PAIRS, (k - 3) % 2
                pe.wait_ge(sem("pt_done"), g + 1)
                if p == 0:
                    pe.wait_ge(sem("acc_free"), turn * 2 + k // PAIRS + 2)
                for h in range(2):
                    for dst, blk, half in ((0, 0, 0), (128, 1, 0), (128, 2, 1)):
                        first = p == 0 and h == 0 and dst == 0
                        last = pe.matmul(OB[:, dst:dst + 128], PT[:, par, h, blk * 128:blk * 128 + 128],
                                         VO[:, half, 2 * p + h, :], start=first, stop=(p == PAIRS - 1 and h == 1),
                                         skip_group_check=True)
                last.then_inc(sem("pv_done"), 1)

            pe.wait_ge(sem("fold_lo"), 8)
            pe.wait_ge(sem("consts"), 5)
            pe.wait_ge(sem("acc_free"), 1)
            with pe.Fori(0, B // 2) as i:
                for k in range(STEPS):
                    g = i * STEPS + k
                    b = k // PAIRS
                    if k % PAIRS == 0:
                        pe.wait_ge(sem("xl_done"), i * 2 + b + 1)
                        pe.wait_ge(sem("xh_done"), i * 2 + b + 1)
                    pe.wait_ge(sem("vo_done"), g + 1)
                    project_u(g, k)
                    transposes(g, k)
                    weighted_sums(g, k, i)
                    pe.wait_ge(sem("u_lo"), g + 1)
                    t, q4 = k % 2, k % 8 // 2
                    mm3(UB, (xh[b][:, t * 128:t * 128 + 128], xl[b][:, t * 128:t * 128 + 128]),
                        (NVh[:, q4 * CH:q4 * CH + CH], NVl[:, q4 * CH:q4 * CH + CH])).then_inc(sem("vo_ready"), 1)
                    par = k % 2
                    mm3(bank(2 * par, 256), (xh[b][:, 0:128], xl[b][:, 0:128]),
                        (Uh[:, :].rearrange("p (h c) -> p h c", h=2)[:, :, 0:128],
                         Ul[:, :].rearrange("p (h c) -> p h c", h=2)[:, :, 0:128]))
                    mm3(bank(2 * par + 1), (xh[b][:, 128:256], xl[b][:, 128:256]),
                        (Uh[:, :], Ul[:, :])).then_inc(sem("s_ready"), 1)
            for k in range(3):
                if k < 2:
                    transposes(B * PAIRS + k, k)
                weighted_sums(B * PAIRS + k, k)
            ln_tensor(pe, 0)

            pe.wait_ge(sem("ctx_dve"), CTX_DVE["wq_lo"])
            for c in range(NC_):
                cc = slice(c * CH, c * CH + CH)
                pe.wait_ge(sem("ln_lo"), c + 1)
                mm3(bank(c), (wqh[:, :], wql[:, :]), (XTh[:, cc], XTl[:, cc])).then_inc(sem("q_ready"), 1)
            for c in range(NC_):
                pe.wait_ge(sem("q_sq"), c + 1)
                pe.matmul(bank(4 + c), blockones[:, :], SQ[:, c * CH:c * CH + CH], start=True, stop=True).then_inc(sem("q_norm"), 1)
            for c in range(NC_):
                pe.wait_ge(sem("q_done"), c + 1)
                for t in range(4 * c, 4 * c + 4):
                    dst = bank(c)[:, t % 4 * 128:t % 4 * 128 + 128]
                    pe.matmul(dst, Q[:, t * 128:t * 128 + 128], G2[:, t // 2, :], start=True, stop=False)
                    last = pe.matmul(dst, ones[0:1, :], brow[0:1, 256:384], start=False, stop=True)
                last.then_inc(sem("b_out"), 1)
            pe.wait_ge(sem("x_added"), NC_)
            ln_tensor(pe, 1, XS, "xs_done")
            pe.wait_ge(sem("ctx_dve"), CTX_DVE["wr_split"])
            for c in range(NC_):
                cc = slice(c * CH, c * CH + CH)
                pe.wait_ge(sem("ln_lo"), NC_ + c + 1)
                mm3(bank(4 + c), (wrh[:, :], wrl[:, :]), (XTh[:, cc], XTl[:, cc])).then_inc(sem("router_T"), 1)
            for t in range(T):
                pe.wait_ge(sem("router_out"), t // 4 + 1)
                last = pe.transpose(bank(0)[:, t * 16:t * 16 + 16], LT[:, t * 128:t * 128 + 128], ident[0:16, 0:16])
            last.then_inc(sem("logits_T"), 1)
            pe.wait_ge(sem("gates_split"), 1)
            for t in range(T):
                last = pe.transpose(bank(4 + t // 4)[:, t % 4 * 128:t % 4 * 128 + 128], GI[:, t, :].bitcast(F32), ident[:, :])
                if t % 4 == 3:
                    last.then_inc(sem("gates_T"), 1)
            def residual(done):
                for t in range(T):
                    pe.matmul(bank(t // 4)[:, t % 4 * 128:t % 4 * 128 + 128], X[:, t, :], ident[:, :],
                              start=t % 4 == 0, stop=True, skip_group_check=True)
            residual(None)
            pe.wait_ge(sem("gates_out"), NC_)

            def down(U, k):
                s, c, n = (k - 3) // 8 % 2, (k - 3) // 2 % 4, (k - 3) % 2
                w = slice(HID + n * 128, HID + n * 128 + 128)
                pe.wait_ge(sem("hl_done"), U + 1)
                return mm3(bank(c), (W0h[s][:, w], W0l[s][:, w]), (HH[:, (k - 3) % 4, :], HL[:, (k - 3) % 4, :]),
                           start=False, skip=True).then_inc(sem("down_done"), 1)

            pe.wait_ge(sem("w2_zero"), 2)
            pe.wait_ge(sem("sel2_done"), 1)
            with pe.Fori(0, E0 // 2) as i:
                for k in range(16):
                    s, c, n = k // 8, k // 2 % 4, k % 2
                    cc = slice(c * CH, c * CH + CH)
                    U = i * 16 + k
                    if k % 8 == 0:
                        pe.wait_ge(sem("w_sel"), i * 2 + s + 1)
                        pe.wait_ge(sem("w_split"), i * 2 + s + 3)
                    pe.wait_ge(sem("sg_done"), U + 1)
                    w = slice(n * 128, n * 128 + 128)
                    mm3(bank(6 + n), (W0h[s][:, w], W0l[s][:, w]), (XTh[:, cc], XTl[:, cc])).then_inc(sem("up_ready"), 1)
                    down(U, k)
                    if n == 0:
                        pe.matmul(bank(4 + c % 2), esel[s][:, :], SELT[:, cc], start=True, stop=True).then_inc(sem("gb_ready"), 1)
            for k in range(3):
                down(E0 * 8 + k, k)
            for t in range(T):
                pe.wait_ge(sem("experts_out"), t // 4 + 1)
                last = pe.transpose(bank(4 + t // 4)[:, t % 4 * 128:t % 4 * 128 + 128], OT[:, t * 128:t * 128 + 128], ident[:, :])
                if t % 4 == 3:
                    last.then_inc(sem("experts_T"), 1)
            ln_tensor(pe, 2)
            pe.wait_ge(sem("l1_split"), 5)
            for t in range(T):
                p, tok = t % 2, slice(t * 128, t * 128 + 128)
                pe.wait_ge(sem("ln_lo"), 2 * NC_ + max(t // 4 + 1, 3 + p if t < 2 else 0))
                for n, (b0, what, free) in enumerate(((4, "dq_ready", "qs_done"), (2, "dk_ready", "pr_done"),
                                                      (6, "dz_ready", "z_pos"))):
                    if t >= 2:
                        pe.wait_ge(sem(free), t - 1)
                    w = slice(n * CH, n * CH + CH)
                    if n == 2:
                        pe.matmul(bank(b0 + p), onesr[:, :], abr[:, :], start=True, stop=False)
                    mm3(bank(b0 + p), (XTh[:, tok], XTl[:, tok]), (wdh[:, w], wdl[:, w]), start=n < 2).then_inc(sem(what), 1)
                if t % 4 == 3:
                    c = t // 4
                    cc = slice(c * CH, c * CH + CH)
                    w = slice(3 * CH, 3 * CH + 128)
                    if c >= 2:
                        pe.wait_ge(sem("vp_done"), 2 * c - 2)
                    mm3(bank(c % 2), (wdh[:, w], wdl[:, w]), (XTh[:, cc], XTl[:, cc])).then_inc(sem("dv_ready"), 1)
            pe.wait_ge(sem("pr_done"), T)
            for n in (1, 0):
                pe.wait_ge(sem("ab_placed"), 4 - 2 * n)
                for r in range(2):
                    last = pe.transpose(bank(2)[0:64, n * S + r * 128:n * S + r * 128 + 128],
                                        ABt[:, r, n, :, :].rearrange("p h b -> p (h b)"), ident[:, :])
            last.then_inc(sem("ab_T"), 1)

            def product(g, col, src, w, done, first=False):
                for t in range(2):
                    dst = PS[:, ds(g * S + col + t * 128, 128)] if not isinstance(g, int) else PS[:, g * S + col + t * 128:g * S + col + t * 128 + 128]
                    for h in range(H1):
                        last = pe.matmul(dst, src[:, h * S + t * 128:h * S + t * 128 + 128], w[:, :],
                                         start=first and t == 0 and h == 0, stop=h == H1 - 1, skip_group_check=True)
                last.then_inc(sem(done), 1)

            def states_product(g, par):
                pe.wait_ge(sem("scan1_done"), g + 1)
                product(g, 3 * CH + S, r0b[1 - par], wo1, "y0_done", first=par == 1)

            def floors_product(g, par):
                pe.wait_ge(sem("scan2_done"), g + 1)
                product(g, 3 * CH, rb[par], wo1e, "y1_done")

            pe.wait_ge(sem("wu_done"), 1)
            pe.wait_ge(sem("vp_done"), 2 * NC_)
            pe.wait_ge(sem("ab_in"), 1)
            with pe.Fori(0, B // 2) as i:
                for k in range(2):
                    g = i * 2 + k
                    pe.wait_ge(sem("dsel_done"), g + 1)
                    for r in range(4):
                        pe.wait_ge(sem("w_copied"), g * 4 + r + 1)
                        for h in range(2):
                            last = pe.matmul(bank(r % 2)[:, h * S:h * S + S], dsel[k][:, 2 * r + h, :], WUr[:, 0, :], start=True, stop=True)
                        last.then_inc(sem("w_bc"), 1)
                        pe.wait_ge(sem("qr_done"), g * 4 + r + 1)
                        for h in range(2):
                            last = pe.matmul(bank(2)[:, h * S:h * S + S], dsel[k][:, 2 * r + h, :], WUr[:, 1, :], start=True, stop=True)
                        last.then_inc(sem("u_bc"), 1)
                    states_product(g, k)
                    floors_product(g, k)
            states_product(B, 0)
            floors_product(B, 0)
            floors_product(B + 1, 1)
            ln_tensor(pe, 3)
            for t in range(T):
                pe.wait_ge(sem("ln_hi"), 3 * NC_ + t // 4 + 1)
                b = t // 2
                last = pe.matmul(bank(4 + t // 8)[:, t % 8 * SC:t % 8 * SC + SC], XTf[:, t * 128:t * 128 + 128], KK[:, b * SC:b * SC + SC],
                                 start=True, stop=True)
            last.then_inc(sem("es_ready"), 1)
            pe.wait_ge(sem("e_prob"), 1)
            for t in range(T):
                last = pe.transpose(bank(t // 4)[0:64, t % 4 * 128:t % 4 * 128 + 128], SE[:, t, :], ident[:, :])
                if t % 4 == 3:
                    last.then_inc(sem("e_T"), 1)
            for t in range(T):
                pe.wait_ge(sem("e_pt"), t // 4 + 1)
                last = pe.matmul(bank(4 + t // 4)[:, t % 4 * 128:t % 4 * 128 + 128], PE_T[:, t * 128:t * 128 + 128], vE[:, t // 2, :],
                                 start=True, stop=True)
                if t % 4 == 3:
                    last.then_inc(sem("e_out"), 1)
            ln_tensor(pe, 4)
            for c in range(NC_):
                cc = slice(c * CH, c * CH + CH)
                pe.wait_ge(sem("ln_lo"), 3 * NC_ + c + 1)
                mm3(bank(4 + c), (wr1h[:, :], wr1l[:, :]), (XTh[:, cc], XTl[:, cc])).then_inc(sem("router_T"), 1)
            for t in range(T):
                pe.wait_ge(sem("router_out"), NC_ + NC_)
                last = pe.transpose(bank(4 + t // 8)[:, t % 8 * E1:t % 8 * E1 + E1], FL[:, t * 128:t * 128 + 128], ident[0:64, 0:64])
            last.then_inc(sem("logits_T"), 1)
            residual(None)
            def shared_down(c):
                pe.wait_ge(sem("sh_hl"), c + 1)
                mm3(bank(c), (wshh[:, 256:384], wshl[:, 256:384]), (FHH[:, c % 2, :], FHL[:, c % 2, :]),
                    start=False, skip=True).then_inc(sem("sh_down"), 1)

            for c in range(NC_):
                cc = slice(c * CH, c * CH + CH)
                if c:
                    pe.wait_ge(sem("sh_sg"), c)
                mm3(bank(6), (wshh[:, 0:128], wshl[:, 0:128]), (XTh[:, cc], XTl[:, cc])).then_inc(sem("sh_g"), 1)
                if c:
                    pe.wait_ge(sem("sh_h"), c)
                mm3(bank(7), (wshh[:, 128:256], wshl[:, 128:256]), (XTh[:, cc], XTl[:, cc])).then_inc(sem("sh_u"), 1)
                if c:
                    shared_down(c - 1)
            shared_down(NC_ - 1)
            pe.wait_ge(sem("sh_h"), NC_)
            pe.wait_ge(sem("gates_split"), 1 + 1)
            for t in range(T):
                last = pe.transpose(bank(4 + t // 4)[:, t % 4 * 128:t % 4 * 128 + 128], GI1[:, t, :].bitcast(F32), ident[:, :])
                if t % 4 == 3:
                    last.then_inc(sem("gates_T"), 1)
            pe.wait_ge(sem("gates_out"), NC_ + NC_)

            def f_down(U, k):
                s, c = (k - 2) // 4 % 2, (k - 2) % 4
                pe.wait_ge(sem("fhl_done"), U + 1)
                mm3(bank(c), (W3h[s][:, 256:384], W3l[s][:, 256:384]), (FHH[:, (k - 2) % 4, :], FHL[:, (k - 2) % 4, :]),
                    start=False, skip=True).then_inc(sem("fdown_done"), 1)

            with pe.Fori(0, E1 // 4) as i:
                for k in range(8):
                    s, c = k // 4, k % 4
                    cc = slice(c * CH, c * CH + CH)
                    U = i * 8 + k
                    if c == 0:
                        pe.wait_ge(sem("f_sel"), i * 2 + s + 1)
                        pe.wait_ge(sem("f_split"), i * 2 + s + 3)
                    pe.wait_ge(sem("fg_done"), U + 1)
                    mm3(bank(4 + k % 2), (W3h[s][:, 0:128], W3l[s][:, 0:128]), (XTh[:, cc], XTl[:, cc])).then_inc(sem("g_ready"), 1)
                    pe.wait_ge(sem("ft_done"), U + 2)
                    mm3(bank(6), (W3h[s][:, 128:256], W3l[s][:, 128:256]), (XTh[:, cc], XTl[:, cc])).then_inc(sem("fu_ready"), 1)
                    f_down(U, k)
                    pe.wait_ge(sem("fh_done"), U + 1)
                    pe.matmul(bank(7), fsel[s][:, :, :].rearrange("p e i -> p (e i)"), SELT1[:, cc], start=True, stop=True).then_inc(sem("fgb_ready"), 1)
            for k in range(2):
                f_down(E1 * 2 + k, k)
            for t in range(T):
                pe.wait_ge(sem("experts_out"), NC_ + t // 4 + 1)
                last = pe.transpose(bank(4 + t // 4)[:, t % 4 * 128:t % 4 * 128 + 128], OT1[:, t * 128:t * 128 + 128], ident[:, :])
                if t % 4 == 3:
                    last.then_inc(sem("experts_T"), 1)


def host_layout(v):
    f = np.ascontiguousarray
    x, c = v["x"].reshape(N, D), v["ctx_1024"].reshape(B * SC, D)
    tiles = lambda m: m.reshape(-1, 128, m.shape[-1]).transpose(1, 0, 2)
    lay = lambda *m: np.stack(m, axis=1)
    both = lambda n: np.concatenate([v["L0_ffn_" + n], v["L0_ffn_" + n + "_s"]])
    return {k: f(m) for k, m in {
        "x": tiles(x), "xT": x.T, "ctxT": c.T,
        "w64q": v["L0_attn_W_Q"].transpose(1, 0, 2), "w64k": v["L0_attn_W_K"].transpose(1, 0, 2),
        "w64v": v["L0_attn_W_V"].transpose(1, 0, 2), "w64o": v["L0_attn_W_O"].transpose(2, 0, 1),
        "wx": lay(*(v["L0_xattn_W" + n].T for n in "kvoq")),
        "brow": np.concatenate([v["L0_xattn_b" + n] for n in "kvo"])[None],
        "bq": v["L0_xattn_bq"][:, None],
        "wr0": v["L0_ffn_router_w"], "rw": both("rms_w").T,
        "w12": np.concatenate([both("w1"), both("w2").reshape(E0, 2, 128, D).transpose(0, 2, 1, 3).reshape(E0, 128, HID)], axis=2),
        "wd": np.concatenate([v["L1_attn_W_" + n].T for n in ("q", "k", "alpha_w", "v")], axis=1),
        "abias": v["L1_attn_W_alpha_b"][None], "wo1": v["L1_attn_W_o"].T,
        "wqe": lay(v["L1_xattn_Wq"].T, v["L1_xattn_Wq"]),
        "wr1": v["L1_ffn_router_w"].T, "ebias": np.broadcast_to(v["L1_ffn_e_bias"][None], (128, E1)),
        "wsh": np.concatenate([v["L1_ffn_S" + n] for n in ("Wg", "Wu", "Wd")], axis=1),
        "w3": np.concatenate([v["L1_ffn_" + n].reshape(E1 // 2, 2, D, I1).transpose(0, 2, 1, 3).reshape(E1 // 2, D, 128)
                              for n in ("Wg", "Wu")] + [v["L1_ffn_Wd"].reshape(E1 // 2, 128, D)], axis=2),
    }.items()}


def kernel(**inputs):
    import concourse.bacc as bacc
    from concourse.bass_utils import run_bass_kernel_spmd

    nc = bacc.Bacc("TRN2", target_bir_lowering=False, num_devices=1)
    arrays = host_layout({k: np.asarray(v) for k, v in inputs.items()})
    drams = {k: nc.dram_tensor("in_" + k, m.shape, mybir.dt.from_np(m.dtype), kind="ExternalInput").ap()
             for k, m in arrays.items()}
    out = nc.dram_tensor("out", (128, T, D), F32, kind="ExternalOutput").ap()
    decoder_program(nc, drams, out)
    got = run_bass_kernel_spmd(nc, [{"in_" + k: m for k, m in arrays.items()}], core_ids=[0])
    return got.results[0]["out"].transpose(1, 0, 2).reshape(B, S, D)
```

```python
import math
from contextlib import ExitStack

import numpy as np
import concourse.bass as bass
from concourse import mybir
from concourse.alu_op_type import AluOpType as ALU

ACT = mybir.ActivationFunctionType
AX = mybir.AxisListType
F32 = mybir.dt.float32
F32R = mybir.dt.float32r
ds = bass.ds

B, S, D = 8, 256, 128
N = B * S
T = N // 128
SC = 64
CH = 512
NC_ = N // CH
H0, DH = 16, 64
PAIRS = H0 // 2
HX, DX = 16, 8
E0, E0R, HID = 16, 14, 256
H1 = 8
E1, I1, K1 = 64, 64, 8
LN_EPS, RMS_EPS, EPS = 1e-5, 1.1920929e-07, 1e-8
BIG = 1e30


def decoder_program(nc, a, out):
    CTX_PE = {"ck_ready": 1, "cv_ready": 2, "kn_ready": 3, "gt_ready": 4, "g2_ready": 5, "ke_ready": 6, "ve_ready": 7, "kk_ready": 8}
    CTX_ACT = {"ck_exp": 1, "cv_done": 2, "wq_hi": 3, "g2_done": 11, "ke_done": 12, "ve_done": 13, "kk_done": 14}
    CTX_DVE = {"ck_neg": 1, "ck_done": 2, "kn_sum": 3, "gbt_done": 4, "wq_lo": 5, "wr_split": 7}
    CTX_POOL = {"ck_sq": 1, "kn_done": 2}
    ctx = ExitStack()
    sems = {}

    def sem(name):
        if name not in sems:
            sems[name] = ctx.enter_context(nc.semaphore(name))
        return sems[name]

    def sb(name, shape, dt=F32, scope=ctx):
        return scope.enter_context(nc.sbuf_tensor(name, shape, dt))

    with ctx:
        PS = ctx.enter_context(nc.psum_tensor("PS", [128, 8 * CH], F32))

        def bank(n, w=CH, k=1):
            return PS[:, n * CH:n * CH + (k - 1) * CH + w]

        Xp = sb("Xp", [128, (B + 1) * S])
        X = Xp[:, S:].rearrange("p (t d) -> p t d", d=D)
        XTh = sb("XTh", [128, N], F32R)
        XTl = sb("XTl", [128, N], F32R)
        ident = sb("ident", [128, 128])
        blockones = sb("blockones", [128, 128])
        sel2 = sb("sel2", [128, 72], F32R)
        cmask = sb("cmask", [128, 2 * 128])
        ones = sb("ones", [128, 128])
        scratch = sb("scratch", [128, 16])
        st = sb("st", [128, T, 6])
        mv = sb("mv", [128, T, 2])
        rs = sb("rs", [128, T])
        nm = sb("nm", [128, T])
        nb = sb("nb", [128, T])
        rs2 = sb("rs2", [128, T])
        ms = sb("ms", [128, T])
        neghalf = sb("neghalf", [128, T])
        ctxT = sb("ctxT", [128, B * SC])

        halfones = sb("halfones", [128, 2])
        wx = sb("wx", [128, 4, 128])
        bq = sb("bq", [128, 1])
        brow = sb("brow", [1, 3 * 128])
        G2 = sb("G2", [128, B, 128])
        wqh = sb("wqh", [128, 128], F32R)
        wql = sb("wql", [128, 128], F32R)
        wrh = sb("wrh", [128, 128], F32R)
        wrl = sb("wrl", [128, 128], F32R)
        wr_in = sb("wr_in", [128, E0R])

        wd_in = sb("wd_in", [128, 3 * CH + 128])
        wdh = sb("wdh", [128, 3 * CH + 128], F32R)
        wdl = sb("wdl", [128, 3 * CH + 128], F32R)
        abias = sb("abias", [1, CH])
        abr = sb("abr", [33, CH], F32R)
        onesr = sb("onesr", [33, 128], F32R)
        wo1 = sb("wo1", [128, 128])
        wqe = sb("wqe", [128, 2, 128])
        KK = sb("KK", [128, B * SC])
        vE = sb("vE", [64, B, 128])
        wr1_in = sb("wr1_in", [128, E1])
        wr1h = sb("wr1h", [128, 128], F32R)
        wr1l = sb("wr1l", [128, 128], F32R)
        ebias = sb("ebias", [128, E1])
        wsh = sb("wsh", [128, 384])
        wshh = sb("wshh", [128, 384], F32R)
        wshl = sb("wshl", [128, 384], F32R)
        tiny = sb("tiny", [128, 1])
        zero = sb("zero", [128, 1])
        wo1e = sb("wo1e", [128, 128])

        sa = ExitStack()
        Mh = sb("Mh", [128, H0 * 128], F32R, sa)
        Ml = sb("Ml", [128, H0 * 128], F32R, sa)
        NVh = sb("NVh", [128, H0 * 128], F32R, sa)
        NVl = sb("NVl", [128, H0 * 128], F32R, sa)
        xall = sb("xall", [128, (B + 1) * S], F32, sa)
        xh = [sb(f"xh{k}", [128, S], F32R, sa) for k in range(2)]
        xl = [sb(f"xl{k}", [128, S], F32R, sa) for k in range(2)]
        VO = sb("VO", [128, 2, H0, 128], F32, sa)
        P = sb("P", [128, 4, 768], F32, sa)
        PT = sb("PT", [128, 2, 2, 384], F32, sa)
        Uh = sb("Uh", [128, CH], F32R, sa)
        Ul = sb("Ul", [128, CH], F32R, sa)
        mn = sb("mn", [128, 2, 4], F32, sa)
        ls = sb("ls", [128, 2, 4], F32, sa)
        rl = sb("rl", [128, 2, 4], F32, sa)
        wraw = ExitStack()
        w64 = {n: sb("w64" + n, [64, H0, 128], F32, wraw) for n in "qkvo"}
        cx = ExitStack()
        ce = sb("ce", [128, 4, 128], F32, cx)
        ck = sb("ck", [128, 4, 128], F32, cx)
        cv = sb("cv", [128, 4, 128], F32, cx)
        csq = sb("csq", [128, 4, 128], F32, cx)
        GBT = sb("GBT", [128, B, 128], F32, cx)
        kn = sb("kn", [128, B], F32, cx)
        cx.close()
        wraw.close()
        sa.close()

        sbs = ExitStack()
        EQ = sb("EQ", [128, N], F32, sbs)
        RQ = sb("RQ", [128, N], F32, sbs)
        Q = sb("Q", [128, N], F32, sbs)
        SQ = sb("SQ", [128, N], F32, sbs)
        sbs.close()

        sc = ExitStack()
        XS = sb("XS", [128, T, 128], F32, sc)
        LT = sb("LT", [16, N], F32, sc)
        Lg = sb("Lg", [128, T, E0R], F32, sc)
        lm = sb("lm", [128, T], F32, sc)
        lz = sb("lz", [128, T], F32, sc)
        G20 = sb("G20", [128, T, 20], F32, sc)
        M8 = sb("M8", [128, T, 8], F32, sc)
        RPL = sb("RPL", [128, T, 8], F32, sc)
        RP = sb("RP", [128, T, 20], F32, sc)
        GI = sb("GI", [128, T, 128], F32R, sc)
        SELT = sb("SELT", [128, N], F32R, sc)
        rw = sb("rw", [128, E0], F32, sc)
        W0 = [sb(f"W0_{k}", [128, 2 * HID], F32, sc) for k in range(2)]
        W0h = [sb(f"W0h{k}", [128, 2 * HID], F32R, sc) for k in range(2)]
        W0l = [sb(f"W0l{k}", [128, 2 * HID], F32R, sc) for k in range(2)]
        esel = [sb(f"esel{k}", [128, 128], F32R, sc) for k in range(2)]
        SG = sb("SG", [128, 2, CH], F32, sc)
        Hf = sb("Hf", [128, 4, CH], F32, sc)
        HH = sb("HH", [128, 4, CH], F32R, sc)
        HL = sb("HL", [128, 4, CH], F32R, sc)
        OT = sb("OT", [128, N], F32, sc)
        sc.close()

        sd = ExitStack()
        VP = sb("VP", [128, N], F32, sd)
        AB64 = sb("AB64", [64, 2, S], F32, sd)
        mb = sb("mb", [64, S + 1], F32, sd)
        db = sb("db", [64, S + 1], F32, sd)
        ea = sb("ea", [64, S], F32, sd)
        eb = sb("eb", [64, S], F32, sd)
        rd = sb("rd", [64, S], F32, sd)
        wu = sb("wu", [64, 2, S], F32, sd)
        WUr = sb("WUr", [128, 2, S], F32R, sd)
        dsel = [sb(f"dsel{k}", [128, H1, 128], F32R, sd) for k in range(2)]
        sd1 = ExitStack()
        QS = sb("QS", [128, 2, CH], F32, sd1)
        PR = sb("PR", [128, 2, CH], F32, sd1)
        ZA = sb("ZA", [128, T, CH], F32, sd1)
        ZR = sb("ZR", [128, T, CH], F32, sd1)
        ABs = sb("ABs", [128, 2, T, H1], F32, sd1)
        ABt = sb("ABt", [128, 2, 2, H1, B], F32, sd1)
        VS = sb("VS", [128, N], F32, sd1)
        sd1.close()
        kTe = sb("kTe", [128, B * SC], F32, sd)
        R = H1 * S
        Wb = [sb(f"Wb{k}", [128, R], F32, sd) for k in range(2)]
        qb = sb("qb", [128, R], F32, sd)
        r0b = [sb(f"r0b{k}", [128, R], F32, sd) for k in range(2)]
        dfb = [sb(f"dfb{k}", [128, R], F32, sd) for k in range(2)]
        sgb = sb("sgb", [128, R], F32, sd)
        gb = [sb(f"gb{k}", [128, R], F32, sd) for k in range(2)]
        rb = [sb(f"rb{k}", [128, R], F32, sd) for k in range(2)]
        sd.close()

        se = ExitStack()
        XTf = sb("XTf", [128, N], F32, se)
        SE = sb("SE", [128, T, SC], F32, se)
        PE_T = sb("PE_T", [64, N], F32, se)
        em = sb("em", [128, T], F32, se)
        el = sb("el", [128, T], F32, se)
        se.close()

        sf = ExitStack()
        FL = sb("FL", [64, N], F32, sf)
        SCo = sb("SCo", [128, T, E1], F32, sf)
        SF = sb("SF", [128, T, E1], F32, sf)
        h1 = sb("h1", [128, T * 8, 4], F32, sf)
        l1 = sb("l1", [128, T * 8, 4], F32, sf)
        h2 = sb("h2", [128, T * 8, 2], F32, sf)
        l2 = sb("l2", [128, T * 8, 2], F32, sf)
        t2 = sb("t2", [128, T * 8, 2], F32, sf)
        h3 = sb("h3", [128, T * 8, 1], F32, sf)
        l3 = sb("l3", [128, T * 8, 1], F32, sf)
        t3 = sb("t3", [128, T * 8, 1], F32, sf)
        GS = sb("GS", [128, T, 12], F32, sf)
        F8 = sb("F8", [128, T, 8], F32, sf)
        FR = sb("FR", [128, T, 8], F32, sf)
        GR = sb("GR", [128, T, 12], F32, sf)
        gm = sb("gm", [128, T, 8], F32, sf)
        FM = sb("FM", [128, T, E1], F32, sf)
        FRP = sb("FRP", [128, T, E1], F32, sf)
        fs = sb("fs", [128, T], F32, sf)
        fi = sb("fi", [128, T], F32, sf)
        GI1 = sb("GI1", [128, T, 128], F32R, sf)
        SELT1 = sb("SELT1", [128, N], F32R, sf)
        W3 = [sb(f"W3_{k}", [128, 384], F32, sf) for k in range(2)]
        W3h = [sb(f"W3h{k}", [128, 384], F32R, sf) for k in range(2)]
        W3l = [sb(f"W3l{k}", [128, 384], F32R, sf) for k in range(2)]
        fsel = [sb(f"fsel{k}", [128, 2, 64], F32R, sf) for k in range(2)]
        FG = sb("FG", [128, 2, CH], F32, sf)
        FU = sb("FU", [128, 2, CH], F32, sf)
        FH = sb("FH", [128, 4, CH], F32, sf)
        FHH = sb("FHH", [128, 4, CH], F32R, sf)
        FHL = sb("FHL", [128, 4, CH], F32R, sf)
        OT1 = sb("OT1", [128, N], F32, sf)
        sf.close()
        NEG = -3e38
        F_STEPS, F_RECIP, F_GROUPS = 40, 2, 23
        SP_GROUPS = ((0, 6), (6, 12), (12, 16))

        block = ctx.enter_context(nc.Block())

        def piece(q):
            r, h = q // 2, q % 2
            return (h * 128, 128) if r == 0 else (256 + h * 256, 256)

        def scores(par, q):
            r, h = q // 2, q % 2
            c = (2 * par + r) * CH + h * (128 if r == 0 else 256)
            return PS[:, c:c + (128 if r == 0 else 256)]

        PTP = bank(4, CH, 2).rearrange("p (a c) -> p a c", a=2)[:, :, 0:384]
        UB, OB = bank(6), bank(7)

        def fold_bank(n):
            return bank(4 + n % 4)

        def sum_bank(t):
            return bank(4 + t // 4)[:, t % 4 * 128:t % 4 * 128 + 128]
        STEPS = 2 * PAIRS

        def tiles(c):
            return range(4 * c, 4 * c + 4)

        def ln_stats(dve, n, c, src=None):
            for t in tiles(c):
                dve.bn_stats(st[:, t, :], src(t) if src else X[:, t, :]).then_inc(sem("ln_st"), 1)
            for t in tiles(c):
                dve.wait_ge(sem("ln_st"), T * n + t + 1)
                last = dve.bn_aggr(mv[:, t, :], st[:, t, :])
            last.then_inc(sem("ln_mv"), 1)

        def ln_factors(pool, n, c):
            cc, k = slice(4 * c, 4 * c + 4), NC_ * n + c + 1
            pool.wait_ge(sem("ln_mv"), k)
            pool.tensor_scalar(ms[:, cc], mv[:, cc, 1], LN_EPS, None, ALU.add).then_inc(sem("ln_ms"), 1)
            pool.tensor_scalar(nm[:, cc], mv[:, cc, 0], -1.0, None, ALU.mult).then_inc(sem("ln_ms"), 1)
            pool.wait_ge(sem("ln_ms"), 2 * k)
            pool.tensor_tensor(rs[:, cc], ms[:, cc], neghalf[:, cc], ALU.pow).then_inc(sem("ln_rs"), 1)
            pool.wait_ge(sem("ln_rs"), k)
            pool.tensor_tensor(nb[:, cc], nm[:, cc], rs[:, cc], ALU.mult).then_inc(sem("ln_nb"), 1)

        def ln_norm(act, n, c, src=None):
            act.wait_ge(sem("ln_nb"), NC_ * n + c + 1)
            for t in tiles(c):
                act.activation(X[:, t, :], src(t) if src else X[:, t, :], ACT.Identity, scale=rs[:, t:t + 1],
                               bias=nb[:, t:t + 1]).then_inc(sem("ln_x"), 1)

        def ln_transpose(pe, n, c, src=None, ready=None):
            for t in tiles(c):
                pe.wait_ge(sem(ready or "ln_x"), t + 1 if ready else T * n + t + 1)
                last = pe.transpose(bank(c)[:, t % 4 * 128:t % 4 * 128 + 128], (src or X)[:, t, :], ident[:, :])
            last.then_inc(sem("ln_T"), 1)

        def ln_hi(act, n, c):
            act.wait_ge(sem("ln_T"), NC_ * n + c + 1)
            act.activation(XTh[:, c * CH:c * CH + CH], bank(c), ACT.Copy).then_inc(sem("ln_hi"), 1)

        def ln_lo(dve, n, c):
            dve.wait_ge(sem("ln_hi"), NC_ * n + c + 1)
            dve.tensor_tensor(XTl[:, c * CH:c * CH + CH], bank(c), XTh[:, c * CH:c * CH + CH].bitcast(F32),
                              ALU.subtract).then_inc(sem("ln_lo"), 1)

        def in_turn(first, second, behind):
            for c in range(NC_ + behind):
                if c < NC_:
                    first(c)
                if c >= behind:
                    second(c - behind)

        @block.sync
        def _(sp):
            sp.dma_start(ctxT[:, :], a["ctxT"]).then_inc(sem("ctx_in"), 16)
            sp.dma_start(wx[:, :, :], a["wx"]).then_inc(sem("ctx_in"), 16)
            sp.dma_start(brow[:, :], a["brow"]).then_inc(sem("ctx_in"), 16)
            sp.dma_start(bq[:, :], a["bq"]).then_inc(sem("ctx_in"), 16)
            for n in "voqk":
                sp.dma_start(w64[n][:, :, :], a["w64" + n]).then_inc(sem("w_vo_in" if n in "vo" else "w_qk_in"), 16)
            sp.dma_start(xall[:, 0:N], a["xT"]).then_inc(sem("xT_in"), 16)
            sp.dma_start(X, a["x"]).then_inc(sem("x_in"), 16)
            sp.dma_start(wr_in[:, :], a["wr0"]).then_inc(sem("wr_in"), 16)
            for name, dst in (("wd", wd_in), ("abias", abias), ("wo1", wo1), ("wqe", wqe), ("wr1", wr1_in),
                              ("ebias", ebias), ("wsh", wsh)):
                sp.dma_start(dst[tuple([slice(None)] * len(dst.shape))], a[name]).then_inc(sem("l1_in"), 16)
            sp.wait_ge(sem("x_added"), NC_)
            sp.dma_start(rw[:, :], a["rw"]).then_inc(sem("rw_in"), 16)
            with sp.Fori(0, E0 // 2) as i:
                for s in range(2):
                    sp.wait_ge(sem("w_split"), i * 2 + s + 2)
                    sp.dma_start(W0[s][:, :], a["w12"][ds(i * 2 + s, 1), :, :].rearrange("o p n -> p (o n)")).then_inc(sem(f"w_in{s}"), 16)
            sp.wait_ge(sem("x_added"), 2 * NC_ + NC_)
            with sp.Fori(0, E1 // 4) as i:
                for s in range(2):
                    sp.wait_ge(sem("f_split"), i * 2 + s + 1)
                    sp.dma_start(W3[s][:, :], a["w3"][ds(i * 2 + s, 1), :, :].rearrange("o p n -> p (o n)")).then_inc(sem(f"w_in{s}"), 16)
            for c in range(NC_):
                sp.wait_ge(sem("ln_x"), 5 * T + 4 * c + 4)
                sp.dma_start(out[:, 4 * c:4 * c + 4, :], X[:, 4 * c:4 * c + 4, :]).then_inc(sem("out_done"), 16)
            sp.wait_ge(sem("out_done"), 16 * NC_)

        @block.gpsimd
        def _(pool):
            pool.memset(ident[:, :], 0.0).then_inc(sem("zeroed"), 1)
            pool.memset(blockones[:, :], 1.0).then_inc(sem("zeroed"), 1)
            pool.memset(cmask[:, :], 0.0).then_inc(sem("zeroed"), 1)
            pool.memset(ones[:, :], 1.0).then_inc(sem("consts"), 1)
            pool.memset(neghalf[:, :], -0.5).then_inc(sem("consts"), 1)
            pool.memset(wrh[:, :].bitcast(F32), 0.0).then_inc(sem("wr_zero"), 1)
            pool.memset(wrl[:, :].bitcast(F32), 0.0).then_inc(sem("wr_zero"), 1)
            pool.wait_ge(sem("zeroed"), 3)
            pool.affine_select(out=ident[:, :], in_=ident[:, :], compare_op=ALU.not_equal, fill=1.0,
                               base=0, pattern=[[-1, 128]], channel_multiplier=1).then_inc(sem("consts"), 1)
            pool.affine_select(out=cmask[:, 128:256], in_=cmask[:, 128:256], compare_op=ALU.is_ge, fill=BIG,
                               base=0, pattern=[[-1, 128]], channel_multiplier=1).then_inc(sem("consts"), 1)
            pool.affine_select(out=blockones[:, :], in_=blockones[:, :], compare_op=ALU.is_ge, fill=0.0,
                               base=0, pattern=[[-DX, HX], [0, DX]], channel_multiplier=1).then_inc(sem("zeroed"), 1)
            pool.wait_ge(sem("zeroed"), 4)
            pool.affine_select(out=blockones[:, :], in_=blockones[:, :], compare_op=ALU.is_ge, fill=0.0,
                               base=DX - 1, pattern=[[DX, HX], [0, DX]], channel_multiplier=-1).then_inc(sem("consts"), 1)
            pool.memset(xall[:, N:], 0.0).then_inc(sem("x_pad"), 1)
            pool.memset(P[:, 2, :], 0.0).then_inc(sem("norm_done"), 1)
            pool.memset(PT[:, 1, :, :], 0.0).then_inc(sem("pt_done"), 1)
            pool.memset(VO[:, :, :, :], 0.0).then_inc(sem("vo_done"), 1)

            pool.wait_ge(sem("ctx_dve"), CTX_DVE["ck_done"])
            pool.tensor_tensor(csq[:, :, :], ck[:, :, :], ck[:, :, :], ALU.mult).then_inc(sem("ctx_pool"), 1)
            pool.wait_ge(sem("ctx_dve"), CTX_DVE["kn_sum"])
            pool.tensor_tensor(kn[:, :], kn[:, :], neghalf[:, 0:B], ALU.pow).then_inc(sem("ctx_pool"), 1)

            def divide(g, k):
                slot, par = (k - 1) % 4, (k - 1) % 2
                pool.wait_ge(sem("rl_done"), g + 1)
                for r, w in ((0, 128), (1, 256)):
                    v = P[:, slot, 256 * r:256 * r + 2 * w].rearrange("p (h c) -> p h c", h=2)
                    f = rl[:, par, 2 * r:2 * r + 2].rearrange("p (h o) -> p h o", o=1).to_broadcast([128, 2, w])
                    last = pool.tensor_tensor(v, v, f, ALU.mult)
                last.then_inc(sem("norm_done"), 1)

            with pool.Fori(0, B // 2) as i:
                for k in range(STEPS):
                    divide(i * STEPS + k, k)
            divide(B * PAIRS, 0)
            for c in range(NC_):
                ln_factors(pool, 0, c)

            for c in range(NC_):
                cc = slice(c * CH, c * CH + CH)
                pool.wait_ge(sem("q_elu"), c + 1)
                pool.tensor_tensor(SQ[:, cc], Q[:, cc], Q[:, cc], ALU.mult).then_inc(sem("q_sq"), 1)
            for c in range(NC_):
                cc = slice(4 * c, 4 * c + 4)
                ln_factors(pool, 1, c)
                pool.tensor_tensor(ms[:, cc], mv[:, cc, 1], rs[:, cc], ALU.mult).then_inc(sem("rms"), 1)
                pool.wait_ge(sem("rms"), 4 * c + 1)
                pool.tensor_tensor(ms[:, cc], ms[:, cc], rs[:, cc], ALU.mult).then_inc(sem("rms"), 1)
                pool.wait_ge(sem("rms"), 4 * c + 2)
                pool.tensor_scalar(ms[:, cc], ms[:, cc], RMS_EPS, None, ALU.add).then_inc(sem("rms"), 1)
                pool.wait_ge(sem("rms"), 4 * c + 3)
                pool.tensor_tensor(rs2[:, cc], ms[:, cc], neghalf[:, cc], ALU.pow).then_inc(sem("rms"), 1)
            pool.memset(GI[:, :, :].bitcast(F32), 0.0).then_inc(sem("c_zeros"), 1)
            pool.memset(G20[:, :, :], -1.0).then_inc(sem("g20_init"), 1)
            pool.memset(RPL[:, :, :], -1.0).then_inc(sem("g20_init"), 1)
            pool.memset(Hf[:, 3, :], 0.0).then_inc(sem("h_done"), 2)
            pool.memset(HH[:, 1:3, :].bitcast(F32), 0.0).then_inc(sem("hl_done"), 1)
            pool.memset(HL[:, 1:3, :].bitcast(F32), 0.0).then_inc(sem("hl_done"), 1)
            pool.memset(W0h[1][:, :].bitcast(F32), 0.0).then_inc(sem("c_zeros"), 1)
            pool.memset(W0l[1][:, :].bitcast(F32), 0.0).then_inc(sem("c_zeros"), 1)
            pool.wait_ge(sem("c_zeros"), 3)
            pool.memset(GI[:, :, E0R:E0].bitcast(F32), 1.0).then_inc(sem("c_zeros"), 1)
            pool.memset(SG[:, 0, 0:1], 0.0).then_inc(sem("w_split"), 2)
            pool.memset(SG[:, 1, 0:1], 0.0).then_inc(sem("sg_done"), 2)
            pool.memset(esel[0][:, :].bitcast(F32), 0.0).then_inc(sem("down_done"), 16)
            pool.wait_ge(sem("rw_in"), 16)
            with pool.Fori(0, E0 // 2) as i:
                for s in range(2):
                    e = i * 2 + s
                    pool.wait_ge(sem(f"w_in{s}"), i * 16 + 16)
                    pool.tensor_tensor(W0[s][:, 0:HID], W0[s][:, 0:HID], rw[:, ds(e, 1)].to_broadcast([128, HID]),
                                       ALU.mult).then_inc(sem("w_scaled"), 1)
                    pool.wait_ge(sem("w_scaled"), e + 1)
                    pool.wait_ge(sem("down_done"), i * 16 + 11 + 8 * s)
                    pool.tensor_tensor(W0h[s][:, :], W0[s][:, :], ones[:, 0:1].to_broadcast([128, 2 * HID]),
                                       ALU.mult).then_inc(sem("w_rounded"), 1)
                    pool.tensor_copy(esel[s][:, :], sel2[:, ds(e, 1)].to_broadcast([128, 128]).bitcast(F32R)).then_inc(sem("w_sel"), 1)
                    pool.wait_ge(sem("w_rounded"), e + 1)
                    pool.tensor_tensor(W0l[s][:, :], W0[s][:, :], W0h[s][:, :].bitcast(F32), ALU.subtract).then_inc(sem("w_split"), 1)
            for c in range(NC_):
                ln_factors(pool, 2, c)
            for t in range(T):
                pool.wait_ge(sem("z_ln"), t + 1)
                pool.wait_ge(sem("z_pos"), t + 1)
                pool.tensor_tensor(ZR[:, t, :], ZR[:, t, :], ZA[:, t, :], ALU.add).then_inc(sem("z_sp"), 1)
            pool.memset(mb[:, 0:1], -BIG).then_inc(sem("d_init"), 1)
            pool.memset(db[:, 0:1], 0.0).then_inc(sem("d_init"), 1)
            pool.wait_ge(sem("ab_placed"), 4)
            pool.wait_ge(sem("ab_T"), 1)
            pool.wait_ge(sem("vp_done"), 2 * NC_)
            for k in range(2):
                pool.memset(gb[k][:, :], 0.0).then_inc(sem("floor_done"), 1)
            pool.memset(Wb[1][:, :], 0.0).then_inc(sem("w_copied"), 2)
            pool.memset(r0b[1][:, :], 0.0).then_inc(sem("signed_done"), 1)
            pool.memset(rb[0][:, :], 0.0).then_inc(sem("scan2_done"), 1)
            pool.wait_ge(sem("floor_done"), 2)

            def floor_terms(g, par):
                pool.wait_ge(sem("sgn_done"), g + 1)
                pool.wait_ge(sem("abs_done"), g + 1)
                pool.tensor_tensor(dfb[par][:, :], dfb[par][:, :], sgb[:, :], ALU.mult).then_inc(sem("signed_done"), 1)
                pool.wait_ge(sem("signed_done"), g + 2)
                pool.wait_ge(sem("scan2_done"), g + 1)
                later = lambda x: x[:, :].rearrange("p (h t) -> p h t", h=H1)[:, :, 1:]
                pool.tensor_tensor(later(gb[par]), later(dfb[par]), later(r0b[par]), ALU.add).then_inc(sem("floor_done"), 1)

            with pool.Fori(0, B // 2) as i:
                for k in range(2):
                    floor_terms(i * 2 + k, k)
            for c in range(NC_):
                ln_factors(pool, 3, c)
            for h in range(2):
                tt = slice(8 * h, 8 * h + 8)
                pool.wait_ge(sem("es_step"), 11 + h)
                pool.tensor_tensor(SE[:, tt, :], SE[:, tt, :], el[:, tt].rearrange("p (t o) -> p t o", o=1).to_broadcast([128, 8, SC]),
                                   ALU.mult).then_inc(sem("e_prob"), 1)
            for c in range(NC_):
                ln_factors(pool, 4, c)
            pool.wait_ge(sem("x_added"), 2 * NC_ + NC_)
            pool.memset(zero[:, :], 0.0).then_inc(sem("f_init"), 1)
            pool.memset(GS[:, :, :], NEG).then_inc(sem("f_init"), 1)
            pool.memset(FR[:, :, :], NEG).then_inc(sem("f_init"), 1)
            pool.memset(FH[:, 3, :], 0.0).then_inc(sem("fh_done"), 1)
            pool.memset(FHH[:, 2, :].bitcast(F32), 0.0).then_inc(sem("f_init"), 1)
            pool.memset(FHL[:, 2, :].bitcast(F32), 0.0).then_inc(sem("fhl_done"), 1)
            pool.memset(W3h[1][:, :].bitcast(F32), 0.0).then_inc(sem("f_init"), 1)
            pool.memset(W3l[1][:, :].bitcast(F32), 0.0).then_inc(sem("f_init"), 1)
            pool.memset(scratch[:, 1:2], 0.0).then_inc(sem("fg_done"), 2)
            pool.memset(scratch[:, 2:3], 0.0).then_inc(sem("ft_done"), 2)
            pool.memset(scratch[:, 3:4], 0.0).then_inc(sem("fdown_done"), 8)
            pool.memset(scratch[:, 4:5], 0.0).then_inc(sem("f_split"), 2)
            pool.wait_ge(sem("f_init"), 6)
            halves = (slice(0, 8), slice(8, 16))
            for h, tt in enumerate(halves):
                pool.wait_ge(sem("f_step"), F_RECIP * (h + 1))
                pool.tensor_tensor(SF[:, tt, :], SCo[:, tt, :], ebias[:, :].rearrange("p (o e) -> p o e", o=1)
                                   .to_broadcast([128, 8, E1]), ALU.add).then_inc(sem("f_pool"), 1)

            def shared_rest(c):
                pool.wait_ge(sem("sh_hh"), c + 1)
                if c >= 2:
                    pool.wait_ge(sem("sh_down"), c - 1)
                pool.tensor_tensor(FHL[:, c % 2, :], FH[:, c % 2, :], FHH[:, c % 2, :].bitcast(F32), ALU.subtract).then_inc(sem("sh_hl"), 1)

            shared_rest(0)
            shared_rest(1)
            for h, tt in enumerate(halves):
                pool.wait_ge(sem("f_step"), F_GROUPS + h)
                g8 = lambda x: x[:, tt, :].rearrange("p t (g e) -> p (t g) e", e=8)
                pool.tensor_tensor(g8(FM), g8(SF), gm[:, tt, :].rearrange("p t (g o) -> p (t g) o", o=1)
                                   .to_broadcast([128, 64, 8]), ALU.mult).then_inc(sem("f_mask"), 1)
                pool.wait_ge(sem("f_mask"), h + 1)
                pool.tensor_tensor(FM[:, tt, :], FM[:, tt, :], zero[:, 0:1].rearrange("p (t o) -> p t o", o=1)
                                   .to_broadcast([128, 8, E1]), ALU.add).then_inc(sem("f_pool"), 1)
            shared_rest(2)
            shared_rest(3)
            for h, tt in enumerate(halves):
                pool.wait_ge(sem("f_hi"), h + 1)
                pool.tensor_tensor(GI1[:, tt, 64:128], FM[:, tt, :], GI1[:, tt, 0:64].bitcast(F32), ALU.subtract).then_inc(sem("gates_split"), 1)

            with pool.Fori(0, E1 // 4) as i:
                for s in range(2):
                    j = i * 2 + s
                    pool.wait_ge(sem(f"w_in{s}"), E0 // 2 * 16 + i * 16 + 16)
                    pool.wait_ge(sem("fdown_done"), i * 8 + 6 + 4 * s)
                    pool.tensor_tensor(W3h[s][:, :], W3[s][:, :], ones[:, 0:1].to_broadcast([128, 384]), ALU.mult).then_inc(sem("f_rounded"), 1)
                    pool.tensor_copy(fsel[s][:, :, :], sel2[:, ds(j * 2, 2)].rearrange("p (e o) -> p e o", o=1)
                                     .to_broadcast([128, 2, 64])).then_inc(sem("f_sel"), 1)
                    pool.wait_ge(sem("f_rounded"), j + 1)
                    pool.tensor_tensor(W3l[s][:, :], W3[s][:, :], W3h[s][:, :].bitcast(F32), ALU.subtract).then_inc(sem("f_split"), 1)
            for c in range(NC_):
                ln_factors(pool, 5, c)

        @block.scalar
        def _(act):
            act.wait_ge(sem("ctx_pe"), CTX_PE["ck_ready"])
            act.activation(ce[:, :, :], bank(0).rearrange("p (a d) -> p a d", a=4), ACT.Exp).then_inc(sem("ctx_act"), 1)
            act.wait_ge(sem("ctx_pe"), CTX_PE["cv_ready"])
            act.activation(cv[:, :, :], bank(1).rearrange("p (a d) -> p a d", a=4), ACT.Copy).then_inc(sem("ctx_act"), 1)
            act.activation(wqh[:, :], wx[:, 3, :], ACT.Copy).then_inc(sem("ctx_act"), 1)
            for n in range(8):
                act.wait_ge(sem("fold"), n + 1)
                dst = (NVh if n < 4 else Mh)[:, n % 4 * CH:n % 4 * CH + CH]
                act.activation(dst, fold_bank(n), ACT.Copy, scale=1.0 if n < 4 else -1.0 / math.sqrt(DH)).then_inc(sem("fold_hi"), 1)

            def split_x(b, slot):
                act.activation(xh[slot][:, :], xall[:, ds(b * S, S)] if not isinstance(b, int) else xall[:, b * S:b * S + S],
                               ACT.Copy).then_inc(sem("xh_done"), 1)

            act.wait_ge(sem("xT_in"), 16)
            act.wait_ge(sem("x_pad"), 1)
            split_x(0, 0)
            act.wait_ge(sem("ctx_pool"), CTX_POOL["kn_done"])
            act.wait_ge(sem("ctx_pe"), CTX_PE["g2_ready"])
            for b in range(B):
                src = bank(2 + b % 2)[:, b // 2 * 128:b // 2 * 128 + 128]
                act.activation(G2[:, b, :], src, ACT.Copy, scale=kn[:, b:b + 1]).then_inc(sem("ctx_act"), 1)

            def exps(g, k):
                par, slot = (k - 1) % 2, (k - 1) % 4
                for q in range(4):
                    c, w = piece(q)
                    act.wait_ge(sem("masked"), g * 4 + q + 1)
                    last = act.activation(P[:, slot, c:c + w], P[:, slot, c:c + w], ACT.Exp, scale=-1.0,
                                          bias=mn[:, par, q:q + 1], accum_out=ls[:, par, q:q + 1])
                last.then_inc(sem("exp_done"), 1)

            with act.Fori(0, B // 2) as i:
                for k in range(STEPS):
                    g = i * STEPS + k
                    act.wait_ge(sem("u_ready"), g + 1)
                    act.activation(Uh[:, :], UB, ACT.Copy).then_inc(sem("u_hi"), 1)
                    exps(g, k)
                    act.wait_ge(sem("vo_ready"), g + 1)
                    t, q4 = k % 2, k % 8 // 2
                    act.activation(VO[:, t, 4 * q4:4 * q4 + 4, :], UB, ACT.Copy).then_inc(sem("vo_done"), 1)
                    if k in (4, 12):
                        split_x(i * 2 + (1 if k == 4 else 2), 1 if k == 4 else 0)
            exps(B * PAIRS, 0)

            in_turn(lambda c: ln_norm(act, 0, c), lambda c: ln_hi(act, 0, c), 1)

            for c in range(NC_):
                act.wait_ge(sem("q_ready"), c + 1)
                act.activation(EQ[:, c * CH:c * CH + CH], bank(4 + c), ACT.Exp, bias=bq[:, 0:1]).then_inc(sem("q_exp"), 1)

            for c in range(NC_):
                act.wait_ge(sem("q_norm"), c + 1)
                act.activation(RQ[:, c * CH:c * CH + CH], bank(c), ACT.Ln, scale=float(DX)).then_inc(sem("q_ln"), 1)
            for c in range(NC_):
                act.wait_ge(sem("q_ln"), c + 1)
                act.activation(RQ[:, c * CH:c * CH + CH], RQ[:, c * CH:c * CH + CH], ACT.Exp, scale=-0.5).then_inc(sem("q_inv"), 1)

            def norm_and_scale(c):
                ln_norm(act, 1, c)
                act.wait_ge(sem("rms"), 4 * c + 4)
                for t in tiles(c):
                    act.wait_ge(sem("ln_x"), T + t + 1)
                    act.activation(XS[:, t, :], X[:, t, :], ACT.Copy, scale=rs2[:, t:t + 1]).then_inc(sem("xs_done"), 1)

            in_turn(norm_and_scale, lambda c: ln_hi(act, 1, c), 1)
            for c in range(NC_):
                act.wait_ge(sem("router_T"), c + 1)
                act.activation(LT[:, c * CH:c * CH + CH], bank(4 + c)[0:16, :], ACT.Copy).then_inc(sem("router_out"), 1)
            act.wait_ge(sem("lg_sub"), 1)
            act.activation(Lg[:, :, :], Lg[:, :, :], ACT.Exp).then_inc(sem("lg_exp"), 1)
            for c in range(NC_):
                act.wait_ge(sem("gates_T"), c + 1)
                act.activation(SELT[:, c * CH:c * CH + CH], bank(4 + c), ACT.Copy).then_inc(sem("gates_out"), 1)

            def round_h(U, k):
                act.wait_ge(sem("h_done"), U + 2)
                act.activation(HH[:, (k - 1) % 4, :], Hf[:, (k - 1) % 4, :], ACT.Copy).then_inc(sem("hh_done"), 1)

            with act.Fori(0, E0 // 2) as i:
                for k in range(16):
                    U = i * 16 + k
                    act.wait_ge(sem("h_done"), U + 1)
                    act.wait_ge(sem("up_ready"), U + 1)
                    act.activation(SG[:, k % 2, :], bank(6 + k % 2), ACT.Silu).then_inc(sem("sg_done"), 1)
                    round_h(U, k)
            round_h(E0 * 8, 0)
            for c in range(NC_):
                act.wait_ge(sem("down_done"), E0 * 8 + 3 + 16)
                act.activation(OT[:, c * CH:c * CH + CH], bank(c), ACT.Copy).then_inc(sem("experts_out"), 1)
            in_turn(lambda c: ln_norm(act, 2, c, sum_bank), lambda c: ln_hi(act, 2, c), 1)
            for first, end in SP_GROUPS:
                for t in range(first, end):
                    act.wait_ge(sem("dq_ready"), t + 1)
                    if t >= 2:
                        act.wait_ge(sem("pr_done"), t - 1)
                    act.activation(QS[:, t % 2, :], bank(4 + t % 2), ACT.Copy).then_inc(sem("qs_done"), 1)
                    act.wait_ge(sem("dz_ready"), t + 1)
                    act.activation(ZA[:, t, :], bank(6 + t % 2), ACT.Abs).then_inc(sem("z_abs"), 1)
                    act.wait_ge(sem("z_abs"), t + 1)
                    act.activation(ZA[:, t, :], ZA[:, t, :], ACT.Exp, scale=-1.0).then_inc(sem("z_exp"), 1)
                for t in range(first, end):
                    act.wait_ge(sem("z_exp"), t + 1)
                    act.activation(ZA[:, t, :], ZA[:, t, :], ACT.Ln, bias=1.0).then_inc(sem("z_ln"), 1)
            act.wait_ge(sem("ctx_pe"), CTX_PE["ke_ready"])
            act.activation(kTe[:, :], bank(4), ACT.Copy).then_inc(sem("ctx_act"), 1)
            act.wait_ge(sem("ctx_pe"), CTX_PE["ve_ready"])
            act.activation(vE[:, :, :], bank(5, CH, 2)[0:64, :].rearrange("p (b d) -> p b d", b=B), ACT.Copy).then_inc(sem("ctx_act"), 1)
            act.wait_ge(sem("ctx_pe"), CTX_PE["kk_ready"])
            act.activation(KK[:, :], bank(7), ACT.Copy, scale=1.0 / math.sqrt(D)).then_inc(sem("ctx_act"), 1)

            act.wait_ge(sem("ea_arg"), 1)
            act.activation(ea[:, :], ea[:, :], ACT.Exp).then_inc(sem("e_ab"), 1)
            act.activation(eb[:, :], eb[:, :], ACT.Exp).then_inc(sem("e_ab"), 1)

            def head_selector(b, slot):
                src = (sel2[:, ds(b, 64)] if not isinstance(b, int) else sel2[:, b:b + 64]).bitcast(F32)
                act.activation(dsel[slot][:, :, :], src.rearrange("p (h k) -> p h k", k=B)[:, :, 0:1].to_broadcast([128, H1, 128]),
                               ACT.Copy).then_inc(sem("dsel_done"), 1)

            head_selector(0, 0)
            act.wait_ge(sem("w_copied"), 2)
            with act.Fori(0, B // 2) as i:
                for k in range(2):
                    g = i * 2 + k
                    act.wait_ge(sem("scan2_done"), g + 1)
                    for r in range(4):
                        act.wait_ge(sem("w_bc"), g * 4 + r + 1)
                        act.activation(Wb[k][:, r * CH:r * CH + CH], bank(r % 2), ACT.Copy).then_inc(sem("w_copied"), 1)
                    act.wait_ge(sem("u_bc"), g * 4 + 1)
                    head_selector(g + 1, 1 - k)
                    act.wait_ge(sem("signed_done"), g + 1)
                    act.wait_ge(sem("scan1_done"), g + 2)
                    act.activation(sgb[:, :], r0b[k][:, :], ACT.Sign, bias=tiny[:, 0:1]).then_inc(sem("sgn_done"), 1)
                    act.wait_ge(sem("diff_done"), g + 2)
                    act.activation(dfb[k][:, :], dfb[k][:, :], ACT.Abs).then_inc(sem("abs_done"), 1)
            def transposed(c):
                act.wait_ge(sem("ln_T"), 3 * NC_ + c + 1)
                act.activation(XTf[:, c * CH:c * CH + CH], bank(c), ACT.Copy).then_inc(sem("ln_hi"), 1)

            in_turn(lambda c: ln_norm(act, 3, c), transposed, 1)
            for h in range(2):
                act.wait_ge(sem("es_step"), 6 + 2 * h)
                act.activation(SE[:, 8 * h:8 * h + 8, :], SE[:, 8 * h:8 * h + 8, :], ACT.Exp).then_inc(sem("e_exp"), 1)
            for c in range(NC_):
                act.wait_ge(sem("e_T"), c + 1)
                act.activation(PE_T[:, c * CH:c * CH + CH], bank(c)[0:64, :], ACT.Copy).then_inc(sem("e_pt"), 1)
            in_turn(lambda c: ln_norm(act, 4, c), lambda c: ln_hi(act, 4, c), 1)
            for c in range(NC_):
                act.wait_ge(sem("router_T"), NC_ + c + 1)
                act.activation(FL[:, c * CH:c * CH + CH], bank(4 + c)[0:64, :], ACT.Copy).then_inc(sem("router_out"), 1)
                if c % 2:
                    h = c // 2
                    act.wait_ge(sem("logits_T"), h + 2)
                    act.activation(SCo[:, 8 * h:8 * h + 8, :], bank(4 + h).rearrange("p (t e) -> p t e", e=E1), ACT.Exp,
                                   scale=-1.0).then_inc(sem("f_exp"), 1)
            for c in range(NC_):
                act.wait_ge(sem("sh_g"), c + 1)
                if c >= 2:
                    act.wait_ge(sem("sh_h"), c - 1)
                act.activation(FG[:, c % 2, :], bank(6), ACT.Silu).then_inc(sem("sh_sg"), 1)
                act.wait_ge(sem("sh_h"), c + 1)
                if c >= 2:
                    act.wait_ge(sem("sh_down"), c - 1)
                act.activation(FHH[:, c % 2, :], FH[:, c % 2, :], ACT.Copy).then_inc(sem("sh_hh"), 1)
            for h in range(2):
                act.wait_ge(sem("f_step"), F_STEPS - 1 + h)
                act.activation(GI1[:, 8 * h:8 * h + 8, 0:64], FM[:, 8 * h:8 * h + 8, :], ACT.Copy).then_inc(sem("f_hi"), 1)
            for c in range(NC_):
                act.wait_ge(sem("gates_T"), NC_ + c + 1)
                act.activation(SELT1[:, c * CH:c * CH + CH], bank(4 + c), ACT.Copy).then_inc(sem("gates_out"), 1)

            def round_f(U, k):
                act.wait_ge(sem("fh_done"), U + 1)
                act.activation(FHH[:, (k - 1) % 4, :], FH[:, (k - 1) % 4, :], ACT.Copy).then_inc(sem("fhh_done"), 1)

            act.wait_ge(sem("sh_down"), NC_)
            with act.Fori(0, E1 // 4) as i:
                for k in range(8):
                    U = i * 8 + k
                    act.wait_ge(sem("ft_done"), U + 1)
                    act.wait_ge(sem("g_ready"), U + 1)
                    act.activation(FG[:, k % 2, :], bank(4 + k % 2), ACT.Silu).then_inc(sem("fg_done"), 1)
                    round_f(U, k)
            round_f(E1 * 2, 0)
            act.wait_ge(sem("fdown_done"), E1 * 2 + 2 + 8)
            for c in range(NC_):
                act.activation(OT1[:, c * CH:c * CH + CH], bank(c), ACT.Copy).then_inc(sem("experts_out"), 1)
            for c in range(NC_):
                ln_norm(act, 5, c, sum_bank)

        @block.vector
        def _(dve):
            dve.wait_ge(sem("consts"), 5)
            dve.memset(sel2[:, 64:72].bitcast(F32), 0.0)
            dve.tensor_tensor(sel2[:, 0:64], ident[:, 0:64], ident[:, 64:128], ALU.add).then_inc(sem("sel2_done"), 1)
            dve.tensor_reduce(halfones[:, :], ident[:, :].rearrange("p (a c) -> p a c", a=2), AX.X, ALU.add).then_inc(sem("halves"), 1)
            dve.wait_ge(sem("ctx_act"), CTX_ACT["ck_exp"])
            dve.tensor_scalar(ce[:, :, :], ce[:, :, :], 1.0, -1.0, ALU.min, ALU.add).then_inc(sem("ctx_dve"), 1)
            dve.wait_ge(sem("ctx_dve"), CTX_DVE["ck_neg"])
            dve.tensor_tensor(ck[:, :, :], bank(0).rearrange("p (a d) -> p a d", a=4), ce[:, :, :], ALU.max).then_inc(sem("ctx_dve"), 1)
            def fold_rest(n):
                dve.wait_ge(sem("fold_hi"), n + 1)
                cols = slice(n % 4 * CH, n % 4 * CH + CH)
                hi, lo = (NVh, NVl) if n < 4 else (Mh, Ml)
                dve.scalar_tensor_tensor(lo[:, cols], fold_bank(n), 1.0 if n < 4 else -1.0 / math.sqrt(DH),
                                         hi[:, cols].bitcast(F32), ALU.mult, ALU.subtract).then_inc(sem("fold_lo"), 1)

            dve.wait_ge(sem("ctx_pe"), CTX_PE["kn_ready"])
            dve.tensor_scalar(kn[:, :], bank(2, B), float(S), None, ALU.mult).then_inc(sem("ctx_dve"), 1)
            for n in range(4):
                fold_rest(n)
            dve.wait_ge(sem("ctx_pe"), CTX_PE["gt_ready"])
            dve.tensor_tensor(GBT[:, :, :], bank(0, CH, 2).rearrange("p (b d) -> p b d", b=B),
                              blockones[:, :].rearrange("p (o d) -> p o d", o=1).to_broadcast([128, B, 128]),
                              ALU.mult).then_inc(sem("ctx_dve"), 1)
            for n in range(4, 8):
                fold_rest(n)

            def split_x(b, slot):
                dve.tensor_tensor(xl[slot][:, :], xall[:, ds(b * S, S)] if not isinstance(b, int) else xall[:, b * S:b * S + S],
                                  xh[slot][:, :].bitcast(F32), ALU.subtract).then_inc(sem("xl_done"), 1)

            dve.wait_ge(sem("xh_done"), 1)
            split_x(0, 0)
            dve.memset(Xp[:, 0:S], 0.0)
            dve.wait_ge(sem("fold_lo"), 8)
            dve.memset(bank(7), 0.0).then_inc(sem("acc_free"), 1)
            dve.wait_ge(sem("ctx_act"), CTX_ACT["g2_done"])
            dve.memset(bank(2, CH, 2), 0.0).then_inc(sem("s_ready"), 1)
            dve.wait_ge(sem("ctx_act"), CTX_ACT["wq_hi"])
            dve.tensor_tensor(wql[:, :], wx[:, 3, :], wqh[:, :].bitcast(F32), ALU.subtract).then_inc(sem("ctx_dve"), 1)
            dve.wait_ge(sem("wr_in"), 16)
            dve.wait_ge(sem("wr_zero"), 2)
            dve.tensor_copy(wrh[:, 0:E0R], wr_in[:, :]).then_inc(sem("ctx_dve"), 1)
            dve.wait_ge(sem("ctx_dve"), CTX_DVE["wr_split"] - 1)
            dve.tensor_tensor(wrl[:, 0:E0R], wr_in[:, :], wrh[:, 0:E0R].bitcast(F32), ALU.subtract).then_inc(sem("ctx_dve"), 1)

            dve.wait_ge(sem("x_in"), 16)

            def mask_and_max(g, k):
                par, slot = (k - 1) % 2, (k - 1) % 4
                dve.wait_ge(sem("s_ready"), g + 1)
                dve.memset(scratch[:, 5:6], 0.0)
                for q in range(4):
                    c, w = piece(q)
                    dve.tensor_tensor_reduce(out=P[:, slot, c:c + w], in0=scores(par, q), in1=cmask[:, 256 - w:256],
                                             scale=1.0, scalar=3e38, op0=ALU.add, op1=ALU.min,
                                             accum_out=mn[:, par, q:q + 1]).then_inc(sem("masked"), 1)

            def invert(g, k):
                par = (k - 1) % 2
                dve.wait_ge(sem("exp_done"), g + 1)
                dve.reciprocal(rl[:, par, :], ls[:, par, :]).then_inc(sem("rl_done"), 1)

            def copy_pt(g, k):
                dve.wait_ge(sem("t_ready"), g + 1)
                dve.tensor_copy(PT[:, k % 2, :, :], PTP).then_inc(sem("pt_done"), 1)

            def add_out(b, g):
                dve.wait_ge(sem("pv_done"), g + 1)
                x = Xp[:, ds(b * S, S)] if not isinstance(b, int) else Xp[:, b * S:b * S + S]
                dve.tensor_tensor(x, x, OB[:, 0:256], ALU.add).then_inc(sem("acc_free"), 1)

            with dve.Fori(0, B // 2) as i:
                for k in range(STEPS):
                    g = i * STEPS + k
                    mask_and_max(g, k)
                    dve.wait_ge(sem("u_hi"), g + 1)
                    dve.tensor_tensor(Ul[:, :], UB, Uh[:, :].bitcast(F32), ALU.subtract).then_inc(sem("u_lo"), 1)
                    copy_pt(g, k)
                    if k in (2, 10):
                        add_out(i * 2 + k // 8, g)
                    invert(g, k)
                    if k in (4, 12):
                        dve.wait_ge(sem("xh_done"), i * 2 + (2 if k == 4 else 3))
                        split_x(i * 2 + (1 if k == 4 else 2), 1 if k == 4 else 0)
            G = B * PAIRS
            mask_and_max(G, 0)
            copy_pt(G, 0)
            invert(G, 0)
            copy_pt(G + 1, 1)
            add_out(B, G + 2)
            dve.wait_ge(sem("acc_free"), B + 2)
            in_turn(lambda c: ln_stats(dve, 0, c), lambda c: ln_lo(dve, 0, c), 2)

            for c in range(NC_):
                cc = slice(c * CH, c * CH + CH)
                dve.wait_ge(sem("q_exp"), c + 1)
                dve.tensor_scalar(EQ[:, cc], EQ[:, cc], 1.0, -1.0, ALU.min, ALU.add).then_inc(sem("q_neg"), 1)
                dve.wait_ge(sem("q_neg"), c + 1)
                dve.scalar_tensor_tensor(Q[:, cc], bank(4 + c), bq[:, 0:1], EQ[:, cc], ALU.add, ALU.max).then_inc(sem("q_elu"), 1)
            dve.memset(tiny[:, :], 1e-37)
            dve.memset(abr[:, :].bitcast(F32), 0.0).then_inc(sem("wr1"), 1)
            dve.memset(onesr[:, :].bitcast(F32), 1.0).then_inc(sem("l1_split"), 1)
            dve.wait_ge(sem("l1_in"), 16 * 7)
            dve.memset(wr1h[:, :].bitcast(F32), 0.0).then_inc(sem("wr1"), 1)
            dve.memset(wr1l[:, :].bitcast(F32), 0.0).then_inc(sem("wr1"), 1)
            dve.wait_ge(sem("wr1"), 3)
            dve.tensor_copy(wr1h[:, 0:E1], wr1_in[:, :]).then_inc(sem("wr1"), 1)
            dve.tensor_copy(wdh[:, :], wd_in[:, :]).then_inc(sem("wr1"), 1)
            dve.tensor_copy(wshh[:, :], wsh[:, :]).then_inc(sem("wr1"), 1)
            dve.tensor_copy(abr[0:1, :], abias[:, :]).then_inc(sem("wr1"), 1)
            dve.wait_ge(sem("wr1"), 7)
            dve.tensor_tensor(abr[32:33, :], abias[:, :], abr[0:1, :].bitcast(F32), ALU.subtract).then_inc(sem("l1_split"), 1)
            dve.tensor_tensor(wr1l[:, 0:E1], wr1_in[:, :], wr1h[:, 0:E1].bitcast(F32), ALU.subtract).then_inc(sem("l1_split"), 1)
            dve.tensor_tensor(wdl[:, :], wd_in[:, :], wdh[:, :].bitcast(F32), ALU.subtract).then_inc(sem("l1_split"), 1)
            dve.tensor_scalar(wo1e[:, :], wo1[:, :], EPS / 2, None, ALU.mult)
            dve.tensor_tensor(wshl[:, :], wsh[:, :], wshh[:, :].bitcast(F32), ALU.subtract).then_inc(sem("l1_split"), 1)

            for c in range(NC_):
                cc = slice(c * CH, c * CH + CH)
                dve.wait_ge(sem("q_sq"), c + 1)
                dve.wait_ge(sem("q_inv"), c + 1)
                dve.tensor_tensor(Q[:, cc], Q[:, cc], RQ[:, cc], ALU.mult).then_inc(sem("q_done"), 1)

            def add_bank(c, b):
                x = Xp[:, S + c * CH:S + c * CH + CH]
                dve.tensor_tensor(x, x, bank(b), ALU.add).then_inc(sem("x_added"), 1)

            def add_query_out(c):
                dve.wait_ge(sem("b_out"), c + 1)
                add_bank(c, 4 + c)
                dve.wait_ge(sem("x_added"), c + 1)
                ln_stats(dve, 1, c)

            in_turn(add_query_out, lambda c: ln_lo(dve, 1, c), 2)

            dve.wait_ge(sem("rms"), 4 * NC_)
            dve.reciprocal(lm[:, :], rs2[:, :]).then_inc(sem("g_step"), 1)
            dve.wait_ge(sem("g_step"), 1)
            dve.wait_ge(sem("logits_T"), 1)
            bc = lambda v, w: v.rearrange("p (t o) -> p t o", o=1).to_broadcast([128, T, w])
            dve.tensor_tensor(Lg[:, :, :], bank(0, 256).rearrange("p (t e) -> p t e", e=16)[:, :, 0:E0R],
                              bc(lm[:, :], E0R), ALU.mult).then_inc(sem("g_step"), 1)
            dve.wait_ge(sem("g_step"), 2)
            dve.tensor_reduce(lz[:, :], Lg[:, :, :], AX.X, ALU.max).then_inc(sem("g_step"), 1)
            dve.wait_ge(sem("g_step"), 3)
            dve.tensor_tensor(Lg[:, :, :], Lg[:, :, :], bc(lz[:, :], E0R), ALU.subtract).then_inc(sem("lg_sub"), 1)
            dve.wait_ge(sem("lg_exp"), 1)
            dve.tensor_reduce(lm[:, :], Lg[:, :, :], AX.X, ALU.add).then_inc(sem("g_step"), 1)
            dve.wait_ge(sem("g_step"), 4)
            dve.reciprocal(lz[:, :], lm[:, :]).then_inc(sem("g_step"), 1)
            dve.wait_ge(sem("g_step"), 5)
            dve.wait_ge(sem("g20_init"), 2)
            dve.tensor_tensor(G20[:, :, 0:E0R], Lg[:, :, :], bc(lz[:, :], E0R), ALU.mult).then_inc(sem("g_step"), 1)
            dve.wait_ge(sem("g_step"), 6)
            for t in range(T):
                last = dve.max(M8[:, t, :], G20[:, t, :])
            last.then_inc(sem("g_step"), 1)
            dve.wait_ge(sem("g_step"), 7)
            dve.tensor_copy(RPL[:, :, 0:2], M8[:, :, 0:2]).then_inc(sem("g_step"), 1)
            dve.wait_ge(sem("g_step"), 8)
            for t in range(T):
                last = dve.match_replace(RP[:, t, :], RPL[:, t, :], G20[:, t, :], -5.0)
            last.then_inc(sem("g_step"), 1)
            dve.wait_ge(sem("g_step"), 9)
            dve.scalar_tensor_tensor(Lg[:, :, :], RP[:, :, 0:E0R], -4.0, G20[:, :, 0:E0R], ALU.is_lt, ALU.mult).then_inc(sem("g_step"), 1)
            dve.wait_ge(sem("g_step"), 10)
            dve.tensor_reduce(lm[:, :], Lg[:, :, :], AX.X, ALU.add).then_inc(sem("g_step"), 1)
            dve.wait_ge(sem("g_step"), 11)
            dve.tensor_scalar(lm[:, :], lm[:, :], 1e-9, None, ALU.add).then_inc(sem("g_step"), 1)
            dve.wait_ge(sem("g_step"), 12)
            dve.reciprocal(lz[:, :], lm[:, :]).then_inc(sem("g_step"), 1)
            dve.wait_ge(sem("g_step"), 13)
            dve.tensor_tensor(Lg[:, :, :], Lg[:, :, :], bc(lz[:, :], E0R), ALU.mult).then_inc(sem("g_step"), 1)
            dve.wait_ge(sem("g_step"), 14)
            dve.wait_ge(sem("c_zeros"), 4)
            dve.tensor_copy(GI[:, :, 0:E0R], Lg[:, :, :]).then_inc(sem("g_step"), 1)
            dve.wait_ge(sem("g_step"), 15)
            dve.tensor_tensor(GI[:, :, 64:64 + E0R], Lg[:, :, :], GI[:, :, 0:E0R].bitcast(F32), ALU.subtract).then_inc(sem("gates_split"), 1)

            def rest_h(U, k):
                dve.wait_ge(sem("hh_done"), U + 1)
                dve.tensor_tensor(HL[:, (k - 1) % 4, :], Hf[:, (k - 1) % 4, :], HH[:, (k - 1) % 4, :].bitcast(F32),
                                  ALU.subtract).then_inc(sem("hl_done"), 1)

            with dve.Fori(0, E0 // 2) as i:
                for k in range(16):
                    U = i * 16 + k
                    if k % 2 == 0:
                        dve.wait_ge(sem("gb_ready"), i * 8 + k // 2 + 1)
                    dve.wait_ge(sem("sg_done"), U + 3)
                    dve.tensor_tensor(Hf[:, k % 4, :], SG[:, k % 2, :], bank(4 + k // 2 % 2), ALU.mult).then_inc(sem("h_done"), 1)
                    rest_h(U, k)
            rest_h(E0 * 8, 0)

            def sums_stats(c):
                dve.wait_ge(sem("experts_T"), c + 1)
                ln_stats(dve, 2, c, sum_bank)

            in_turn(sums_stats, lambda c: ln_lo(dve, 2, c), 2)
            def softplus_sums(first, end):
                dve.wait_ge(sem("z_sp"), end)
                dve.tensor_reduce(ABs[:, 0, first:end, :].rearrange("p t h -> p (t h)"),
                                  ZR[:, first:end, :].rearrange("p t (h d) -> p (t h) d", h=H1), AX.X, ALU.add).then_inc(sem("ab_sums"), 1)

            def signed_values(c):
                cc = slice(c * CH, c * CH + CH)
                dve.wait_ge(sem("dv_ready"), c + 1)
                dve.tensor_scalar(VS[:, cc], bank(c % 2), 0.0, 2 * EPS, ALU.is_ge, ALU.mult).then_inc(sem("vp_done"), 1)
                dve.wait_ge(sem("vp_done"), 2 * c + 1)
                dve.scalar_tensor_tensor(VP[:, cc], bank(c % 2), EPS, VS[:, cc], ALU.subtract, ALU.add).then_inc(sem("vp_done"), 1)

            for t in range(T):
                p = t % 2
                dve.wait_ge(sem("qs_done"), t + 1)
                dve.wait_ge(sem("dk_ready"), t + 1)
                dve.tensor_tensor(PR[:, p, :], bank(2 + p), QS[:, p, :], ALU.mult).then_inc(sem("pr_done"), 1)
                dve.wait_ge(sem("z_abs"), t + 1)
                dve.tensor_scalar(ZR[:, t, :], bank(6 + p), 0.0, None, ALU.max).then_inc(sem("z_pos"), 1)
                dve.wait_ge(sem("pr_done"), t + 1)
                dve.tensor_reduce(ABs[:, 1, t, :], PR[:, p, :].rearrange("p (h d) -> p h d", h=H1), AX.X, ALU.add).then_inc(sem("b_sum"), 1)
                if t % 4 == 3:
                    signed_values(t // 4)
                for first, end in SP_GROUPS:
                    if t == end + 1:
                        softplus_sums(first, end)
            softplus_sums(*SP_GROUPS[-1])
            dve.wait_ge(sem("b_sum"), T)
            dve.wait_ge(sem("ab_sums"), len(SP_GROUPS))
            for n, scale in ((1, 1.0 / math.sqrt(64)), (0, -1.0)):
                src = ABs[:, n, :, :].rearrange("p (b r) h -> p r h b", r=2)
                for r in range(2):
                    dve.tensor_scalar(ABt[:, r, n, :, :], src[:, r, :, :], scale, None, ALU.mult).then_inc(sem("ab_placed"), 1)
            dve.wait_ge(sem("ab_T"), 1)
            dve.tensor_copy(AB64[:, :, :], bank(2)[0:64, :].rearrange("p (n t) -> p n t", n=2)).then_inc(sem("ab_in"), 1)
            dve.wait_ge(sem("ab_in"), 1)
            dve.wait_ge(sem("d_init"), 2)
            av, bv = AB64[:, 0, :], AB64[:, 1, :]
            dve.tensor_tensor_scan(mb[:, 1:], av, bv, -BIG, ALU.add, ALU.max).then_inc(sem("r_step"), 1)
            dve.wait_ge(sem("r_step"), 1)
            dve.tensor_tensor(ea[:, :], av, mb[:, 0:S], ALU.add).then_inc(sem("r_step"), 1)
            dve.tensor_tensor(eb[:, :], bv, mb[:, 1:], ALU.subtract).then_inc(sem("r_step"), 1)
            dve.wait_ge(sem("r_step"), 3)
            dve.tensor_tensor(ea[:, :], ea[:, :], mb[:, 1:], ALU.subtract).then_inc(sem("ea_arg"), 1)
            dve.wait_ge(sem("e_ab"), 2)
            dve.tensor_tensor_scan(db[:, 1:], ea[:, :], eb[:, :], 0.0, ALU.mult, ALU.add).then_inc(sem("r_step"), 1)
            dve.wait_ge(sem("r_step"), 4)
            dve.reciprocal(rd[:, :], db[:, 1:]).then_inc(sem("r_step"), 1)
            dve.tensor_tensor(ea[:, :], ea[:, :], db[:, 0:S], ALU.mult).then_inc(sem("r_step"), 1)
            dve.wait_ge(sem("r_step"), 6)
            dve.tensor_tensor(wu[:, 0, :], ea[:, :], rd[:, :], ALU.mult).then_inc(sem("r_step"), 1)
            dve.tensor_tensor(wu[:, 1, :], eb[:, :], rd[:, :], ALU.mult).then_inc(sem("r_step"), 1)
            dve.wait_ge(sem("r_step"), 8)
            dve.tensor_copy(WUr[0:64, :, :], wu[:, :, :]).then_inc(sem("r_step"), 1)
            dve.wait_ge(sem("r_step"), 9)
            dve.tensor_tensor(WUr[64:128, :, :], wu[:, :, :], WUr[0:64, :, :].bitcast(F32), ALU.subtract).then_inc(sem("wu_done"), 1)
            dve.memset(scratch[:, 6:7], 0.0).then_inc(sem("qr_done"), 1)
            dve.memset(scratch[:, 7:8], 0.0).then_inc(sem("u_bc"), 1)
            dve.memset(bank(3), 0.0).then_inc(sem("scan1_done"), 1)
            dve.memset(scratch[:, 10:11], 0.0).then_inc(sem("diff_done"), 1)
            dve.memset(scratch[:, 8:9], 0.0).then_inc(sem("y0_done"), 1)
            dve.memset(scratch[:, 9:10], 0.0).then_inc(sem("y1_done"), 1)

            def last_scan(g, par):
                dve.wait_ge(sem("floor_done"), g + 2)
                dve.wait_ge(sem("y1_done"), g + 1)
                dve.tensor_tensor_scan(rb[1 - par][:, :], Wb[1 - par][:, :], gb[1 - par][:, :], 0.0, ALU.mult, ALU.add).then_inc(sem("scan2_done"), 1)

            dve.wait_ge(sem("w_copied"), 2)
            dve.wait_ge(sem("signed_done"), 1)
            with dve.Fori(0, B // 2) as i:
                for k in range(2):
                    g = i * 2 + k
                    dve.wait_ge(sem("diff_done"), g + 1)
                    for r in range(4):
                        dve.wait_ge(sem("u_bc"), g * 4 + r + 2)
                        v = VP[:, ds(g * S, S)].rearrange("p (o t) -> p o t", o=1).to_broadcast([128, 2, S])
                        dve.tensor_tensor(qb[:, r * CH:r * CH + CH].rearrange("p (h t) -> p h t", h=2),
                                          bank(2).rearrange("p (h t) -> p h t", h=2), v, ALU.mult).then_inc(sem("qr_done"), 1)
                    dve.wait_ge(sem("qr_done"), g * 4 + 5)
                    dve.wait_ge(sem("w_copied"), g * 4 + 6)
                    dve.wait_ge(sem("y0_done"), g + 1)
                    dve.wait_ge(sem("floor_done"), g + 1)
                    dve.tensor_tensor_scan(r0b[k][:, :], Wb[k][:, :], qb[:, :], 0.0, ALU.mult, ALU.add).then_inc(sem("scan1_done"), 1)
                    dve.wait_ge(sem("scan1_done"), g + 2)
                    dve.scalar_tensor_tensor(dfb[k][:, :], qb[:, :], -2.0, r0b[k][:, :], ALU.mult, ALU.add).then_inc(sem("diff_done"), 1)
                    last_scan(g, k)
            last_scan(B, 0)
            for c in range(NC_):
                dve.wait_ge(sem("y1_done"), 2 * c + 5)
                add_bank(c, 4 + c)
                dve.wait_ge(sem("x_added"), NC_ + c + 1)
                ln_stats(dve, 3, c)

            def masked_scores(h):
                sc_ = bank(4 + h).rearrange("p (b r s) -> p b r s", b=B // 2, r=2)
                sev = SE[:, 8 * h:8 * h + 8, :].rearrange("p (b r) s -> p b r s", r=2)
                dve.wait_ge(sem("es_ready"), 2 * h + 2)
                dve.tensor_tensor(sev[:, :, 0, :], sc_[:, :, 0, :], cmask[:, 128:192].rearrange("p (o s) -> p o s", o=1)
                                  .to_broadcast([128, B // 2, SC]), ALU.subtract).then_inc(sem("es_step"), 1)
                dve.tensor_copy(sev[:, :, 1, :], sc_[:, :, 1, :]).then_inc(sem("es_step"), 1)

            def row_reduce(h, after, op):
                tt = slice(8 * h, 8 * h + 8)
                dve.wait_ge(sem("es_step"), after)
                dve.tensor_reduce(em[:, tt], SE[:, tt, :], AX.X, op).then_inc(sem("es_step"), 1)

            def less_maximum(h, after):
                tt = slice(8 * h, 8 * h + 8)
                dve.wait_ge(sem("es_step"), after)
                dve.tensor_tensor(SE[:, tt, :], SE[:, tt, :], em[:, tt].rearrange("p (t o) -> p t o", o=1).to_broadcast([128, 8, SC]),
                                  ALU.subtract).then_inc(sem("es_step"), 1)

            masked_scores(0)
            row_reduce(0, 2, ALU.max)
            masked_scores(1)
            less_maximum(0, 3)
            row_reduce(1, 5, ALU.max)
            less_maximum(1, 7)
            for h in range(2):
                dve.wait_ge(sem("e_exp"), h + 1)
                row_reduce(h, 8, ALU.add)
            for h in range(2):
                dve.wait_ge(sem("es_step"), 9 + h)
                dve.reciprocal(el[:, 8 * h:8 * h + 8], em[:, 8 * h:8 * h + 8]).then_inc(sem("es_step"), 1)
            for c in range(NC_):
                dve.wait_ge(sem("e_out"), c + 1)
                add_bank(c, 4 + c)
                dve.wait_ge(sem("x_added"), 2 * NC_ + c + 1)
                ln_stats(dve, 4, c)
                if c >= 2:
                    ln_lo(dve, 4, c - 2)
            ln_lo(dve, 4, 2)
            ln_lo(dve, 4, 3)

            count = [0]
            last_step = [0, 0]
            dve.wait_ge(sem("f_init"), 6)

            def step(ops, pool_steps=0):
                for h in range(2):
                    if pool_steps:
                        dve.wait_ge(sem("f_pool"), pool_steps + h)
                    else:
                        dve.wait_ge(sem("f_step"), last_step[h])
                    tt = slice(8 * h, 8 * h + 8)
                    last = [op(tt) for op in ops][-1]
                    last.then_inc(sem("f_step"), 1)
                    count[0] += 1
                    last_step[h] = count[0]

            def by_tile(op):
                return lambda tt: [op(t) for t in range(tt.start, tt.stop)][-1]

            def shared_hidden(c):
                dve.wait_ge(sem("sh_u"), c + 1)
                dve.wait_ge(sem("sh_sg"), c + 1)
                if c >= 2:
                    dve.wait_ge(sem("sh_hl"), c - 1)
                    dve.wait_ge(sem("sh_hh"), c - 1)
                dve.tensor_tensor(FH[:, c % 2, :], FG[:, c % 2, :], bank(7), ALU.mult).then_inc(sem("sh_h"), 1)

            gr = lambda x, tt: x[:, 8 * tt.start:8 * tt.stop, :]
            g8 = lambda x, tt: x[:, tt, :].rearrange("p t (g e) -> p (t g) e", e=8)
            tg = lambda x, tt: gr(x, tt).rearrange("p (t g) o -> p t (g o)", g=8)
            b8 = lambda v, w: v.rearrange("p (t o) -> p t o", o=1).to_broadcast([128, 8, w])
            for h in range(2):
                tt = slice(8 * h, 8 * h + 8)
                dve.wait_ge(sem("f_exp"), h + 1)
                dve.tensor_scalar(SCo[:, tt, :], SCo[:, tt, :], 1.0, None, ALU.add).then_inc(sem("f_step"), 1)
                dve.wait_ge(sem("f_step"), 2 * h + 1)
                dve.reciprocal(SCo[:, tt, :], SCo[:, tt, :]).then_inc(sem("f_step"), 1)
                count[0] += 2
            shared_hidden(0)
            step([lambda tt: dve.tensor_tensor(gr(h1, tt), g8(SF, tt)[:, :, 0:4], g8(SF, tt)[:, :, 4:8], ALU.max),
                  lambda tt: dve.tensor_tensor(gr(l1, tt), g8(SF, tt)[:, :, 0:4], g8(SF, tt)[:, :, 4:8], ALU.min)], pool_steps=1)
            step([lambda tt: dve.tensor_tensor(gr(h2, tt), gr(h1, tt)[:, :, 0:2], gr(h1, tt)[:, :, 2:4], ALU.max),
                  lambda tt: dve.tensor_tensor(gr(t2, tt), gr(h1, tt)[:, :, 0:2], gr(h1, tt)[:, :, 2:4], ALU.min),
                  lambda tt: dve.tensor_tensor(gr(l2, tt), gr(l1, tt)[:, :, 0:2], gr(l1, tt)[:, :, 2:4], ALU.max)])
            step([lambda tt: dve.tensor_tensor(gr(l2, tt), gr(l2, tt), gr(t2, tt), ALU.max)])
            step([lambda tt: dve.tensor_tensor(gr(h3, tt), gr(h2, tt)[:, :, 0:1], gr(h2, tt)[:, :, 1:2], ALU.max),
                  lambda tt: dve.tensor_tensor(gr(t3, tt), gr(h2, tt)[:, :, 0:1], gr(h2, tt)[:, :, 1:2], ALU.min),
                  lambda tt: dve.tensor_tensor(gr(l3, tt), gr(l2, tt)[:, :, 0:1], gr(l2, tt)[:, :, 1:2], ALU.max)])
            step([lambda tt: dve.tensor_tensor(gr(l3, tt), gr(l3, tt), gr(t3, tt), ALU.max)])
            step([lambda tt: dve.tensor_tensor(GS[:, tt, 0:8], tg(h3, tt), tg(l3, tt), ALU.add)])
            step([by_tile(lambda t: dve.max(F8[:, t, :], GS[:, t, 0:8]))])
            shared_hidden(1)
            step([lambda tt: dve.tensor_copy(FR[:, tt, 0:4], F8[:, tt, 0:4])])
            step([by_tile(lambda t: dve.match_replace(GR[:, t, :], FR[:, t, :], GS[:, t, :], -NEG))])
            step([lambda tt: dve.tensor_scalar(gm[:, tt, :], GR[:, tt, 0:8], 2.9e38, None, ALU.is_ge)])
            shared_hidden(2)
            step([by_tile(lambda t: dve.max(F8[:, t, :], FM[:, t, :]))], pool_steps=3)
            step([by_tile(lambda t: dve.match_replace(FRP[:, t, :], F8[:, t, :], FM[:, t, :], NEG))])
            shared_hidden(3)
            step([lambda tt: dve.scalar_tensor_tensor(FM[:, tt, :], FRP[:, tt, :], -2.9e38, SCo[:, tt, :], ALU.is_le, ALU.mult)])
            step([lambda tt: dve.tensor_reduce(fs[:, tt], FM[:, tt, :], AX.X, ALU.add)])
            step([lambda tt: dve.tensor_scalar(fs[:, tt], fs[:, tt], 1e-20, None, ALU.add)])
            step([lambda tt: dve.reciprocal(fi[:, tt], fs[:, tt])])
            step([lambda tt: dve.tensor_scalar(fi[:, tt], fi[:, tt], 2.5, None, ALU.mult)])
            step([lambda tt: dve.tensor_tensor(FM[:, tt, :], FM[:, tt, :], b8(fi[:, tt], E1), ALU.mult)])

            def rest_f(U, k):
                dve.wait_ge(sem("fhh_done"), U + 1)
                dve.tensor_tensor(FHL[:, (k - 1) % 4, :], FH[:, (k - 1) % 4, :], FHH[:, (k - 1) % 4, :].bitcast(F32),
                                  ALU.subtract).then_inc(sem("fhl_done"), 1)

            dve.wait_ge(sem("sh_hl"), NC_)
            dve.wait_ge(sem("sh_hh"), NC_)
            dve.wait_ge(sem("sh_down"), NC_)
            with dve.Fori(0, E1 // 4) as i:
                for k in range(8):
                    U = i * 8 + k
                    dve.wait_ge(sem("fg_done"), U + 3)
                    dve.wait_ge(sem("fu_ready"), U + 1)
                    dve.tensor_tensor(FU[:, k % 2, :], FG[:, k % 2, :], bank(6), ALU.mult).then_inc(sem("ft_done"), 1)
                    rest_f(U, k)
                    dve.wait_ge(sem("ft_done"), U + 3)
                    dve.wait_ge(sem("fgb_ready"), U + 1)
                    dve.tensor_tensor(FH[:, k % 4, :], FU[:, k % 2, :], bank(7), ALU.mult).then_inc(sem("fh_done"), 1)
            rest_f(E1 * 2, 0)
            for c in range(NC_):
                dve.wait_ge(sem("experts_T"), NC_ + c + 1)
                ln_stats(dve, 5, c, sum_bank)

        @block.tensor
        def _(pe):
            def mm3(dst, l, r, start=True, stop=True, skip=False):
                pe.matmul(dst, l[0], r[0], start=start, stop=False, skip_group_check=skip)
                pe.matmul(dst, l[0], r[1], start=False, stop=False, skip_group_check=skip)
                return pe.matmul(dst, l[1], r[0], start=False, stop=stop, skip_group_check=skip)

            def fold(n):
                pe.wait_ge(sem("w_vo_in" if n < 4 else "w_qk_in"), 32)
                if n >= 4:
                    pe.wait_ge(sem("fold_lo"), n - 3)
                l, r = (w64["v"], w64["o"]) if n < 4 else (w64["q"], w64["k"])
                for h in range(4):
                    last = pe.matmul(fold_bank(n)[:, h * 128:h * 128 + 128], l[:, n % 4 * 4 + h, :], r[:, n % 4 * 4 + h, :],
                                     start=True, stop=True)
                last.then_inc(sem("fold"), 1)

            pe.wait_ge(sem("ctx_in"), 64)
            pe.wait_ge(sem("consts"), 5)
            for n in range(2):
                for p in range(4):
                    dst = bank(n)[:, p * 128:p * 128 + 128]
                    pe.matmul(dst, ctxT[:, p * 128:p * 128 + 128], wx[:, n, :], start=True, stop=False)
                    last = pe.matmul(dst, ones[0:1, :], brow[0:1, n * 128:n * 128 + 128], start=False, stop=True)
                last.then_inc(sem("ctx_pe"), 1)
            for n in range(4):
                fold(n)
            pe.wait_ge(sem("halves"), 1)
            pe.wait_ge(sem("ctx_pool"), CTX_POOL["ck_sq"])
            for p in range(4):
                last = pe.matmul(bank(2)[:, 2 * p:2 * p + 2], csq[:, p, :], halfones[:, :], start=True, stop=True)
            last.then_inc(sem("ctx_pe"), 1)
            pe.wait_ge(sem("ctx_dve"), CTX_DVE["ck_done"])
            pe.wait_ge(sem("ctx_act"), CTX_ACT["cv_done"])
            for b in range(B):
                r = slice(b % 2 * 64, b % 2 * 64 + 64)
                last = pe.matmul(bank(b % 2)[:, b // 2 * 128:b // 2 * 128 + 128], cv[r, b // 2, :], ck[r, b // 2, :],
                                 start=True, stop=True)
            last.then_inc(sem("ctx_pe"), 1)
            for n in range(4, 8):
                fold(n)
            pe.wait_ge(sem("ctx_dve"), CTX_DVE["gbt_done"])
            pe.wait_ge(sem("ctx_dve"), CTX_DVE["kn_sum"])
            for b in range(B):
                last = pe.matmul(bank(2 + b % 2)[:, b // 2 * 128:b // 2 * 128 + 128], GBT[:, b % 2 * 4 + b // 2, :], wx[:, 2, :],
                                 start=True, stop=True)
            last.then_inc(sem("ctx_pe"), 1)
            def project_u(g, k):
                b, p = k // PAIRS, k % PAIRS
                for h in range(2):
                    w = slice((2 * p + h) * 128, (2 * p + h) * 128 + 128)
                    last = mm3(UB[:, h * S:h * S + S], (Mh[:, w], Ml[:, w]), (xh[b][:, :], xl[b][:, :]))
                last.then_inc(sem("u_ready"), 1)

            def transposes(g, k):
                slot = (k - 2) % 4
                pe.wait_ge(sem("norm_done"), g + 1)
                pe.wait_ge(sem("pt_done"), g + 1)
                for h in range(2):
                    for j, c in enumerate((h * 128, 256 + h * 256, 384 + h * 256)):
                        last = pe.transpose(bank(4 + h)[:, j * 128:j * 128 + 128], P[:, slot, c:c + 128], ident[:, :])
                last.then_inc(sem("t_ready"), 1)

            def weighted_sums(g, k, turn=None):
                p, par = (k - 3) % PAIRS, (k - 3) % 2
                pe.wait_ge(sem("pt_done"), g + 1)
                if p == 0:
                    pe.wait_ge(sem("acc_free"), turn * 2 + k // PAIRS + 2)
                for h in range(2):
                    for dst, blk, half in ((0, 0, 0), (128, 1, 0), (128, 2, 1)):
                        first = p == 0 and h == 0 and dst == 0
                        last = pe.matmul(OB[:, dst:dst + 128], PT[:, par, h, blk * 128:blk * 128 + 128],
                                         VO[:, half, 2 * p + h, :], start=first, stop=(p == PAIRS - 1 and h == 1),
                                         skip_group_check=True)
                last.then_inc(sem("pv_done"), 1)

            pe.wait_ge(sem("fold_lo"), 8)
            pe.wait_ge(sem("consts"), 5)
            pe.wait_ge(sem("acc_free"), 1)
            with pe.Fori(0, B // 2) as i:
                for k in range(STEPS):
                    g = i * STEPS + k
                    b = k // PAIRS
                    if k % PAIRS == 0:
                        pe.wait_ge(sem("xl_done"), i * 2 + b + 1)
                        pe.wait_ge(sem("xh_done"), i * 2 + b + 1)
                    pe.wait_ge(sem("vo_done"), g + 1)
                    project_u(g, k)
                    transposes(g, k)
                    weighted_sums(g, k, i)
                    pe.wait_ge(sem("u_lo"), g + 1)
                    t, q4 = k % 2, k % 8 // 2
                    mm3(UB, (xh[b][:, t * 128:t * 128 + 128], xl[b][:, t * 128:t * 128 + 128]),
                        (NVh[:, q4 * CH:q4 * CH + CH], NVl[:, q4 * CH:q4 * CH + CH])).then_inc(sem("vo_ready"), 1)
                    par = k % 2
                    mm3(bank(2 * par, 256), (xh[b][:, 0:128], xl[b][:, 0:128]),
                        (Uh[:, :].rearrange("p (h c) -> p h c", h=2)[:, :, 0:128],
                         Ul[:, :].rearrange("p (h c) -> p h c", h=2)[:, :, 0:128]))
                    mm3(bank(2 * par + 1), (xh[b][:, 128:256], xl[b][:, 128:256]),
                        (Uh[:, :], Ul[:, :])).then_inc(sem("s_ready"), 1)
            for k in range(3):
                if k < 2:
                    transposes(B * PAIRS + k, k)
                weighted_sums(B * PAIRS + k, k)

            def project_query(c):
                cc = slice(c * CH, c * CH + CH)
                pe.wait_ge(sem("ln_lo"), c + 1)
                mm3(bank(4 + c), (wqh[:, :], wql[:, :]), (XTh[:, cc], XTl[:, cc])).then_inc(sem("q_ready"), 1)

            pe.wait_ge(sem("ctx_dve"), CTX_DVE["wq_lo"])
            in_turn(lambda c: ln_transpose(pe, 0, c), project_query, 2)
            for c in range(NC_):
                pe.wait_ge(sem("q_sq"), c + 1)
                pe.matmul(bank(c), blockones[:, :], SQ[:, c * CH:c * CH + CH], start=True, stop=True).then_inc(sem("q_norm"), 1)
            for c in range(NC_):
                pe.wait_ge(sem("q_done"), c + 1)
                for t in tiles(c):
                    dst = bank(4 + c)[:, t % 4 * 128:t % 4 * 128 + 128]
                    pe.matmul(dst, Q[:, t * 128:t * 128 + 128], G2[:, t // 2, :], start=True, stop=False)
                    last = pe.matmul(dst, ones[0:1, :], brow[0:1, 256:384], start=False, stop=True)
                last.then_inc(sem("b_out"), 1)

            def gate_logits(c):
                cc = slice(c * CH, c * CH + CH)
                pe.wait_ge(sem("ln_lo"), NC_ + c + 1)
                pe.wait_ge(sem("x_added"), c + 1)
                mm3(bank(4 + c), (wrh[:, :], wrl[:, :]), (XTh[:, cc], XTl[:, cc])).then_inc(sem("router_T"), 1)

            pe.wait_ge(sem("ctx_dve"), CTX_DVE["wr_split"])
            in_turn(lambda c: ln_transpose(pe, 1, c, XS, "xs_done"), gate_logits, 2)
            for t in range(T):
                pe.wait_ge(sem("router_out"), t // 4 + 1)
                last = pe.transpose(bank(0)[:, t * 16:t * 16 + 16], LT[:, t * 128:t * 128 + 128], ident[0:16, 0:16])
            last.then_inc(sem("logits_T"), 1)
            pe.wait_ge(sem("gates_split"), 1)
            for t in range(T):
                last = pe.transpose(bank(4 + t // 4)[:, t % 4 * 128:t % 4 * 128 + 128], GI[:, t, :].bitcast(F32), ident[:, :])
                if t % 4 == 3:
                    last.then_inc(sem("gates_T"), 1)
            def residual(done):
                for t in range(T):
                    pe.matmul(bank(t // 4)[:, t % 4 * 128:t % 4 * 128 + 128], X[:, t, :], ident[:, :],
                              start=t % 4 == 0, stop=True, skip_group_check=True)
            residual(None)
            pe.wait_ge(sem("gates_out"), NC_)

            def down(U, k):
                s, c, n = (k - 3) // 8 % 2, (k - 3) // 2 % 4, (k - 3) % 2
                w = slice(HID + n * 128, HID + n * 128 + 128)
                pe.wait_ge(sem("hl_done"), U + 1)
                return mm3(bank(c), (W0h[s][:, w], W0l[s][:, w]), (HH[:, (k - 3) % 4, :], HL[:, (k - 3) % 4, :]),
                           start=False, skip=True).then_inc(sem("down_done"), 1)

            pe.wait_ge(sem("c_zeros"), 4)
            pe.wait_ge(sem("sel2_done"), 1)
            with pe.Fori(0, E0 // 2) as i:
                for k in range(16):
                    s, c, n = k // 8, k // 2 % 4, k % 2
                    cc = slice(c * CH, c * CH + CH)
                    U = i * 16 + k
                    if k % 8 == 0:
                        pe.wait_ge(sem("w_sel"), i * 2 + s + 1)
                        pe.wait_ge(sem("w_split"), i * 2 + s + 3)
                    pe.wait_ge(sem("sg_done"), U + 1)
                    w = slice(n * 128, n * 128 + 128)
                    mm3(bank(6 + n), (W0h[s][:, w], W0l[s][:, w]), (XTh[:, cc], XTl[:, cc])).then_inc(sem("up_ready"), 1)
                    down(U, k)
                    if n == 0:
                        pe.matmul(bank(4 + c % 2), esel[s][:, :], SELT[:, cc], start=True, stop=True).then_inc(sem("gb_ready"), 1)
            for k in range(3):
                down(E0 * 8 + k, k)
            for t in range(T):
                pe.wait_ge(sem("experts_out"), t // 4 + 1)
                last = pe.transpose(bank(4 + t // 4)[:, t % 4 * 128:t % 4 * 128 + 128], OT[:, t * 128:t * 128 + 128], ident[:, :])
                if t % 4 == 3:
                    last.then_inc(sem("experts_T"), 1)
            for c in range(NC_):
                ln_transpose(pe, 2, c)
            pe.wait_ge(sem("l1_split"), 5)
            for t in range(T):
                p, tok = t % 2, slice(t * 128, t * 128 + 128)
                pe.wait_ge(sem("ln_lo"), 2 * NC_ + max(t // 4 + 1, 3 + p if t < 2 else 0))
                for n, (b0, what, free) in enumerate(((4, "dq_ready", "qs_done"), (2, "dk_ready", "pr_done"),
                                                      (6, "dz_ready", "z_pos"))):
                    if t >= 2:
                        pe.wait_ge(sem(free), t - 1)
                    w = slice(n * CH, n * CH + CH)
                    if n == 2:
                        pe.matmul(bank(b0 + p), onesr[:, :], abr[:, :], start=True, stop=False)
                    mm3(bank(b0 + p), (XTh[:, tok], XTl[:, tok]), (wdh[:, w], wdl[:, w]), start=n < 2).then_inc(sem(what), 1)
                if t % 4 == 3:
                    c = t // 4
                    cc = slice(c * CH, c * CH + CH)
                    w = slice(3 * CH, 3 * CH + 128)
                    if c >= 2:
                        pe.wait_ge(sem("vp_done"), 2 * c - 2)
                    mm3(bank(c % 2), (wdh[:, w], wdl[:, w]), (XTh[:, cc], XTl[:, cc])).then_inc(sem("dv_ready"), 1)
            pe.wait_ge(sem("pr_done"), T)
            pe.wait_ge(sem("z_pos"), T)
            pe.wait_ge(sem("l1_in"), 16 * 7)
            pe.matmul(bank(4), wqe[:, 0, :], ctxT[:, :], start=True, stop=True).then_inc(sem("ctx_pe"), 1)
            for b in range(B):
                last = pe.matmul(bank(5 + b // 4)[0:64, b % 4 * 128:b % 4 * 128 + 128], ctxT[:, b * SC:b * SC + SC], wqe[:, 0, :],
                                 start=True, stop=True)
            last.then_inc(sem("ctx_pe"), 1)
            pe.wait_ge(sem("ctx_act"), CTX_ACT["ke_done"])
            pe.matmul(bank(7), wqe[:, 1, :], kTe[:, :], start=True, stop=True).then_inc(sem("ctx_pe"), 1)

            for n in (1, 0):
                pe.wait_ge(sem("ab_placed"), 4 - 2 * n)
                for r in range(2):
                    last = pe.transpose(bank(2)[0:64, n * S + r * 128:n * S + r * 128 + 128],
                                        ABt[:, r, n, :, :].rearrange("p h b -> p (h b)"), ident[:, :])
            last.then_inc(sem("ab_T"), 1)

            def product(g, col, src, w, done, first=False):
                for t in range(2):
                    dst = PS[:, ds(g * S + col + t * 128, 128)] if not isinstance(g, int) else PS[:, g * S + col + t * 128:g * S + col + t * 128 + 128]
                    for h in range(H1):
                        last = pe.matmul(dst, src[:, h * S + t * 128:h * S + t * 128 + 128], w[:, :],
                                         start=first and t == 0 and h == 0, stop=h == H1 - 1, skip_group_check=True)
                last.then_inc(sem(done), 1)

            def states_product(g, par):
                pe.wait_ge(sem("scan1_done"), g + 1)
                product(g, 3 * CH + S, r0b[1 - par], wo1, "y0_done", first=par == 1)

            def floors_product(g, par):
                pe.wait_ge(sem("scan2_done"), g + 1)
                product(g, 3 * CH, rb[par], wo1e, "y1_done")

            pe.wait_ge(sem("wu_done"), 1)
            pe.wait_ge(sem("vp_done"), 2 * NC_)
            pe.wait_ge(sem("ab_in"), 1)
            with pe.Fori(0, B // 2) as i:
                for k in range(2):
                    g = i * 2 + k
                    pe.wait_ge(sem("dsel_done"), g + 1)
                    for r in range(4):
                        pe.wait_ge(sem("w_copied"), g * 4 + r + 1)
                        for h in range(2):
                            last = pe.matmul(bank(r % 2)[:, h * S:h * S + S], dsel[k][:, 2 * r + h, :], WUr[:, 0, :], start=True, stop=True)
                        last.then_inc(sem("w_bc"), 1)
                        pe.wait_ge(sem("qr_done"), g * 4 + r + 1)
                        for h in range(2):
                            last = pe.matmul(bank(2)[:, h * S:h * S + S], dsel[k][:, 2 * r + h, :], WUr[:, 1, :], start=True, stop=True)
                        last.then_inc(sem("u_bc"), 1)
                    states_product(g, k)
                    floors_product(g, k)
            states_product(B, 0)
            floors_product(B, 0)
            floors_product(B + 1, 1)
            def context_scores(c):
                pe.wait_ge(sem("ln_hi"), 3 * NC_ + c + 1)
                for t in tiles(c):
                    b = t // 2
                    last = pe.matmul(bank(4 + t // 8)[:, t % 8 * SC:t % 8 * SC + SC], XTf[:, t * 128:t * 128 + 128],
                                     KK[:, b * SC:b * SC + SC], start=True, stop=True)
                last.then_inc(sem("es_ready"), 1)

            pe.wait_ge(sem("ctx_act"), CTX_ACT["kk_done"])
            pe.wait_ge(sem("x_added"), NC_ + 1)
            in_turn(lambda c: ln_transpose(pe, 3, c), context_scores, 1)
            for t in range(T):
                pe.wait_ge(sem("e_prob"), t // 8 + 1)
                last = pe.transpose(bank(t // 4)[0:64, t % 4 * 128:t % 4 * 128 + 128], SE[:, t, :], ident[:, :])
                if t % 4 == 3:
                    last.then_inc(sem("e_T"), 1)
            for t in range(T):
                pe.wait_ge(sem("e_pt"), t // 4 + 1)
                last = pe.matmul(bank(4 + t // 4)[:, t % 4 * 128:t % 4 * 128 + 128], PE_T[:, t * 128:t * 128 + 128], vE[:, t // 2, :],
                                 start=True, stop=True)
                if t % 4 == 3:
                    last.then_inc(sem("e_out"), 1)
            def router_logits(c):
                cc = slice(c * CH, c * CH + CH)
                pe.wait_ge(sem("ln_lo"), 3 * NC_ + c + 1)
                mm3(bank(4 + c), (wr1h[:, :], wr1l[:, :]), (XTh[:, cc], XTl[:, cc])).then_inc(sem("router_T"), 1)

            def logits_by_token(h):
                pe.wait_ge(sem("router_out"), NC_ + 2 * h + 2)
                for t in range(8 * h, 8 * h + 8):
                    last = pe.transpose(bank(4 + h)[:, t % 8 * E1:t % 8 * E1 + E1], FL[:, t * 128:t * 128 + 128], ident[0:64, 0:64])
                last.then_inc(sem("logits_T"), 1)

            def router_step(c):
                router_logits(c)
                if c % 2:
                    logits_by_token(c // 2)

            in_turn(lambda c: ln_transpose(pe, 4, c), router_step, 2)
            residual(None)
            def shared_down(c):
                pe.wait_ge(sem("sh_hl"), c + 1)
                mm3(bank(c), (wshh[:, 256:384], wshl[:, 256:384]), (FHH[:, c % 2, :], FHL[:, c % 2, :]),
                    start=False, skip=True).then_inc(sem("sh_down"), 1)

            for c in range(NC_):
                cc = slice(c * CH, c * CH + CH)
                if c:
                    pe.wait_ge(sem("sh_sg"), c)
                mm3(bank(6), (wshh[:, 0:128], wshl[:, 0:128]), (XTh[:, cc], XTl[:, cc])).then_inc(sem("sh_g"), 1)
                if c:
                    pe.wait_ge(sem("sh_h"), c)
                mm3(bank(7), (wshh[:, 128:256], wshl[:, 128:256]), (XTh[:, cc], XTl[:, cc])).then_inc(sem("sh_u"), 1)
                if c:
                    shared_down(c - 1)
            shared_down(NC_ - 1)
            pe.wait_ge(sem("sh_h"), NC_)
            for t in range(T):
                pe.wait_ge(sem("gates_split"), 2 + t // 8)
                last = pe.transpose(bank(4 + t // 4)[:, t % 4 * 128:t % 4 * 128 + 128], GI1[:, t, :].bitcast(F32), ident[:, :])
                if t % 4 == 3:
                    last.then_inc(sem("gates_T"), 1)
            pe.wait_ge(sem("gates_out"), NC_ + NC_)

            def f_down(U, k):
                s, c = (k - 2) // 4 % 2, (k - 2) % 4
                pe.wait_ge(sem("fhl_done"), U + 1)
                mm3(bank(c), (W3h[s][:, 256:384], W3l[s][:, 256:384]), (FHH[:, (k - 2) % 4, :], FHL[:, (k - 2) % 4, :]),
                    start=False, skip=True).then_inc(sem("fdown_done"), 1)

            with pe.Fori(0, E1 // 4) as i:
                for k in range(8):
                    s, c = k // 4, k % 4
                    cc = slice(c * CH, c * CH + CH)
                    U = i * 8 + k
                    if c == 0:
                        pe.wait_ge(sem("f_sel"), i * 2 + s + 1)
                        pe.wait_ge(sem("f_split"), i * 2 + s + 3)
                    pe.wait_ge(sem("fg_done"), U + 1)
                    mm3(bank(4 + k % 2), (W3h[s][:, 0:128], W3l[s][:, 0:128]), (XTh[:, cc], XTl[:, cc])).then_inc(sem("g_ready"), 1)
                    pe.wait_ge(sem("ft_done"), U + 2)
                    mm3(bank(6), (W3h[s][:, 128:256], W3l[s][:, 128:256]), (XTh[:, cc], XTl[:, cc])).then_inc(sem("fu_ready"), 1)
                    f_down(U, k)
                    pe.wait_ge(sem("fh_done"), U + 1)
                    pe.matmul(bank(7), fsel[s][:, :, :].rearrange("p e i -> p (e i)"), SELT1[:, cc], start=True, stop=True).then_inc(sem("fgb_ready"), 1)
            for k in range(2):
                f_down(E1 * 2 + k, k)
            for t in range(T):
                pe.wait_ge(sem("experts_out"), NC_ + t // 4 + 1)
                last = pe.transpose(bank(4 + t // 4)[:, t % 4 * 128:t % 4 * 128 + 128], OT1[:, t * 128:t * 128 + 128], ident[:, :])
                if t % 4 == 3:
                    last.then_inc(sem("experts_T"), 1)


def host_layout(v):
    f = np.ascontiguousarray
    x, c = v["x"].reshape(N, D), v["ctx_1024"].reshape(B * SC, D)
    tiles = lambda m: m.reshape(-1, 128, m.shape[-1]).transpose(1, 0, 2)
    lay = lambda *m: np.stack(m, axis=1)
    both = lambda n: np.concatenate([v["L0_ffn_" + n], v["L0_ffn_" + n + "_s"]])
    return {k: f(m) for k, m in {
        "x": tiles(x), "xT": x.T, "ctxT": c.T,
        "w64q": v["L0_attn_W_Q"].transpose(1, 0, 2), "w64k": v["L0_attn_W_K"].transpose(1, 0, 2),
        "w64v": v["L0_attn_W_V"].transpose(1, 0, 2), "w64o": v["L0_attn_W_O"].transpose(2, 0, 1),
        "wx": lay(*(v["L0_xattn_W" + n].T for n in "kvoq")),
        "brow": np.concatenate([v["L0_xattn_b" + n] for n in "kvo"])[None],
        "bq": v["L0_xattn_bq"][:, None],
        "wr0": v["L0_ffn_router_w"], "rw": both("rms_w").T,
        "w12": np.concatenate([both("w1"), both("w2").reshape(E0, 2, 128, D).transpose(0, 2, 1, 3).reshape(E0, 128, HID)], axis=2),
        "wd": np.concatenate([v["L1_attn_W_" + n].T for n in ("q", "k", "alpha_w", "v")], axis=1),
        "abias": v["L1_attn_W_alpha_b"][None], "wo1": v["L1_attn_W_o"].T,
        "wqe": lay(v["L1_xattn_Wq"].T, v["L1_xattn_Wq"]),
        "wr1": v["L1_ffn_router_w"].T, "ebias": np.broadcast_to(v["L1_ffn_e_bias"][None], (128, E1)),
        "wsh": np.concatenate([v["L1_ffn_S" + n] for n in ("Wg", "Wu", "Wd")], axis=1),
        "w3": np.concatenate([v["L1_ffn_" + n].reshape(E1 // 2, 2, D, I1).transpose(0, 2, 1, 3).reshape(E1 // 2, D, 128)
                              for n in ("Wg", "Wu")] + [v["L1_ffn_Wd"].reshape(E1 // 2, 128, D)], axis=2),
    }.items()}


def kernel(**inputs):
    import concourse.bacc as bacc
    from concourse.bass_utils import run_bass_kernel_spmd

    nc = bacc.Bacc("TRN2", target_bir_lowering=False, num_devices=1)
    arrays = host_layout({k: np.asarray(v) for k, v in inputs.items()})
    drams = {k: nc.dram_tensor("in_" + k, m.shape, mybir.dt.from_np(m.dtype), kind="ExternalInput").ap()
             for k, m in arrays.items()}
    out = nc.dram_tensor("out", (128, T, D), F32, kind="ExternalOutput").ap()
    decoder_program(nc, drams, out)
    got = run_bass_kernel_spmd(nc, [{"in_" + k: m for k, m in arrays.items()}], core_ids=[0])
    return got.results[0]["out"].transpose(1, 0, 2).reshape(B, S, D)
```

```python
import math
from contextlib import ExitStack

import numpy as np
import concourse.bass as bass
from concourse import mybir
from concourse.alu_op_type import AluOpType as ALU

ACT = mybir.ActivationFunctionType
AX = mybir.AxisListType
F32 = mybir.dt.float32
F32R = mybir.dt.float32r
ds = bass.ds

B, S, D = 8, 256, 128
N = B * S
T = N // 128
SC = 64
CH = 512
NC_ = N // CH
H0, DH = 16, 64
PAIRS = H0 // 2
HX, DX = 16, 8
E0, E0R, HID = 16, 14, 256
H1 = 8
E1, I1 = 64, 64
LN_EPS, RMS_EPS, EPS = 1e-5, 1.1920929e-07, 1e-8
BIG = 1e30


def decoder_program(nc, a, out):
    CTX_PE = {"ck_ready": 1, "cv_ready": 2, "kn_ready": 3, "gt_ready": 4, "g2_ready": 5,
              "ke_ready": 6, "ve_ready": 7, "kk_ready": 8}
    CTX_ACT = {"ck_exp": 1, "cv_done": 2, "wq_hi": 3, "g2_done": 11, "ke_done": 12, "ve_done": 13, "kk_done": 14}
    CTX_DVE = {"ck_neg": 1, "ck_done": 2, "kn_sum": 3, "gbt_done": 4, "wq_lo": 5, "wr_split": 7}
    CTX_POOL = {"ck_sq": 1, "kn_done": 2}
    ctx = ExitStack()
    sems = {}

    def sem(name):
        if name not in sems:
            sems[name] = ctx.enter_context(nc.semaphore(name))
        return sems[name]

    def sb(name, shape, dt=F32, scope=ctx):
        return scope.enter_context(nc.sbuf_tensor(name, shape, dt))

    with ctx:
        PS = ctx.enter_context(nc.psum_tensor("PS", [128, 8 * CH], F32))

        def bank(n, w=CH, k=1):
            return PS[:, n * CH:n * CH + (k - 1) * CH + w]

        Xp = sb("Xp", [128, (B + 1) * S])
        X = Xp[:, S:].rearrange("p (t d) -> p t d", d=D)
        XTh = sb("XTh", [128, N], F32R)
        XTl = sb("XTl", [128, N], F32R)
        ident = sb("ident", [128, 128])
        blockones = sb("blockones", [128, 128])
        sel2 = sb("sel2", [128, 72], F32R)
        cmask = sb("cmask", [128, 2 * 128])
        ones = sb("ones", [128, 128])
        scratch = sb("scratch", [128, 24])
        st = sb("st", [128, T, 6])
        mv = sb("mv", [128, T, 2])
        rs = sb("rs", [128, T])
        nm = sb("nm", [128, T])
        nb = sb("nb", [128, T])
        rs2 = sb("rs2", [128, T])
        ms = sb("ms", [128, T])
        neghalf = sb("neghalf", [128, T])
        ctxT = sb("ctxT", [128, B * SC])

        halfones = sb("halfones", [128, 2])
        wx = sb("wx", [128, 4, 128])
        bq = sb("bq", [128, 1])
        brow = sb("brow", [1, 3 * 128])
        G2 = sb("G2", [128, B, 128])
        wqh = sb("wqh", [128, 128], F32R)
        wql = sb("wql", [128, 128], F32R)
        wrh = sb("wrh", [128, 128], F32R)
        wrl = sb("wrl", [128, 128], F32R)
        wr_in = sb("wr_in", [128, E0R])

        wd_in = sb("wd_in", [128, 3 * CH + 128])
        wdh = sb("wdh", [128, 3 * CH + 128], F32R)
        wdl = sb("wdl", [128, 3 * CH + 128], F32R)
        abias = sb("abias", [1, CH])
        abr = sb("abr", [33, CH], F32R)
        onesr = sb("onesr", [33, 128], F32R)
        wo1 = sb("wo1", [128, 128])
        wqe = sb("wqe", [128, 2, 128])
        KK = sb("KK", [128, B * SC])
        vE = sb("vE", [64, B, 128])
        wr1_in = sb("wr1_in", [128, E1])
        wr1h = sb("wr1h", [128, 128], F32R)
        wr1l = sb("wr1l", [128, 128], F32R)
        ebias = sb("ebias", [128, E1])
        wsh = sb("wsh", [128, 384])
        wshh = sb("wshh", [128, 384], F32R)
        wshl = sb("wshl", [128, 384], F32R)
        tiny = sb("tiny", [128, 1])
        zero = sb("zero", [128, 1])
        wo1e = sb("wo1e", [128, 128])

        sa = ExitStack()
        Mh = sb("Mh", [128, H0 * 128], F32R, sa)
        Ml = sb("Ml", [128, H0 * 128], F32R, sa)
        NVh = sb("NVh", [128, H0 * 128], F32R, sa)
        NVl = sb("NVl", [128, H0 * 128], F32R, sa)
        xall = sb("xall", [128, (B + 1) * S], F32, sa)
        xh = [sb(f"xh{k}", [128, S], F32R, sa) for k in range(2)]
        xl = [sb(f"xl{k}", [128, S], F32R, sa) for k in range(2)]
        VO = sb("VO", [128, 2, H0, 128], F32, sa)
        P = sb("P", [128, 4, 768], F32, sa)
        PT = sb("PT", [128, 2, 2, 384], F32, sa)
        Uh = sb("Uh", [128, CH], F32R, sa)
        Ul = sb("Ul", [128, CH], F32R, sa)
        mn = sb("mn", [128, 2, 4], F32, sa)
        ls = sb("ls", [128, 2, 4], F32, sa)
        rl = sb("rl", [128, 2, 4], F32, sa)
        wraw = ExitStack()
        w64 = {n: sb("w64" + n, [64, H0, 128], F32, wraw) for n in "qkvo"}
        cx = ExitStack()
        ce = sb("ce", [128, 4, 128], F32, cx)
        ck = sb("ck", [128, 4, 128], F32, cx)
        cv = sb("cv", [128, 4, 128], F32, cx)
        csq = sb("csq", [128, 4, 128], F32, cx)
        GBT = sb("GBT", [128, B, 128], F32, cx)
        kn = sb("kn", [128, B], F32, cx)
        cx.close()
        wraw.close()
        sa.close()

        sbs = ExitStack()
        EQ = sb("EQ", [128, N], F32, sbs)
        RQ = sb("RQ", [128, N], F32, sbs)
        Q = sb("Q", [128, N], F32, sbs)
        SQ = sb("SQ", [128, N], F32, sbs)
        sbs.close()

        sc = ExitStack()
        XS = sb("XS", [128, T, 128], F32, sc)
        LT = sb("LT", [16, N], F32, sc)
        Lg = sb("Lg", [128, T, E0R], F32, sc)
        lm = sb("lm", [128, T], F32, sc)
        lz = sb("lz", [128, T], F32, sc)
        G20 = sb("G20", [128, T, 20], F32, sc)
        M8 = sb("M8", [128, T, 8], F32, sc)
        RPL = sb("RPL", [128, T, 8], F32, sc)
        RP = sb("RP", [128, T, 20], F32, sc)
        GI = sb("GI", [128, T, 128], F32R, sc)
        SELT = sb("SELT", [128, N], F32R, sc)
        rw = sb("rw", [128, E0], F32, sc)
        W0 = [sb(f"W0_{k}", [128, 2 * HID], F32, sc) for k in range(2)]
        W0h = [sb(f"W0h{k}", [128, 2 * HID], F32R, sc) for k in range(2)]
        W0l = [sb(f"W0l{k}", [128, 2 * HID], F32R, sc) for k in range(2)]
        esel = [sb(f"esel{k}", [128, 128], F32R, sc) for k in range(2)]
        SG = sb("SG", [128, 2, CH], F32, sc)
        Hf = sb("Hf", [128, 4, CH], F32, sc)
        HH = sb("HH", [128, 4, CH], F32R, sc)
        HL = sb("HL", [128, 4, CH], F32R, sc)
        OT = sb("OT", [128, N], F32, sc)
        sc.close()

        sd = ExitStack()
        VP = sb("VP", [128, N], F32, sd)
        AB64 = sb("AB64", [64, 2, S], F32, sd)
        mb = sb("mb", [64, S + 1], F32, sd)
        db = sb("db", [64, S + 1], F32, sd)
        ea = sb("ea", [64, S], F32, sd)
        eb = sb("eb", [64, S], F32, sd)
        rd = sb("rd", [64, S], F32, sd)
        wu = sb("wu", [64, 2, S], F32, sd)
        WUr = sb("WUr", [128, 2, S], F32R, sd)
        dsel = [sb(f"dsel{k}", [128, H1, 128], F32R, sd) for k in range(2)]
        kTe = sb("kTe", [128, B * SC], F32, sd)
        sd1 = ExitStack()
        QS = sb("QS", [128, 2, CH], F32, sd1)
        PR = sb("PR", [128, 2, CH], F32, sd1)
        ZA = sb("ZA", [128, T, CH], F32, sd1)
        ZR = sb("ZR", [128, T, CH], F32, sd1)
        ABs = sb("ABs", [128, 2, T, H1], F32, sd1)
        ABt = sb("ABt", [128, 2, 2, H1, B], F32, sd1)
        VS = sb("VS", [128, N], F32, sd1)
        sd1.close()
        R = H1 * S
        Wb = [sb(f"Wb{k}", [128, R], F32, sd) for k in range(2)]
        qb = sb("qb", [128, R], F32, sd)
        r0b = [sb(f"r0b{k}", [128, R], F32, sd) for k in range(2)]
        OD = qb
        dfb = [sb(f"dfb{k}", [128, R], F32, sd) for k in range(2)]
        sgb = sb("sgb", [128, R], F32, sd)
        gb = [sb(f"gb{k}", [128, R], F32, sd) for k in range(2)]
        rb = [sb(f"rb{k}", [128, R], F32, sd) for k in range(2)]
        sd.close()

        se = ExitStack()
        XTf = sb("XTf", [128, N], F32, se)
        SE = sb("SE", [128, T, SC], F32, se)
        PE_T = sb("PE_T", [64, N], F32, se)
        em = sb("em", [128, T], F32, se)
        el = sb("el", [128, T], F32, se)
        se.close()

        sf = ExitStack()
        FL = sb("FL", [64, N], F32, sf)
        SCo = sb("SCo", [128, T, E1], F32, sf)
        SF = sb("SF", [128, T, E1], F32, sf)
        h1 = sb("h1", [128, T * 8, 4], F32, sf)
        l1 = sb("l1", [128, T * 8, 4], F32, sf)
        h2 = sb("h2", [128, T * 8, 2], F32, sf)
        l2 = sb("l2", [128, T * 8, 2], F32, sf)
        t2 = sb("t2", [128, T * 8, 2], F32, sf)
        h3 = sb("h3", [128, T * 8, 1], F32, sf)
        l3 = sb("l3", [128, T * 8, 1], F32, sf)
        t3 = sb("t3", [128, T * 8, 1], F32, sf)
        GS = sb("GS", [128, T, 12], F32, sf)
        F8 = sb("F8", [128, T, 8], F32, sf)
        FR = sb("FR", [128, T, 8], F32, sf)
        GR = sb("GR", [128, T, 12], F32, sf)
        gm = sb("gm", [128, T, 8], F32, sf)
        FM = sb("FM", [128, T, E1], F32, sf)
        FRP = sb("FRP", [128, T, E1], F32, sf)
        fs = sb("fs", [128, T], F32, sf)
        fi = sb("fi", [128, T], F32, sf)
        GI1 = sb("GI1", [128, T, 128], F32R, sf)
        SELT1 = sb("SELT1", [128, N], F32R, sf)
        W3 = [sb(f"W3_{k}", [128, 384], F32, sf) for k in range(2)]
        W3h = [sb(f"W3h{k}", [128, 384], F32R, sf) for k in range(2)]
        W3l = [sb(f"W3l{k}", [128, 384], F32R, sf) for k in range(2)]
        fsel = [sb(f"fsel{k}", [128, 2, 64], F32R, sf) for k in range(2)]
        FG = sb("FG", [128, 2, CH], F32, sf)
        FU = sb("FU", [128, 2, CH], F32, sf)
        SG8 = sb("SG8", [128, 8, CH], F32, sf)
        U4 = sb("U4", [128, 4, CH], F32, sf)
        FH = sb("FH", [128, 4, CH], F32, sf)
        FHH = sb("FHH", [128, 4, CH], F32R, sf)
        FHL = sb("FHL", [128, 4, CH], F32R, sf)
        OT1 = sb("OT1", [128, N], F32, sf)
        sf.close()
        NEG = -3e38
        EARLY = ((0, 1, 2, 3), (4, 5), (6, 7), ())
        F_STEPS, F_RECIP, F_GROUPS = 40, 2, 23
        SP_GROUPS = ((0, 8), (8, 12), (12, 16))

        block = ctx.enter_context(nc.Block())

        def piece(q):
            r, h = q // 2, q % 2
            return (h * 128, 128) if r == 0 else (256 + h * 256, 256)

        def scores(par, q):
            r, h = q // 2, q % 2
            c = (2 * par + r) * CH + h * (128 if r == 0 else 256)
            return PS[:, c:c + (128 if r == 0 else 256)]

        PTP = bank(4, CH, 2).rearrange("p (a c) -> p a c", a=2)[:, :, 0:384]
        UB, OB = bank(6), bank(7)

        def fold_bank(n):
            return bank(4 + n % 4)

        def cols(start, n):
            return slice(start, start + n) if isinstance(start, int) else ds(start, n)

        def sum_bank(t):
            return bank(4 + t // 4)[:, t % 4 * 128:t % 4 * 128 + 128]

        GATES_EXP, GATES_PLACED = 1, (10, 11, 12, 13)
        GATE_STEPS = 17
        STEPS = 2 * PAIRS

        def tiles(c):
            return range(4 * c, 4 * c + 4)

        def ln_stats(dve, n, c, src=None):
            for t in tiles(c):
                dve.bn_stats(st[:, t, :], src(t) if src else X[:, t, :]).then_inc(sem("ln_st"), 1)
            for t in tiles(c):
                dve.wait_ge(sem("ln_st"), T * n + t + 1)
                last = dve.bn_aggr(mv[:, t, :], st[:, t, :])
            last.then_inc(sem("ln_mv"), 1)

        def ln_factors(pool, n, c):
            cc, k = slice(4 * c, 4 * c + 4), NC_ * n + c + 1
            pool.wait_ge(sem("ln_mv"), k)
            pool.tensor_scalar(ms[:, cc], mv[:, cc, 1], LN_EPS, None, ALU.add).then_inc(sem("ln_ms"), 1)
            pool.tensor_scalar(nm[:, cc], mv[:, cc, 0], -1.0, None, ALU.mult).then_inc(sem("ln_ms"), 1)
            pool.wait_ge(sem("ln_ms"), 2 * k)
            pool.tensor_tensor(rs[:, cc], ms[:, cc], neghalf[:, cc], ALU.pow).then_inc(sem("ln_rs"), 1)
            pool.wait_ge(sem("ln_rs"), k)
            pool.tensor_tensor(nb[:, cc], nm[:, cc], rs[:, cc], ALU.mult).then_inc(sem("ln_nb"), 1)

        def ln_norm(act, n, c, src=None):
            act.wait_ge(sem("ln_nb"), NC_ * n + c + 1)
            for t in tiles(c):
                act.activation(X[:, t, :], src(t) if src else X[:, t, :], ACT.Identity, scale=rs[:, t:t + 1],
                               bias=nb[:, t:t + 1]).then_inc(sem("ln_x"), 1)

        def ln_transpose(pe, n, c, src=None, ready=None):
            for t in tiles(c):
                pe.wait_ge(sem(ready or "ln_x"), t + 1 if ready else T * n + t + 1)
                last = pe.transpose(bank(c)[:, t % 4 * 128:t % 4 * 128 + 128], (src or X)[:, t, :], ident[:, :])
            last.then_inc(sem("ln_T"), 1)

        def ln_hi(act, n, c):
            act.wait_ge(sem("ln_T"), NC_ * n + c + 1)
            act.activation(XTh[:, c * CH:c * CH + CH], bank(c), ACT.Copy).then_inc(sem("ln_hi"), 1)

        def ln_lo(dve, n, c):
            dve.wait_ge(sem("ln_hi"), NC_ * n + c + 1)
            dve.tensor_tensor(XTl[:, c * CH:c * CH + CH], bank(c), XTh[:, c * CH:c * CH + CH].bitcast(F32),
                              ALU.subtract).then_inc(sem("ln_lo"), 1)

        def in_turn(first, second, behind):
            for c in range(NC_ + behind):
                if c < NC_:
                    first(c)
                if c >= behind:
                    second(c - behind)

        @block.sync
        def _(sp):
            sp.dma_start(ctxT[:, :], a["ctxT"]).then_inc(sem("ctx_in"), 16)
            sp.dma_start(wx[:, :, :], a["wx"]).then_inc(sem("ctx_in"), 16)
            sp.dma_start(brow[:, :], a["brow"]).then_inc(sem("ctx_in"), 16)
            sp.dma_start(bq[:, :], a["bq"]).then_inc(sem("ctx_in"), 16)
            for n in "voqk":
                sp.dma_start(w64[n][:, :, :], a["w64" + n]).then_inc(sem("w_vo_in" if n in "vo" else "w_qk_in"), 16)
            sp.dma_start(xall[:, 0:N], a["xT"]).then_inc(sem("xT_in"), 16)
            sp.dma_start(X, a["x"]).then_inc(sem("x_in"), 16)
            sp.dma_start(wr_in[:, :], a["wr0"]).then_inc(sem("wr_in"), 16)
            for name, dst in (("wd", wd_in), ("abias", abias), ("wo1", wo1), ("wqe", wqe), ("wr1", wr1_in),
                              ("ebias", ebias), ("wsh", wsh)):
                sp.dma_start(dst[tuple([slice(None)] * len(dst.shape))], a[name]).then_inc(sem("l1_in"), 16)
            sp.wait_ge(sem("x_added"), NC_)
            sp.dma_start(rw[:, :], a["rw"]).then_inc(sem("rw_in"), 16)
            with sp.Fori(0, E0 // 2) as i:
                for s in range(2):
                    sp.wait_ge(sem("w_split"), i * 2 + s + 2)
                    sp.dma_start(W0[s][:, :], a["w12"][ds(i * 2 + s, 1), :, :].rearrange("o p n -> p (o n)")).then_inc(sem(f"w_in{s}"), 16)
            sp.wait_ge(sem("x_added"), NC_ + NC_)
            with sp.Fori(0, E1 // 4) as i:
                for s in range(2):
                    sp.wait_ge(sem("f_split"), i * 2 + s + 1)
                    sp.dma_start(W3[s][:, :], a["w3"][ds(i * 2 + s, 1), :, :].rearrange("o p n -> p (o n)")).then_inc(sem(f"w_in{s}"), 16)
            for c in range(NC_):
                sp.wait_ge(sem("ln_x"), 5 * T + 4 * c + 4)
                sp.dma_start(out[:, 4 * c:4 * c + 4, :], X[:, 4 * c:4 * c + 4, :]).then_inc(sem("out_done"), 16)
            sp.wait_ge(sem("out_done"), 16 * NC_)

        @block.gpsimd
        def _(pool):
            pool.memset(ident[:, :], 0.0).then_inc(sem("zeroed"), 1)
            pool.memset(blockones[:, :], 1.0).then_inc(sem("zeroed"), 1)
            pool.memset(cmask[:, :], 0.0).then_inc(sem("zeroed"), 1)
            pool.memset(ones[:, :], 1.0).then_inc(sem("consts"), 1)
            pool.memset(neghalf[:, :], -0.5).then_inc(sem("consts"), 1)
            pool.memset(wrh[:, :].bitcast(F32), 0.0).then_inc(sem("wr_zero"), 1)
            pool.memset(wrl[:, :].bitcast(F32), 0.0).then_inc(sem("wr_zero"), 1)
            pool.wait_ge(sem("zeroed"), 3)
            pool.affine_select(out=ident[:, :], in_=ident[:, :], compare_op=ALU.not_equal, fill=1.0,
                               base=0, pattern=[[-1, 128]], channel_multiplier=1).then_inc(sem("consts"), 1)
            pool.affine_select(out=cmask[:, 128:256], in_=cmask[:, 128:256], compare_op=ALU.is_ge, fill=BIG,
                               base=0, pattern=[[-1, 128]], channel_multiplier=1).then_inc(sem("consts"), 1)
            pool.affine_select(out=blockones[:, :], in_=blockones[:, :], compare_op=ALU.is_ge, fill=0.0,
                               base=0, pattern=[[-DX, HX], [0, DX]], channel_multiplier=1).then_inc(sem("zeroed"), 1)
            pool.wait_ge(sem("zeroed"), 4)
            pool.affine_select(out=blockones[:, :], in_=blockones[:, :], compare_op=ALU.is_ge, fill=0.0,
                               base=DX - 1, pattern=[[DX, HX], [0, DX]], channel_multiplier=-1).then_inc(sem("consts"), 1)
            pool.memset(xall[:, N:], 0.0).then_inc(sem("x_pad"), 1)
            pool.memset(P[:, 2, :], 0.0).then_inc(sem("norm_done"), 1)
            pool.memset(PT[:, 1, :, :], 0.0).then_inc(sem("pt_done"), 1)
            pool.memset(VO[:, :, :, :], 0.0).then_inc(sem("vo_done"), 1)

            pool.wait_ge(sem("ctx_dve"), CTX_DVE["ck_done"])
            pool.tensor_tensor(csq[:, :, :], ck[:, :, :], ck[:, :, :], ALU.mult).then_inc(sem("ctx_pool"), 1)
            pool.wait_ge(sem("ctx_dve"), CTX_DVE["kn_sum"])
            pool.tensor_tensor(kn[:, :], kn[:, :], neghalf[:, 0:B], ALU.pow).then_inc(sem("ctx_pool"), 1)

            def divide(g, k):
                slot, par = (k - 1) % 4, (k - 1) % 2
                pool.wait_ge(sem("rl_done"), g + 1)
                for r, w in ((0, 128), (1, 256)):
                    v = P[:, slot, 256 * r:256 * r + 2 * w].rearrange("p (h c) -> p h c", h=2)
                    f = rl[:, par, 2 * r:2 * r + 2].rearrange("p (h o) -> p h o", o=1).to_broadcast([128, 2, w])
                    last = pool.tensor_tensor(v, v, f, ALU.mult)
                last.then_inc(sem("norm_done"), 1)

            with pool.Fori(0, B // 2) as i:
                for k in range(STEPS):
                    divide(i * STEPS + k, k)
            divide(B * PAIRS, 0)
            for c in range(NC_):
                ln_factors(pool, 0, c)

            for c in range(NC_):
                cc = slice(c * CH, c * CH + CH)
                pool.wait_ge(sem("q_elu"), c + 1)
                pool.tensor_tensor(SQ[:, cc], Q[:, cc], Q[:, cc], ALU.mult).then_inc(sem("q_sq"), 1)
            for c in range(NC_):
                cc = slice(4 * c, 4 * c + 4)
                ln_factors(pool, 1, c)
                pool.tensor_tensor(ms[:, cc], mv[:, cc, 1], rs[:, cc], ALU.mult).then_inc(sem("rms"), 1)
                pool.wait_ge(sem("rms"), 4 * c + 1)
                pool.tensor_tensor(ms[:, cc], ms[:, cc], rs[:, cc], ALU.mult).then_inc(sem("rms"), 1)
                pool.wait_ge(sem("rms"), 4 * c + 2)
                pool.tensor_scalar(ms[:, cc], ms[:, cc], RMS_EPS, None, ALU.add).then_inc(sem("rms"), 1)
                pool.wait_ge(sem("rms"), 4 * c + 3)
                pool.tensor_tensor(rs2[:, cc], ms[:, cc], neghalf[:, cc], ALU.pow).then_inc(sem("rms"), 1)
            pool.memset(scratch[:, 11:12], 0.0).then_inc(sem("w_split"), 2)
            pool.memset(scratch[:, 12:13], 0.0).then_inc(sem("sg_done"), 2)
            pool.memset(scratch[:, 13:14], 0.0).then_inc(sem("h_done"), 2)
            pool.memset(scratch[:, 14:15], 0.0).then_inc(sem("hh_done"), 1)
            pool.memset(scratch[:, 15:16], 0.0).then_inc(sem("hl_done"), 3)
            pool.memset(scratch[:, 16:17], 0.0).then_inc(sem("down_done"), 19)
            pool.wait_ge(sem("rw_in"), 16)
            pool.wait_ge(sem("sel2_done"), 1)
            with pool.Fori(0, E0 // 2) as i:
                for s in range(2):
                    e = i * 2 + s
                    pool.wait_ge(sem(f"w_in{s}"), i * 16 + 16)
                    pool.tensor_tensor(W0[s][:, 0:HID], W0[s][:, 0:HID], rw[:, ds(e, 1)].to_broadcast([128, HID]),
                                       ALU.mult).then_inc(sem("w_scaled"), 1)
                    pool.wait_ge(sem("w_scaled"), e + 1)
                    pool.wait_ge(sem("down_done"), i * 16 + 11 + 8 * s)
                    pool.tensor_tensor(W0h[s][:, :], W0[s][:, :], ones[:, 0:1].to_broadcast([128, 2 * HID]),
                                       ALU.mult).then_inc(sem("w_rounded"), 1)
                    pool.tensor_copy(esel[s][:, :], sel2[:, ds(e, 1)].to_broadcast([128, 128]).bitcast(F32R)).then_inc(sem("w_sel"), 1)
                    pool.wait_ge(sem("w_rounded"), e + 1)
                    pool.tensor_tensor(W0l[s][:, :], W0[s][:, :], W0h[s][:, :].bitcast(F32), ALU.subtract).then_inc(sem("w_split"), 1)
            for c in range(NC_):
                ln_factors(pool, 2, c)
            for t in range(T):
                pool.wait_ge(sem("z_ln"), t + 1)
                pool.wait_ge(sem("z_pos"), t + 1)
                pool.tensor_tensor(ZR[:, t, :], ZR[:, t, :], ZA[:, t, :], ALU.add).then_inc(sem("z_sp"), 1)
            pool.memset(mb[:, 0:1], -BIG).then_inc(sem("d_init"), 1)
            pool.memset(db[:, 0:1], 0.0).then_inc(sem("d_init"), 1)
            pool.wait_ge(sem("ab_placed"), 4)
            pool.wait_ge(sem("ab_T"), 1)
            pool.wait_ge(sem("vp_done"), 2 * NC_)
            for k in range(2):
                pool.memset(gb[k][:, :].rearrange("p (h t) -> p h t", h=H1)[:, :, 0:1], 0.0).then_inc(sem("floor_done"), 1)
            pool.memset(scratch[:, 17:18], 0.0).then_inc(sem("w_copied"), 2)
            pool.memset(scratch[:, 18:19], 0.0).then_inc(sem("signed_done"), 1)
            pool.memset(scratch[:, 19:20], 0.0).then_inc(sem("scan2_done"), 2)

            def floor_terms(g, par):
                pool.wait_ge(sem("sgn_done"), g + 1)
                pool.wait_ge(sem("abs_done"), g + 1)
                pool.tensor_tensor(dfb[par][:, :], dfb[par][:, :], sgb[:, :], ALU.mult).then_inc(sem("signed_done"), 1)
                pool.wait_ge(sem("signed_done"), g + 2)
                pool.wait_ge(sem("scan2_done"), g + 1)
                later = lambda x: x[:, :].rearrange("p (h t) -> p h t", h=H1)[:, :, 1:]
                pool.tensor_tensor(later(gb[par]), later(dfb[par]), later(r0b[par]), ALU.add).then_inc(sem("floor_done"), 1)

            with pool.Fori(0, B // 2) as i:
                for k in range(2):
                    floor_terms(i * 2 + k, k)
            for c in range(NC_):
                ln_factors(pool, 3, c)
            for h in range(2):
                tt = slice(8 * h, 8 * h + 8)
                pool.wait_ge(sem("es_step"), 11 + h)
                pool.tensor_tensor(SE[:, tt, :], SE[:, tt, :], el[:, tt].rearrange("p (t o) -> p t o", o=1).to_broadcast([128, 8, SC]),
                                   ALU.mult).then_inc(sem("e_prob"), 1)
            for c in range(NC_):
                ln_factors(pool, 4, c)
            pool.wait_ge(sem("x_added"), NC_ + NC_)
            pool.memset(zero[:, :], 0.0).then_inc(sem("f_init"), 1)
            pool.memset(GS[:, :, :], NEG).then_inc(sem("f_init"), 1)
            pool.memset(FR[:, :, :], NEG).then_inc(sem("f_init"), 1)
            pool.memset(scratch[:, 21:22], 0.0).then_inc(sem("fh_done"), 1)
            pool.memset(scratch[:, 22:23], 0.0).then_inc(sem("fhh_done"), 1)
            pool.memset(scratch[:, 23:24], 0.0).then_inc(sem("fhl_done"), 2)
            pool.memset(scratch[:, 1:2], 0.0).then_inc(sem("fg_done"), 2)
            pool.memset(scratch[:, 2:3], 0.0).then_inc(sem("ft_done"), 2)
            pool.memset(scratch[:, 3:4], 0.0).then_inc(sem("fdown_done"), 10)
            pool.memset(scratch[:, 4:5], 0.0).then_inc(sem("f_split"), 2)
            pool.wait_ge(sem("f_init"), 3)
            def split_experts(i, s):
                j = i * 2 + s
                pool.wait_ge(sem(f"w_in{s}"), E0 // 2 * 16 + i * 16 + 16)
                pool.tensor_tensor(W3h[s][:, :], W3[s][:, :], ones[:, 0:1].to_broadcast([128, 384]), ALU.mult).then_inc(sem("f_rounded"), 1)
                pool.tensor_copy(fsel[s][:, :, :], sel2[:, cols(j * 2, 2)].rearrange("p (e o) -> p e o", o=1)
                                 .to_broadcast([128, 2, 64])).then_inc(sem("f_sel"), 1)
                pool.wait_ge(sem("f_rounded"), j + 1)
                pool.tensor_tensor(W3l[s][:, :], W3[s][:, :], W3h[s][:, :].bitcast(F32), ALU.subtract).then_inc(sem("f_split"), 1)

            def early_product(k):
                pool.wait_ge(sem("fg_done"), k + 3)
                pool.wait_ge(sem("ft_done"), k + 3)
                pool.tensor_tensor(SG8[:, k, :], SG8[:, k, :], U4[:, k % 4, :], ALU.mult).then_inc(sem("f_early"), 1)

            split_experts(0, 0)
            split_experts(0, 1)
            halves = (slice(0, 8), slice(8, 16))
            for h, tt in enumerate(halves):
                pool.wait_ge(sem("f_step"), F_RECIP * (h + 1))
                pool.tensor_tensor(SF[:, tt, :], SCo[:, tt, :], ebias[:, :].rearrange("p (o e) -> p o e", o=1)
                                   .to_broadcast([128, 8, E1]), ALU.add).then_inc(sem("f_pool"), 1)

            def shared_rest(c):
                pool.wait_ge(sem("sh_hh"), c + 1)
                if c >= 2:
                    pool.wait_ge(sem("sh_down"), c - 1)
                pool.tensor_tensor(FHL[:, c % 2, :], FH[:, c % 2, :], FHH[:, c % 2, :].bitcast(F32), ALU.subtract).then_inc(sem("sh_hl"), 1)

            early_product(0)
            early_product(1)
            shared_rest(0)
            early_product(2)
            early_product(3)
            shared_rest(1)
            for h, tt in enumerate(halves):
                pool.wait_ge(sem("f_step"), F_GROUPS + h)
                g8 = lambda x: x[:, tt, :].rearrange("p t (g e) -> p (t g) e", e=8)
                pool.tensor_tensor(g8(FM), g8(SF), gm[:, tt, :].rearrange("p t (g o) -> p (t g) o", o=1)
                                   .to_broadcast([128, 64, 8]), ALU.mult).then_inc(sem("f_mask"), 1)
                pool.wait_ge(sem("f_mask"), h + 1)
                pool.tensor_tensor(FM[:, tt, :], FM[:, tt, :], zero[:, 0:1].rearrange("p (t o) -> p t o", o=1)
                                   .to_broadcast([128, 8, E1]), ALU.add).then_inc(sem("f_pool"), 1)
            early_product(4)
            early_product(5)
            shared_rest(2)
            early_product(6)
            early_product(7)
            shared_rest(3)
            for h, tt in enumerate(halves):
                pool.wait_ge(sem("f_hi"), h + 1)
                pool.tensor_tensor(GI1[:, tt, 64:128], FM[:, tt, :], GI1[:, tt, 0:64].bitcast(F32), ALU.subtract).then_inc(sem("gates_split"), 1)

            with pool.Fori(1, E1 // 4) as i:
                for s in range(2):
                    pool.wait_ge(sem("fdown_done"), i * 8 + 6 + 4 * s)
                    split_experts(i, s)
            for c in range(NC_):
                ln_factors(pool, 5, c)

        @block.scalar
        def _(act):
            act.wait_ge(sem("ctx_pe"), CTX_PE["ck_ready"])
            act.activation(ce[:, :, :], bank(0).rearrange("p (a d) -> p a d", a=4), ACT.Exp).then_inc(sem("ctx_act"), 1)
            act.wait_ge(sem("ctx_pe"), CTX_PE["cv_ready"])
            act.activation(cv[:, :, :], bank(1).rearrange("p (a d) -> p a d", a=4), ACT.Copy).then_inc(sem("ctx_act"), 1)
            act.activation(wqh[:, :], wx[:, 3, :], ACT.Copy).then_inc(sem("ctx_act"), 1)
            for n in range(8):
                act.wait_ge(sem("fold"), n + 1)
                dst = (NVh if n < 4 else Mh)[:, n % 4 * CH:n % 4 * CH + CH]
                act.activation(dst, fold_bank(n), ACT.Copy, scale=1.0 if n < 4 else -1.0 / math.sqrt(DH)).then_inc(sem("fold_hi"), 1)

            def split_x(b, slot):
                act.activation(xh[slot][:, :], xall[:, ds(b * S, S)] if not isinstance(b, int) else xall[:, b * S:b * S + S],
                               ACT.Copy).then_inc(sem("xh_done"), 1)

            act.wait_ge(sem("xT_in"), 16)
            act.wait_ge(sem("x_pad"), 1)
            split_x(0, 0)
            act.wait_ge(sem("ctx_pool"), CTX_POOL["kn_done"])
            act.wait_ge(sem("ctx_pe"), CTX_PE["g2_ready"])
            for b in range(B):
                src = bank(2 + b % 2)[:, b // 2 * 128:b // 2 * 128 + 128]
                act.activation(G2[:, b, :], src, ACT.Copy, scale=kn[:, b:b + 1]).then_inc(sem("ctx_act"), 1)

            def exps(g, k):
                par, slot = (k - 1) % 2, (k - 1) % 4
                for q in range(4):
                    c, w = piece(q)
                    act.wait_ge(sem("masked"), g * 4 + q + 1)
                    last = act.activation(P[:, slot, c:c + w], P[:, slot, c:c + w], ACT.Exp, scale=-1.0,
                                          bias=mn[:, par, q:q + 1], accum_out=ls[:, par, q:q + 1])
                last.then_inc(sem("exp_done"), 1)

            with act.Fori(0, B // 2) as i:
                for k in range(STEPS):
                    g = i * STEPS + k
                    act.wait_ge(sem("u_ready"), g + 1)
                    act.activation(Uh[:, :], UB, ACT.Copy).then_inc(sem("u_hi"), 1)
                    exps(g, k)
                    act.wait_ge(sem("vo_ready"), g + 1)
                    t, q4 = k % 2, k % 8 // 2
                    act.activation(VO[:, t, 4 * q4:4 * q4 + 4, :], UB, ACT.Copy).then_inc(sem("vo_done"), 1)
                    if k in (4, 12):
                        split_x(i * 2 + (1 if k == 4 else 2), 1 if k == 4 else 0)
            exps(B * PAIRS, 0)

            in_turn(lambda c: ln_norm(act, 0, c), lambda c: ln_hi(act, 0, c), 1)

            for c in range(NC_):
                act.wait_ge(sem("q_ready"), c + 1)
                act.activation(EQ[:, c * CH:c * CH + CH], bank(4 + c), ACT.Exp, bias=bq[:, 0:1]).then_inc(sem("q_exp"), 1)

            for c in range(NC_):
                act.wait_ge(sem("q_norm"), c + 1)
                act.activation(RQ[:, c * CH:c * CH + CH], bank(c), ACT.Ln, scale=float(DX)).then_inc(sem("q_ln"), 1)
            for c in range(NC_):
                act.wait_ge(sem("q_ln"), c + 1)
                act.activation(RQ[:, c * CH:c * CH + CH], RQ[:, c * CH:c * CH + CH], ACT.Exp, scale=-0.5).then_inc(sem("q_inv"), 1)

            def norm_and_scale(c):
                ln_norm(act, 1, c)
                act.wait_ge(sem("rms"), 4 * c + 4)
                for t in tiles(c):
                    act.wait_ge(sem("ln_x"), T + t + 1)
                    act.activation(XS[:, t, :], X[:, t, :], ACT.Copy, scale=rs2[:, t:t + 1]).then_inc(sem("xs_done"), 1)

            in_turn(norm_and_scale, lambda c: ln_hi(act, 1, c), 1)
            for c in range(NC_):
                act.wait_ge(sem("router_T"), c + 1)
                act.activation(LT[:, c * CH:c * CH + CH], bank(4 + c)[0:16, :], ACT.Copy).then_inc(sem("router_out"), 1)

            def gates_out(c):
                act.wait_ge(sem("gates_T"), c + 1)
                act.activation(SELT[:, c * CH:c * CH + CH], bank(4 + c % 2), ACT.Copy).then_inc(sem("gates_out"), 1)

            def round_h(U, k):
                act.wait_ge(sem("h_done"), U + 2)
                act.activation(HH[:, (k - 1) % 4, :], Hf[:, (k - 1) % 4, :], ACT.Copy).then_inc(sem("hh_done"), 1)

            def silu_unit(U, k):
                act.wait_ge(sem("h_done"), U + 1)
                act.wait_ge(sem("up_ready"), U + 1)
                act.activation(SG[:, k % 2, :], bank(6 + k % 2), ACT.Silu).then_inc(sem("sg_done"), 1)

            for k in range(16):
                silu_unit(k, k)
                if k:
                    round_h(k, k)
                if k == GATES_EXP:
                    act.wait_ge(sem("lg_sub"), 1)
                    act.activation(Lg[:, :, :], Lg[:, :, :], ACT.Exp).then_inc(sem("lg_exp"), 1)
                if k in GATES_PLACED:
                    gates_out(GATES_PLACED.index(k))
            with act.Fori(1, E0 // 2) as i:
                for k in range(16):
                    silu_unit(i * 16 + k, k)
                    round_h(i * 16 + k, k)
            round_h(E0 * 8, 0)
            for c in range(NC_):
                act.wait_ge(sem("down_done"), E0 * 8 + 3 + 16)
                act.activation(OT[:, c * CH:c * CH + CH], bank(c), ACT.Copy).then_inc(sem("sums_out"), 1)
            in_turn(lambda c: ln_norm(act, 2, c, sum_bank), lambda c: ln_hi(act, 2, c), 1)
            for first, end in SP_GROUPS:
                for t in range(first, end):
                    act.wait_ge(sem("dq_ready"), t + 1)
                    if t >= 2:
                        act.wait_ge(sem("pr_done"), t - 1)
                    act.activation(QS[:, t % 2, :], bank(4 + t % 2), ACT.Copy).then_inc(sem("qs_done"), 1)
                    act.wait_ge(sem("dz_ready"), t + 1)
                    act.activation(ZA[:, t, :], bank(6 + t % 2), ACT.Abs).then_inc(sem("z_abs"), 1)
                    act.wait_ge(sem("z_abs"), t + 1)
                    act.activation(ZA[:, t, :], ZA[:, t, :], ACT.Exp, scale=-1.0).then_inc(sem("z_exp"), 1)
                for t in range(first, end):
                    act.wait_ge(sem("z_exp"), t + 1)
                    act.activation(ZA[:, t, :], ZA[:, t, :], ACT.Ln, bias=1.0).then_inc(sem("z_ln"), 1)
            act.wait_ge(sem("ctx_pe"), CTX_PE["ke_ready"])
            act.activation(kTe[:, :], bank(4), ACT.Copy).then_inc(sem("ctx_act"), 1)
            act.wait_ge(sem("ctx_pe"), CTX_PE["ve_ready"])
            act.activation(vE[:, :, :], bank(6, CH, 2)[0:64, :].rearrange("p (b d) -> p b d", b=B), ACT.Copy).then_inc(sem("ctx_act"), 1)
            act.wait_ge(sem("ctx_pe"), CTX_PE["kk_ready"])
            act.activation(KK[:, :], bank(5), ACT.Copy, scale=1.0 / math.sqrt(D)).then_inc(sem("ctx_act"), 1)

            act.wait_ge(sem("ea_arg"), 1)
            act.activation(ea[:, :], ea[:, :], ACT.Exp).then_inc(sem("e_ab"), 1)
            act.activation(eb[:, :], eb[:, :], ACT.Exp).then_inc(sem("e_ab"), 1)

            def head_selector(b, slot):
                src = (sel2[:, ds(b, 64)] if not isinstance(b, int) else sel2[:, b:b + 64]).bitcast(F32)
                act.activation(dsel[slot][:, :, :], src.rearrange("p (h k) -> p h k", k=B)[:, :, 0:1].to_broadcast([128, H1, 128]),
                               ACT.Copy).then_inc(sem("dsel_done"), 1)

            head_selector(0, 0)
            act.wait_ge(sem("w_copied"), 2)
            with act.Fori(0, B // 2) as i:
                for k in range(2):
                    g = i * 2 + k
                    act.wait_ge(sem("scan2_done"), g + 1)
                    for r in range(4):
                        act.wait_ge(sem("w_bc"), g * 4 + r + 1)
                        act.activation(Wb[k][:, r * CH:r * CH + CH], bank(4 + r % 2), ACT.Copy).then_inc(sem("w_copied"), 1)
                    act.wait_ge(sem("u_bc"), g * 4 + 1)
                    head_selector(g + 1, 1 - k)
                    act.wait_ge(sem("signed_done"), g + 1)
                    act.wait_ge(sem("scan1_done"), g + 2)
                    act.activation(sgb[:, :], r0b[k][:, :], ACT.Sign, bias=tiny[:, 0:1]).then_inc(sem("sgn_done"), 1)
                    act.wait_ge(sem("diff_done"), g + 2)
                    act.activation(dfb[k][:, :], dfb[k][:, :], ACT.Abs).then_inc(sem("abs_done"), 1)

            def sum_out(c):
                act.wait_ge(sem("y1_done"), 2 * c + 5)
                act.activation(OD[:, c * CH:c * CH + CH], bank(c), ACT.Copy).then_inc(sem("sums_out"), 1)

            act.wait_ge(sem("diff_done"), B + 1)
            for c in range(3):
                sum_out(c)
            for c in range(3):
                ln_norm(act, 3, c, sum_bank)
            sum_out(3)

            def transposed(c):
                act.wait_ge(sem("ln_T"), 3 * NC_ + c + 1)
                act.activation(XTf[:, c * CH:c * CH + CH], bank(c), ACT.Copy).then_inc(sem("ln_hi"), 1)

            transposed(0)
            ln_norm(act, 3, 3, sum_bank)
            for c in range(1, NC_):
                transposed(c)
            for h in range(2):
                act.wait_ge(sem("es_step"), 6 + 2 * h)
                act.activation(SE[:, 8 * h:8 * h + 8, :], SE[:, 8 * h:8 * h + 8, :], ACT.Exp).then_inc(sem("e_exp"), 1)
            for c in range(NC_):
                act.wait_ge(sem("e_T"), c + 1)
                act.activation(PE_T[:, c * CH:c * CH + CH], bank(c)[0:64, :], ACT.Copy).then_inc(sem("e_pt"), 1)
            in_turn(lambda c: ln_norm(act, 4, c), lambda c: ln_hi(act, 4, c), 1)
            for c in range(NC_):
                act.wait_ge(sem("router_T"), NC_ + c + 1)
                act.activation(FL[:, c * CH:c * CH + CH], bank(4 + c)[0:64, :], ACT.Copy).then_inc(sem("router_out"), 1)
                if c % 2:
                    h = c // 2
                    act.wait_ge(sem("logits_T"), h + 2)
                    act.activation(SCo[:, 8 * h:8 * h + 8, :], bank(4 + h).rearrange("p (t e) -> p t e", e=E1), ACT.Exp,
                                   scale=-1.0).then_inc(sem("f_exp"), 1)
            for c in range(NC_):
                act.wait_ge(sem("sh_g"), c + 1)
                if c >= 2:
                    act.wait_ge(sem("sh_h"), c - 1)
                act.activation(FG[:, c % 2, :], bank(6), ACT.Silu).then_inc(sem("sh_sg"), 1)
                for k in EARLY[c]:
                    act.wait_ge(sem("g_ready"), k + 1)
                    act.activation(SG8[:, k, :], bank(4), ACT.Silu).then_inc(sem("fg_done"), 1)
                    act.wait_ge(sem("fu_ready"), k + 1)
                    if k >= 4:
                        act.wait_ge(sem("f_early"), k - 3)
                    act.activation(U4[:, k % 4, :], bank(5), ACT.Copy).then_inc(sem("ft_done"), 1)
                act.wait_ge(sem("sh_h"), c + 1)
                if c >= 2:
                    act.wait_ge(sem("sh_down"), c - 1)
                act.activation(FHH[:, c % 2, :], FH[:, c % 2, :], ACT.Copy).then_inc(sem("sh_hh"), 1)
            for h in range(2):
                act.wait_ge(sem("f_step"), F_STEPS - 1 + h)
                act.activation(GI1[:, 8 * h:8 * h + 8, 0:64], FM[:, 8 * h:8 * h + 8, :], ACT.Copy).then_inc(sem("f_hi"), 1)
            for c in range(NC_):
                act.wait_ge(sem("gates_T"), NC_ + c + 1)
                act.activation(SELT1[:, c * CH:c * CH + CH], bank(4 + c), ACT.Copy).then_inc(sem("gates_out"), 1)

            def round_f(U, k):
                act.wait_ge(sem("fh_done"), U + 1)
                act.activation(FHH[:, (k - 1) % 4, :], FH[:, (k - 1) % 4, :], ACT.Copy).then_inc(sem("fhh_done"), 1)

            act.wait_ge(sem("sh_down"), NC_)
            for k in range(1, 8):
                round_f(k, k)
            with act.Fori(1, E1 // 4) as i:
                for k in range(8):
                    U = i * 8 + k
                    act.wait_ge(sem("ft_done"), U + 1)
                    act.wait_ge(sem("g_ready"), U + 1)
                    act.activation(FG[:, k % 2, :], bank(4 + k % 2), ACT.Silu).then_inc(sem("fg_done"), 1)
                    round_f(U, k)
            round_f(E1 * 2, 0)
            act.wait_ge(sem("fdown_done"), E1 * 2 + 2 + 8)
            for c in range(NC_):
                act.activation(OT1[:, c * CH:c * CH + CH], bank(c), ACT.Copy).then_inc(sem("sums_out"), 1)
            for c in range(NC_):
                ln_norm(act, 5, c, sum_bank)

        @block.vector
        def _(dve):
            dve.wait_ge(sem("consts"), 5)
            dve.memset(sel2[:, 64:72].bitcast(F32), 0.0)
            dve.tensor_tensor(sel2[:, 0:64], ident[:, 0:64], ident[:, 64:128], ALU.add).then_inc(sem("sel2_done"), 1)
            dve.tensor_reduce(halfones[:, :], ident[:, :].rearrange("p (a c) -> p a c", a=2), AX.X, ALU.add).then_inc(sem("halves"), 1)
            dve.wait_ge(sem("ctx_act"), CTX_ACT["ck_exp"])
            dve.tensor_scalar(ce[:, :, :], ce[:, :, :], 1.0, -1.0, ALU.min, ALU.add).then_inc(sem("ctx_dve"), 1)
            dve.wait_ge(sem("ctx_dve"), CTX_DVE["ck_neg"])
            dve.tensor_tensor(ck[:, :, :], bank(0).rearrange("p (a d) -> p a d", a=4), ce[:, :, :], ALU.max).then_inc(sem("ctx_dve"), 1)
            def fold_rest(n):
                dve.wait_ge(sem("fold_hi"), n + 1)
                cols = slice(n % 4 * CH, n % 4 * CH + CH)
                hi, lo = (NVh, NVl) if n < 4 else (Mh, Ml)
                dve.scalar_tensor_tensor(lo[:, cols], fold_bank(n), 1.0 if n < 4 else -1.0 / math.sqrt(DH),
                                         hi[:, cols].bitcast(F32), ALU.mult, ALU.subtract).then_inc(sem("fold_lo"), 1)

            dve.wait_ge(sem("ctx_pe"), CTX_PE["kn_ready"])
            dve.tensor_scalar(kn[:, :], bank(2, B), float(S), None, ALU.mult).then_inc(sem("ctx_dve"), 1)
            for n in range(4):
                fold_rest(n)
            dve.wait_ge(sem("ctx_pe"), CTX_PE["gt_ready"])
            dve.tensor_tensor(GBT[:, :, :], bank(0, CH, 2).rearrange("p (b d) -> p b d", b=B),
                              blockones[:, :].rearrange("p (o d) -> p o d", o=1).to_broadcast([128, B, 128]),
                              ALU.mult).then_inc(sem("ctx_dve"), 1)
            for n in range(4, 8):
                fold_rest(n)

            def split_x(b, slot):
                dve.tensor_tensor(xl[slot][:, :], xall[:, ds(b * S, S)] if not isinstance(b, int) else xall[:, b * S:b * S + S],
                                  xh[slot][:, :].bitcast(F32), ALU.subtract).then_inc(sem("xl_done"), 1)

            dve.wait_ge(sem("xh_done"), 1)
            split_x(0, 0)
            dve.memset(Xp[:, 0:S], 0.0)
            dve.wait_ge(sem("fold_lo"), 8)
            dve.memset(bank(7), 0.0).then_inc(sem("acc_free"), 1)
            dve.wait_ge(sem("ctx_act"), CTX_ACT["g2_done"])
            dve.memset(bank(2, CH, 2), 0.0).then_inc(sem("s_ready"), 1)
            dve.wait_ge(sem("ctx_act"), CTX_ACT["wq_hi"])
            dve.tensor_tensor(wql[:, :], wx[:, 3, :], wqh[:, :].bitcast(F32), ALU.subtract).then_inc(sem("ctx_dve"), 1)
            dve.wait_ge(sem("wr_in"), 16)
            dve.wait_ge(sem("wr_zero"), 2)
            dve.tensor_copy(wrh[:, 0:E0R], wr_in[:, :]).then_inc(sem("ctx_dve"), 1)
            dve.wait_ge(sem("ctx_dve"), CTX_DVE["wr_split"] - 1)
            dve.tensor_tensor(wrl[:, 0:E0R], wr_in[:, :], wrh[:, 0:E0R].bitcast(F32), ALU.subtract).then_inc(sem("ctx_dve"), 1)

            dve.wait_ge(sem("x_in"), 16)

            def mask_and_max(g, k):
                par, slot = (k - 1) % 2, (k - 1) % 4
                dve.wait_ge(sem("s_ready"), g + 1)
                dve.memset(scratch[:, 5:6], 0.0)
                for q in range(4):
                    c, w = piece(q)
                    dve.tensor_tensor_reduce(out=P[:, slot, c:c + w], in0=scores(par, q), in1=cmask[:, 256 - w:256],
                                             scale=1.0, scalar=3e38, op0=ALU.add, op1=ALU.min,
                                             accum_out=mn[:, par, q:q + 1]).then_inc(sem("masked"), 1)

            def invert(g, k):
                par = (k - 1) % 2
                dve.wait_ge(sem("exp_done"), g + 1)
                dve.reciprocal(rl[:, par, :], ls[:, par, :]).then_inc(sem("rl_done"), 1)

            def copy_pt(g, k):
                dve.wait_ge(sem("t_ready"), g + 1)
                dve.tensor_copy(PT[:, k % 2, :, :], PTP).then_inc(sem("pt_done"), 1)

            def add_out(b, g):
                dve.wait_ge(sem("pv_done"), g + 1)
                x = Xp[:, ds(b * S, S)] if not isinstance(b, int) else Xp[:, b * S:b * S + S]
                dve.tensor_tensor(x, x, OB[:, 0:256], ALU.add).then_inc(sem("acc_free"), 1)

            with dve.Fori(0, B // 2) as i:
                for k in range(STEPS):
                    g = i * STEPS + k
                    mask_and_max(g, k)
                    dve.wait_ge(sem("u_hi"), g + 1)
                    dve.tensor_tensor(Ul[:, :], UB, Uh[:, :].bitcast(F32), ALU.subtract).then_inc(sem("u_lo"), 1)
                    copy_pt(g, k)
                    if k in (2, 10):
                        add_out(i * 2 + k // 8, g)
                    invert(g, k)
                    if k in (4, 12):
                        dve.wait_ge(sem("xh_done"), i * 2 + (2 if k == 4 else 3))
                        split_x(i * 2 + (1 if k == 4 else 2), 1 if k == 4 else 0)
            G = B * PAIRS
            mask_and_max(G, 0)
            copy_pt(G, 0)
            invert(G, 0)
            copy_pt(G + 1, 1)
            for c in range(3):
                dve.wait_ge(sem("acc_free"), 2 * c + 4)
                ln_stats(dve, 0, c)
            add_out(B, G + 2)
            dve.wait_ge(sem("acc_free"), B + 2)
            ln_stats(dve, 0, 3)
            for c in range(NC_):
                ln_lo(dve, 0, c)

            for c in range(NC_):
                cc = slice(c * CH, c * CH + CH)
                dve.wait_ge(sem("q_exp"), c + 1)
                dve.tensor_scalar(EQ[:, cc], EQ[:, cc], 1.0, -1.0, ALU.min, ALU.add).then_inc(sem("q_neg"), 1)
                dve.wait_ge(sem("q_neg"), c + 1)
                dve.scalar_tensor_tensor(Q[:, cc], bank(4 + c), bq[:, 0:1], EQ[:, cc], ALU.add, ALU.max).then_inc(sem("q_elu"), 1)
            dve.memset(tiny[:, :], 1e-37)
            dve.memset(abr[:, :].bitcast(F32), 0.0).then_inc(sem("wr1"), 1)
            dve.memset(onesr[:, :].bitcast(F32), 1.0).then_inc(sem("l1_split"), 1)
            dve.wait_ge(sem("l1_in"), 16 * 7)
            dve.memset(wr1h[:, :].bitcast(F32), 0.0).then_inc(sem("wr1"), 1)
            dve.memset(wr1l[:, :].bitcast(F32), 0.0).then_inc(sem("wr1"), 1)
            dve.wait_ge(sem("wr1"), 3)
            dve.tensor_copy(wr1h[:, 0:E1], wr1_in[:, :]).then_inc(sem("wr1"), 1)
            dve.tensor_copy(wdh[:, :], wd_in[:, :]).then_inc(sem("wr1"), 1)
            dve.tensor_copy(wshh[:, :], wsh[:, :]).then_inc(sem("wr1"), 1)
            dve.tensor_copy(abr[0:1, :], abias[:, :]).then_inc(sem("wr1"), 1)
            dve.wait_ge(sem("wr1"), 7)
            dve.tensor_tensor(abr[32:33, :], abias[:, :], abr[0:1, :].bitcast(F32), ALU.subtract).then_inc(sem("l1_split"), 1)
            dve.tensor_tensor(wr1l[:, 0:E1], wr1_in[:, :], wr1h[:, 0:E1].bitcast(F32), ALU.subtract).then_inc(sem("l1_split"), 1)
            dve.tensor_tensor(wdl[:, :], wd_in[:, :], wdh[:, :].bitcast(F32), ALU.subtract).then_inc(sem("l1_split"), 1)
            dve.tensor_scalar(wo1e[:, :], wo1[:, :], EPS / 2, None, ALU.mult)
            dve.tensor_tensor(wshl[:, :], wsh[:, :], wshh[:, :].bitcast(F32), ALU.subtract).then_inc(sem("l1_split"), 1)

            for c in range(NC_):
                cc = slice(c * CH, c * CH + CH)
                dve.wait_ge(sem("q_sq"), c + 1)
                dve.wait_ge(sem("q_inv"), c + 1)
                dve.tensor_tensor(Q[:, cc], Q[:, cc], RQ[:, cc], ALU.mult).then_inc(sem("q_done"), 1)

            def add_bank(c, b):
                x = Xp[:, S + c * CH:S + c * CH + CH]
                dve.tensor_tensor(x, x, bank(b), ALU.add).then_inc(sem("x_added"), 1)

            def add_query_out(c):
                dve.wait_ge(sem("b_out"), c + 1)
                add_bank(c, 4 + c)
                dve.wait_ge(sem("x_added"), c + 1)
                ln_stats(dve, 1, c)

            for c in range(NC_):
                add_query_out(c)
            for c in range(NC_):
                ln_lo(dve, 1, c)

            dve.memset(GI[:, :, :].bitcast(F32), 0.0).then_inc(sem("c_zeros"), 1)
            dve.memset(G20[:, :, :], -1.0).then_inc(sem("c_zeros"), 1)
            dve.memset(RPL[:, :, :], -1.0).then_inc(sem("c_zeros"), 1)
            bc = lambda v, w: v.rearrange("p (t o) -> p t o", o=1).to_broadcast([128, T, w])

            def gates_step(n):
                if n == 0:
                    dve.wait_ge(sem("rms"), 4 * NC_)
                    dve.reciprocal(lm[:, :], rs2[:, :]).then_inc(sem("g_step"), 1)
                elif n == 1:
                    dve.wait_ge(sem("g_step"), 1)
                    dve.wait_ge(sem("logits_T"), 1)
                    dve.tensor_tensor(Lg[:, :, :], bank(4, 256).rearrange("p (t e) -> p t e", e=16)[:, :, 0:E0R],
                                      bc(lm[:, :], E0R), ALU.mult).then_inc(sem("g_step"), 1)
                elif n == 2:
                    dve.wait_ge(sem("g_step"), 2)
                    dve.tensor_reduce(lz[:, :], Lg[:, :, :], AX.X, ALU.max).then_inc(sem("g_step"), 1)
                elif n == 3:
                    dve.wait_ge(sem("g_step"), 3)
                    dve.tensor_tensor(Lg[:, :, :], Lg[:, :, :], bc(lz[:, :], E0R), ALU.subtract).then_inc(sem("lg_sub"), 1)
                elif n == 4:
                    dve.wait_ge(sem("lg_exp"), 1)
                    dve.tensor_reduce(lm[:, :], Lg[:, :, :], AX.X, ALU.add).then_inc(sem("g_step"), 1)
                elif n == 5:
                    dve.wait_ge(sem("g_step"), 4)
                    dve.reciprocal(lz[:, :], lm[:, :]).then_inc(sem("g_step"), 1)
                elif n == 6:
                    dve.wait_ge(sem("g_step"), 5)
                    dve.wait_ge(sem("c_zeros"), 3)
                    dve.tensor_tensor(G20[:, :, 0:E0R], Lg[:, :, :], bc(lz[:, :], E0R), ALU.mult).then_inc(sem("g_step"), 1)
                elif n == 7:
                    dve.wait_ge(sem("g_step"), 6)
                    for t in range(T):
                        last = dve.max(M8[:, t, :], G20[:, t, :])
                    last.then_inc(sem("g_step"), 1)
                elif n == 8:
                    dve.wait_ge(sem("g_step"), 7)
                    dve.tensor_copy(RPL[:, :, 0:2], M8[:, :, 0:2]).then_inc(sem("g_step"), 1)
                elif n == 9:
                    dve.wait_ge(sem("g_step"), 8)
                    for t in range(T):
                        last = dve.match_replace(RP[:, t, :], RPL[:, t, :], G20[:, t, :], -5.0)
                    last.then_inc(sem("g_step"), 1)
                elif n == 10:
                    dve.wait_ge(sem("g_step"), 9)
                    dve.scalar_tensor_tensor(Lg[:, :, :], RP[:, :, 0:E0R], -4.0, G20[:, :, 0:E0R], ALU.is_lt, ALU.mult).then_inc(sem("g_step"), 1)
                elif n == 11:
                    dve.wait_ge(sem("g_step"), 10)
                    dve.tensor_reduce(lm[:, :], Lg[:, :, :], AX.X, ALU.add).then_inc(sem("g_step"), 1)
                elif n == 12:
                    dve.wait_ge(sem("g_step"), 11)
                    dve.tensor_scalar(lm[:, :], lm[:, :], 1e-9, None, ALU.add).then_inc(sem("g_step"), 1)
                elif n == 13:
                    dve.wait_ge(sem("g_step"), 12)
                    dve.reciprocal(lz[:, :], lm[:, :]).then_inc(sem("g_step"), 1)
                elif n == 14:
                    dve.wait_ge(sem("g_step"), 13)
                    dve.tensor_tensor(Lg[:, :, :], Lg[:, :, :], bc(lz[:, :], E0R), ALU.mult).then_inc(sem("g_step"), 1)
                elif n == 15:
                    dve.wait_ge(sem("g_step"), 14)
                    dve.wait_ge(sem("c_zeros"), 3)
                    dve.tensor_copy(GI[:, :, 2:E0], Lg[:, :, :]).then_inc(sem("g_step"), 1)
                elif n == 16:
                    dve.wait_ge(sem("g_step"), 15)
                    dve.tensor_tensor(GI[:, :, 66:64 + E0], Lg[:, :, :], GI[:, :, 2:E0].bitcast(F32), ALU.subtract).then_inc(sem("gates_split"), 1)

            def rest_h(U, k):
                dve.wait_ge(sem("hh_done"), U + 1)
                dve.tensor_tensor(HL[:, (k - 1) % 4, :], Hf[:, (k - 1) % 4, :], HH[:, (k - 1) % 4, :].bitcast(F32),
                                  ALU.subtract).then_inc(sem("hl_done"), 1)

            for k in range(16):
                dve.wait_ge(sem("sg_done"), k + 3)
                dve.tensor_copy(Hf[:, k % 4, :], SG[:, k % 2, :]).then_inc(sem("h_done"), 1)
                if k:
                    rest_h(k, k)
                for n in range(2 * k, 2 * k + 2):
                    if n < GATE_STEPS:
                        gates_step(n)
            with dve.Fori(1, E0 // 2) as i:
                for k in range(16):
                    U = i * 16 + k
                    if k % 2 == 0:
                        dve.wait_ge(sem("gb_ready"), i * 8 + k // 2 - 7)
                    dve.wait_ge(sem("sg_done"), U + 3)
                    dve.tensor_tensor(Hf[:, k % 4, :], SG[:, k % 2, :], bank(4 + k // 2 % 2), ALU.mult).then_inc(sem("h_done"), 1)
                    rest_h(U, k)
            rest_h(E0 * 8, 0)

            def sums_stats(c):
                dve.wait_ge(sem("sums_T"), c + 1)
                ln_stats(dve, 2, c, sum_bank)

            for c in range(NC_):
                sums_stats(c)
            for c in range(NC_):
                ln_lo(dve, 2, c)
            def softplus_sums(first, end):
                dve.wait_ge(sem("z_sp"), end)
                dve.tensor_reduce(ABs[:, 0, first:end, :].rearrange("p t h -> p (t h)"),
                                  ZR[:, first:end, :].rearrange("p t (h d) -> p (t h) d", h=H1), AX.X, ALU.add).then_inc(sem("ab_sums"), 1)

            def signed_values(c):
                cc = slice(c * CH, c * CH + CH)
                dve.wait_ge(sem("dv_ready"), c + 1)
                dve.tensor_scalar(VS[:, cc], bank(c % 2), 0.0, 2 * EPS, ALU.is_ge, ALU.mult).then_inc(sem("vp_done"), 1)
                dve.wait_ge(sem("vp_done"), 2 * c + 1)
                dve.scalar_tensor_tensor(VP[:, cc], bank(c % 2), EPS, VS[:, cc], ALU.subtract, ALU.add).then_inc(sem("vp_done"), 1)

            for t in range(T):
                p = t % 2
                dve.wait_ge(sem("qs_done"), t + 1)
                dve.wait_ge(sem("dk_ready"), t + 1)
                dve.tensor_tensor(PR[:, p, :], bank(2 + p), QS[:, p, :], ALU.mult).then_inc(sem("pr_done"), 1)
                dve.wait_ge(sem("z_abs"), t + 1)
                dve.tensor_scalar(ZR[:, t, :], bank(6 + p), 0.0, None, ALU.max).then_inc(sem("z_pos"), 1)
                dve.wait_ge(sem("pr_done"), t + 1)
                dve.tensor_reduce(ABs[:, 1, t, :], PR[:, p, :].rearrange("p (h d) -> p h d", h=H1), AX.X, ALU.add).then_inc(sem("b_sum"), 1)
                if t % 4 == 3:
                    signed_values(t // 4)
                for first, end in SP_GROUPS:
                    for n in range((end - first) // 2):
                        if t == end + 1 + n:
                            softplus_sums(first + 2 * n, first + 2 * n + 2)
            for t in range(SP_GROUPS[-1][0], T, 2):
                softplus_sums(t, t + 2)
            dve.wait_ge(sem("b_sum"), T)
            dve.wait_ge(sem("ab_sums"), T // 2)
            for n, scale in ((1, 1.0 / math.sqrt(64)), (0, -1.0)):
                src = ABs[:, n, :, :].rearrange("p (b r) h -> p r h b", r=2)
                for r in range(2):
                    dve.tensor_scalar(ABt[:, r, n, :, :], src[:, r, :, :], scale, None, ALU.mult).then_inc(sem("ab_placed"), 1)
            dve.wait_ge(sem("ab_T"), 1)
            dve.tensor_copy(AB64[:, :, :], bank(4)[0:64, :].rearrange("p (n t) -> p n t", n=2)).then_inc(sem("ab_in"), 1)
            dve.wait_ge(sem("ab_in"), 1)
            dve.wait_ge(sem("d_init"), 2)
            av, bv = AB64[:, 0, :], AB64[:, 1, :]
            dve.tensor_tensor_scan(mb[:, 1:], av, bv, -BIG, ALU.add, ALU.max).then_inc(sem("r_step"), 1)
            dve.wait_ge(sem("r_step"), 1)
            dve.tensor_tensor(ea[:, :], av, mb[:, 0:S], ALU.add).then_inc(sem("r_step"), 1)
            dve.tensor_tensor(eb[:, :], bv, mb[:, 1:], ALU.subtract).then_inc(sem("r_step"), 1)
            dve.wait_ge(sem("r_step"), 3)
            dve.tensor_tensor(ea[:, :], ea[:, :], mb[:, 1:], ALU.subtract).then_inc(sem("ea_arg"), 1)
            dve.wait_ge(sem("e_ab"), 2)
            dve.tensor_tensor_scan(db[:, 1:], ea[:, :], eb[:, :], 0.0, ALU.mult, ALU.add).then_inc(sem("r_step"), 1)
            dve.wait_ge(sem("r_step"), 4)
            dve.reciprocal(rd[:, :], db[:, 1:]).then_inc(sem("r_step"), 1)
            dve.tensor_tensor(ea[:, :], ea[:, :], db[:, 0:S], ALU.mult).then_inc(sem("r_step"), 1)
            dve.wait_ge(sem("r_step"), 6)
            dve.tensor_tensor(wu[:, 0, :], ea[:, :], rd[:, :], ALU.mult).then_inc(sem("r_step"), 1)
            dve.tensor_tensor(wu[:, 1, :], eb[:, :], rd[:, :], ALU.mult).then_inc(sem("r_step"), 1)
            dve.wait_ge(sem("r_step"), 8)
            dve.tensor_copy(WUr[0:64, :, :], wu[:, :, :]).then_inc(sem("r_step"), 1)
            dve.wait_ge(sem("r_step"), 9)
            dve.tensor_tensor(WUr[64:128, :, :], wu[:, :, :], WUr[0:64, :, :].bitcast(F32), ALU.subtract).then_inc(sem("wu_done"), 1)
            dve.memset(scratch[:, 6:7], 0.0).then_inc(sem("qr_done"), 2)
            dve.memset(scratch[:, 7:8], 0.0).then_inc(sem("u_bc"), 1)
            dve.memset(scratch[:, 20:21], 0.0).then_inc(sem("scan1_done"), 1)
            dve.memset(scratch[:, 10:11], 0.0).then_inc(sem("diff_done"), 1)
            dve.memset(scratch[:, 8:9], 0.0).then_inc(sem("y0_done"), 2)
            dve.memset(scratch[:, 9:10], 0.0).then_inc(sem("y1_done"), 3)

            def last_scan(g, par):
                dve.wait_ge(sem("floor_done"), g + 2)
                dve.wait_ge(sem("y1_done"), g + 1)
                dve.tensor_tensor_scan(rb[1 - par][:, :], Wb[1 - par][:, :], gb[1 - par][:, :], 0.0, ALU.mult, ALU.add).then_inc(sem("scan2_done"), 1)

            dve.wait_ge(sem("w_copied"), 2)
            dve.wait_ge(sem("signed_done"), 1)

            def recurrence(i, k):
                g = i * 2 + k
                dve.wait_ge(sem("diff_done"), g + 1)
                for r in range(4):
                    dve.wait_ge(sem("u_bc"), g * 4 + r + 2)
                    v = VP[:, cols(g * S, S)].rearrange("p (o t) -> p o t", o=1).to_broadcast([128, 2, S])
                    dve.tensor_tensor(qb[:, r * CH:r * CH + CH].rearrange("p (h t) -> p h t", h=2),
                                      bank(6 + r % 2).rearrange("p (h t) -> p h t", h=2), v, ALU.mult).then_inc(sem("qr_done"), 1)
                dve.wait_ge(sem("qr_done"), g * 4 + 6)
                dve.wait_ge(sem("w_copied"), g * 4 + 6)
                dve.wait_ge(sem("y0_done"), g + 1)
                dve.wait_ge(sem("floor_done"), g + 1)
                dve.tensor_tensor_scan(r0b[k][:, :], Wb[k][:, :], qb[:, :], 0.0, ALU.mult, ALU.add).then_inc(sem("scan1_done"), 1)
                dve.wait_ge(sem("scan1_done"), g + 2)
                dve.scalar_tensor_tensor(dfb[k][:, :], qb[:, :], -2.0, r0b[k][:, :], ALU.mult, ALU.add).then_inc(sem("diff_done"), 1)

            recurrence(0, 0)
            recurrence(0, 1)
            last_scan(1, 1)
            with dve.Fori(1, B // 2) as i:
                for k in range(2):
                    recurrence(i, k)
                    last_scan(i * 2 + k, k)

            def sums_stats(c):
                dve.wait_ge(sem("sums_T"), NC_ + c + 1)
                ln_stats(dve, 3, c, sum_bank)

            for c in range(3):
                sums_stats(c)
            last_scan(B, 0)
            sums_stats(3)

            def masked_scores(h):
                sc_ = bank(4 + h).rearrange("p (b r s) -> p b r s", b=B // 2, r=2)
                sev = SE[:, 8 * h:8 * h + 8, :].rearrange("p (b r) s -> p b r s", r=2)
                dve.wait_ge(sem("es_ready"), 2 * h + 2)
                dve.tensor_tensor(sev[:, :, 0, :], sc_[:, :, 0, :], cmask[:, 128:192].rearrange("p (o s) -> p o s", o=1)
                                  .to_broadcast([128, B // 2, SC]), ALU.subtract).then_inc(sem("es_step"), 1)
                dve.tensor_copy(sev[:, :, 1, :], sc_[:, :, 1, :]).then_inc(sem("es_step"), 1)

            def row_reduce(h, after, op):
                tt = slice(8 * h, 8 * h + 8)
                dve.wait_ge(sem("es_step"), after)
                dve.tensor_reduce(em[:, tt], SE[:, tt, :], AX.X, op).then_inc(sem("es_step"), 1)

            def less_maximum(h, after):
                tt = slice(8 * h, 8 * h + 8)
                dve.wait_ge(sem("es_step"), after)
                dve.tensor_tensor(SE[:, tt, :], SE[:, tt, :], em[:, tt].rearrange("p (t o) -> p t o", o=1).to_broadcast([128, 8, SC]),
                                  ALU.subtract).then_inc(sem("es_step"), 1)

            masked_scores(0)
            row_reduce(0, 2, ALU.max)
            masked_scores(1)
            less_maximum(0, 3)
            row_reduce(1, 5, ALU.max)
            less_maximum(1, 7)
            for h in range(2):
                dve.wait_ge(sem("e_exp"), h + 1)
                row_reduce(h, 8, ALU.add)
            for h in range(2):
                dve.wait_ge(sem("es_step"), 9 + h)
                dve.reciprocal(el[:, 8 * h:8 * h + 8], em[:, 8 * h:8 * h + 8]).then_inc(sem("es_step"), 1)
            for c in range(NC_):
                dve.wait_ge(sem("e_out"), c + 1)
                add_bank(c, 4 + c)
                dve.wait_ge(sem("x_added"), NC_ + c + 1)
                ln_stats(dve, 4, c)
            for c in range(NC_):
                ln_lo(dve, 4, c)

            count = [0]
            last_step = [0, 0]
            dve.wait_ge(sem("f_init"), 3)

            def step(ops, pool_steps=0):
                for h in range(2):
                    if pool_steps:
                        dve.wait_ge(sem("f_pool"), pool_steps + h)
                    else:
                        dve.wait_ge(sem("f_step"), last_step[h])
                    tt = slice(8 * h, 8 * h + 8)
                    last = [op(tt) for op in ops][-1]
                    last.then_inc(sem("f_step"), 1)
                    count[0] += 1
                    last_step[h] = count[0]

            def by_tile(op):
                return lambda tt: [op(t) for t in range(tt.start, tt.stop)][-1]

            def shared_hidden(c):
                dve.wait_ge(sem("sh_u"), c + 1)
                dve.wait_ge(sem("sh_sg"), c + 1)
                if c >= 2:
                    dve.wait_ge(sem("sh_hl"), c - 1)
                    dve.wait_ge(sem("sh_hh"), c - 1)
                dve.tensor_tensor(FH[:, c % 2, :], FG[:, c % 2, :], bank(7), ALU.mult).then_inc(sem("sh_h"), 1)

            gr = lambda x, tt: x[:, 8 * tt.start:8 * tt.stop, :]
            g8 = lambda x, tt: x[:, tt, :].rearrange("p t (g e) -> p (t g) e", e=8)
            tg = lambda x, tt: gr(x, tt).rearrange("p (t g) o -> p t (g o)", g=8)
            b8 = lambda v, w: v.rearrange("p (t o) -> p t o", o=1).to_broadcast([128, 8, w])
            for h in range(2):
                tt = slice(8 * h, 8 * h + 8)
                dve.wait_ge(sem("f_exp"), h + 1)
                dve.tensor_scalar(SCo[:, tt, :], SCo[:, tt, :], 1.0, None, ALU.add).then_inc(sem("f_step"), 1)
                dve.wait_ge(sem("f_step"), 2 * h + 1)
                dve.reciprocal(SCo[:, tt, :], SCo[:, tt, :]).then_inc(sem("f_step"), 1)
                count[0] += 2
            shared_hidden(0)
            step([lambda tt: dve.tensor_tensor(gr(h1, tt), g8(SF, tt)[:, :, 0:4], g8(SF, tt)[:, :, 4:8], ALU.max),
                  lambda tt: dve.tensor_tensor(gr(l1, tt), g8(SF, tt)[:, :, 0:4], g8(SF, tt)[:, :, 4:8], ALU.min)], pool_steps=1)
            step([lambda tt: dve.tensor_tensor(gr(h2, tt), gr(h1, tt)[:, :, 0:2], gr(h1, tt)[:, :, 2:4], ALU.max),
                  lambda tt: dve.tensor_tensor(gr(t2, tt), gr(h1, tt)[:, :, 0:2], gr(h1, tt)[:, :, 2:4], ALU.min),
                  lambda tt: dve.tensor_tensor(gr(l2, tt), gr(l1, tt)[:, :, 0:2], gr(l1, tt)[:, :, 2:4], ALU.max)])
            step([lambda tt: dve.tensor_tensor(gr(l2, tt), gr(l2, tt), gr(t2, tt), ALU.max)])
            step([lambda tt: dve.tensor_tensor(gr(h3, tt), gr(h2, tt)[:, :, 0:1], gr(h2, tt)[:, :, 1:2], ALU.max),
                  lambda tt: dve.tensor_tensor(gr(t3, tt), gr(h2, tt)[:, :, 0:1], gr(h2, tt)[:, :, 1:2], ALU.min),
                  lambda tt: dve.tensor_tensor(gr(l3, tt), gr(l2, tt)[:, :, 0:1], gr(l2, tt)[:, :, 1:2], ALU.max)])
            step([lambda tt: dve.tensor_tensor(gr(l3, tt), gr(l3, tt), gr(t3, tt), ALU.max)])
            step([lambda tt: dve.tensor_tensor(GS[:, tt, 0:8], tg(h3, tt), tg(l3, tt), ALU.add)])
            step([by_tile(lambda t: dve.max(F8[:, t, :], GS[:, t, 0:8]))])
            shared_hidden(1)
            step([lambda tt: dve.tensor_copy(FR[:, tt, 0:4], F8[:, tt, 0:4])])
            step([by_tile(lambda t: dve.match_replace(GR[:, t, :], FR[:, t, :], GS[:, t, :], -NEG))])
            step([lambda tt: dve.tensor_scalar(gm[:, tt, :], GR[:, tt, 0:8], 2.9e38, None, ALU.is_ge)])
            shared_hidden(2)
            step([by_tile(lambda t: dve.max(F8[:, t, :], FM[:, t, :]))], pool_steps=3)
            step([by_tile(lambda t: dve.match_replace(FRP[:, t, :], F8[:, t, :], FM[:, t, :], NEG))])
            shared_hidden(3)
            step([lambda tt: dve.scalar_tensor_tensor(FM[:, tt, :], FRP[:, tt, :], -2.9e38, SCo[:, tt, :], ALU.is_le, ALU.mult)])
            step([lambda tt: dve.tensor_reduce(fs[:, tt], FM[:, tt, :], AX.X, ALU.add)])
            step([lambda tt: dve.tensor_scalar(fs[:, tt], fs[:, tt], 1e-20, None, ALU.add)])
            step([lambda tt: dve.reciprocal(fi[:, tt], fs[:, tt])])
            step([lambda tt: dve.tensor_scalar(fi[:, tt], fi[:, tt], 2.5, None, ALU.mult)])
            step([lambda tt: dve.tensor_tensor(FM[:, tt, :], FM[:, tt, :], b8(fi[:, tt], E1), ALU.mult)])

            def rest_f(U, k):
                dve.wait_ge(sem("fhh_done"), U + 1)
                dve.tensor_tensor(FHL[:, (k - 1) % 4, :], FH[:, (k - 1) % 4, :], FHH[:, (k - 1) % 4, :].bitcast(F32),
                                  ALU.subtract).then_inc(sem("fhl_done"), 1)

            dve.wait_ge(sem("sh_hl"), NC_)
            dve.wait_ge(sem("sh_hh"), NC_)
            dve.wait_ge(sem("sh_down"), NC_)
            for k in range(8):
                dve.wait_ge(sem("f_early"), k + 1)
                dve.wait_ge(sem("fgb_ready"), k + 1)
                dve.tensor_tensor(FH[:, k % 4, :], SG8[:, k, :], bank(7), ALU.mult).then_inc(sem("fh_done"), 1)
                if k:
                    rest_f(k, k)
            with dve.Fori(1, E1 // 4) as i:
                for k in range(8):
                    U = i * 8 + k
                    dve.wait_ge(sem("fg_done"), U + 3)
                    dve.wait_ge(sem("fu_ready"), U + 1)
                    dve.tensor_tensor(FU[:, k % 2, :], FG[:, k % 2, :], bank(6), ALU.mult).then_inc(sem("ft_done"), 1)
                    rest_f(U, k)
                    dve.wait_ge(sem("ft_done"), U + 3)
                    dve.wait_ge(sem("fgb_ready"), U + 1)
                    dve.tensor_tensor(FH[:, k % 4, :], FU[:, k % 2, :], bank(7), ALU.mult).then_inc(sem("fh_done"), 1)
            rest_f(E1 * 2, 0)
            for c in range(NC_):
                dve.wait_ge(sem("sums_T"), 2 * NC_ + c + 1)
                ln_stats(dve, 5, c, sum_bank)

        @block.tensor
        def _(pe):
            def mm3(dst, l, r, start=True, stop=True, skip=False):
                pe.matmul(dst, l[0], r[0], start=start, stop=False, skip_group_check=skip)
                pe.matmul(dst, l[0], r[1], start=False, stop=False, skip_group_check=skip)
                return pe.matmul(dst, l[1], r[0], start=False, stop=stop, skip_group_check=skip)

            def fold(n):
                pe.wait_ge(sem("w_vo_in" if n < 4 else "w_qk_in"), 32)
                if n >= 4:
                    pe.wait_ge(sem("fold_lo"), n - 3)
                l, r = (w64["v"], w64["o"]) if n < 4 else (w64["q"], w64["k"])
                for h in range(4):
                    last = pe.matmul(fold_bank(n)[:, h * 128:h * 128 + 128], l[:, n % 4 * 4 + h, :], r[:, n % 4 * 4 + h, :],
                                     start=True, stop=True)
                last.then_inc(sem("fold"), 1)

            pe.wait_ge(sem("ctx_in"), 64)
            pe.wait_ge(sem("consts"), 5)
            for n in range(2):
                for p in range(4):
                    dst = bank(n)[:, p * 128:p * 128 + 128]
                    pe.matmul(dst, ctxT[:, p * 128:p * 128 + 128], wx[:, n, :], start=True, stop=False)
                    last = pe.matmul(dst, ones[0:1, :], brow[0:1, n * 128:n * 128 + 128], start=False, stop=True)
                last.then_inc(sem("ctx_pe"), 1)
            for n in range(4):
                fold(n)
            pe.wait_ge(sem("halves"), 1)
            pe.wait_ge(sem("ctx_pool"), CTX_POOL["ck_sq"])
            for p in range(4):
                last = pe.matmul(bank(2)[:, 2 * p:2 * p + 2], csq[:, p, :], halfones[:, :], start=True, stop=True)
            last.then_inc(sem("ctx_pe"), 1)
            pe.wait_ge(sem("ctx_dve"), CTX_DVE["ck_done"])
            pe.wait_ge(sem("ctx_act"), CTX_ACT["cv_done"])
            for b in range(B):
                r = slice(b % 2 * 64, b % 2 * 64 + 64)
                last = pe.matmul(bank(b % 2)[:, b // 2 * 128:b // 2 * 128 + 128], cv[r, b // 2, :], ck[r, b // 2, :],
                                 start=True, stop=True)
            last.then_inc(sem("ctx_pe"), 1)
            for n in range(4, 8):
                fold(n)
            pe.wait_ge(sem("ctx_dve"), CTX_DVE["gbt_done"])
            pe.wait_ge(sem("ctx_dve"), CTX_DVE["kn_sum"])
            for b in range(B):
                last = pe.matmul(bank(2 + b % 2)[:, b // 2 * 128:b // 2 * 128 + 128], GBT[:, b % 2 * 4 + b // 2, :], wx[:, 2, :],
                                 start=True, stop=True)
            last.then_inc(sem("ctx_pe"), 1)
            def project_u(g, k):
                b, p = k // PAIRS, k % PAIRS
                for h in range(2):
                    w = slice((2 * p + h) * 128, (2 * p + h) * 128 + 128)
                    last = mm3(UB[:, h * S:h * S + S], (Mh[:, w], Ml[:, w]), (xh[b][:, :], xl[b][:, :]))
                last.then_inc(sem("u_ready"), 1)

            def transposes(g, k):
                slot = (k - 2) % 4
                pe.wait_ge(sem("norm_done"), g + 1)
                pe.wait_ge(sem("pt_done"), g + 1)
                for h in range(2):
                    for j, c in enumerate((h * 128, 256 + h * 256, 384 + h * 256)):
                        last = pe.transpose(bank(4 + h)[:, j * 128:j * 128 + 128], P[:, slot, c:c + 128], ident[:, :])
                last.then_inc(sem("t_ready"), 1)

            def weighted_sums(g, k, turn=None):
                p, par = (k - 3) % PAIRS, (k - 3) % 2
                pe.wait_ge(sem("pt_done"), g + 1)
                if p == 0:
                    pe.wait_ge(sem("acc_free"), turn * 2 + k // PAIRS + 2)
                for h in range(2):
                    for dst, blk, half in ((0, 0, 0), (128, 1, 0), (128, 2, 1)):
                        first = p == 0 and h == 0 and dst == 0
                        last = pe.matmul(OB[:, dst:dst + 128], PT[:, par, h, blk * 128:blk * 128 + 128],
                                         VO[:, half, 2 * p + h, :], start=first, stop=(p == PAIRS - 1 and h == 1),
                                         skip_group_check=True)
                last.then_inc(sem("pv_done"), 1)

            pe.wait_ge(sem("fold_lo"), 8)
            pe.wait_ge(sem("consts"), 5)
            pe.wait_ge(sem("acc_free"), 1)
            with pe.Fori(0, B // 2) as i:
                for k in range(STEPS):
                    g = i * STEPS + k
                    b = k // PAIRS
                    if k % PAIRS == 0:
                        pe.wait_ge(sem("xl_done"), i * 2 + b + 1)
                        pe.wait_ge(sem("xh_done"), i * 2 + b + 1)
                    pe.wait_ge(sem("vo_done"), g + 1)
                    project_u(g, k)
                    transposes(g, k)
                    weighted_sums(g, k, i)
                    pe.wait_ge(sem("u_lo"), g + 1)
                    t, q4 = k % 2, k % 8 // 2
                    mm3(UB, (xh[b][:, t * 128:t * 128 + 128], xl[b][:, t * 128:t * 128 + 128]),
                        (NVh[:, q4 * CH:q4 * CH + CH], NVl[:, q4 * CH:q4 * CH + CH])).then_inc(sem("vo_ready"), 1)
                    par = k % 2
                    mm3(bank(2 * par, 256), (xh[b][:, 0:128], xl[b][:, 0:128]),
                        (Uh[:, :].rearrange("p (h c) -> p h c", h=2)[:, :, 0:128],
                         Ul[:, :].rearrange("p (h c) -> p h c", h=2)[:, :, 0:128]))
                    mm3(bank(2 * par + 1), (xh[b][:, 128:256], xl[b][:, 128:256]),
                        (Uh[:, :], Ul[:, :])).then_inc(sem("s_ready"), 1)
            for k in range(3):
                if k < 2:
                    transposes(B * PAIRS + k, k)
                weighted_sums(B * PAIRS + k, k)

            def project_query(c):
                cc = slice(c * CH, c * CH + CH)
                pe.wait_ge(sem("ln_lo"), c + 1)
                mm3(bank(4 + c), (wqh[:, :], wql[:, :]), (XTh[:, cc], XTl[:, cc])).then_inc(sem("q_ready"), 1)

            pe.wait_ge(sem("ctx_dve"), CTX_DVE["wq_lo"])
            in_turn(lambda c: ln_transpose(pe, 0, c), project_query, 2)
            for c in range(NC_):
                pe.wait_ge(sem("q_sq"), c + 1)
                pe.matmul(bank(c), blockones[:, :], SQ[:, c * CH:c * CH + CH], start=True, stop=True).then_inc(sem("q_norm"), 1)
            for c in range(NC_):
                pe.wait_ge(sem("q_done"), c + 1)
                for t in tiles(c):
                    dst = bank(4 + c)[:, t % 4 * 128:t % 4 * 128 + 128]
                    pe.matmul(dst, Q[:, t * 128:t * 128 + 128], G2[:, t // 2, :], start=True, stop=False)
                    last = pe.matmul(dst, ones[0:1, :], brow[0:1, 256:384], start=False, stop=True)
                last.then_inc(sem("b_out"), 1)

            def gate_logits(c):
                cc = slice(c * CH, c * CH + CH)
                pe.wait_ge(sem("ln_lo"), NC_ + c + 1)
                pe.wait_ge(sem("x_added"), c + 1)
                mm3(bank(4 + c), (wrh[:, :], wrl[:, :]), (XTh[:, cc], XTl[:, cc])).then_inc(sem("router_T"), 1)

            pe.wait_ge(sem("ctx_dve"), CTX_DVE["wr_split"])
            in_turn(lambda c: ln_transpose(pe, 1, c, XS, "xs_done"), gate_logits, 2)
            for t in range(T):
                pe.wait_ge(sem("router_out"), t // 4 + 1)
                last = pe.transpose(bank(4)[:, t * 16:t * 16 + 16], LT[:, t * 128:t * 128 + 128], ident[0:16, 0:16])
            last.then_inc(sem("logits_T"), 1)

            def gates_back(c):
                pe.wait_ge(sem("gates_split"), 1)
                if c >= 2:
                    pe.wait_ge(sem("gates_out"), c - 1)
                for t in tiles(c):
                    last = pe.transpose(bank(4 + c % 2)[:, t % 4 * 128:t % 4 * 128 + 128], GI[:, t, :].bitcast(F32), ident[:, :])
                last.then_inc(sem("gates_T"), 1)

            def residual():
                for t in range(T):
                    pe.matmul(bank(t // 4)[:, t % 4 * 128:t % 4 * 128 + 128], X[:, t, :], ident[:, :],
                              start=t % 4 == 0, stop=True, skip_group_check=True)
            residual()

            def down(U, k):
                s, c, n = (k - 3) // 8 % 2, (k - 3) // 2 % 4, (k - 3) % 2
                w = slice(HID + n * 128, HID + n * 128 + 128)
                pe.wait_ge(sem("hl_done"), U + 1)
                return mm3(bank(c), (W0h[s][:, w], W0l[s][:, w]), (HH[:, (k - 3) % 4, :], HL[:, (k - 3) % 4, :]),
                           start=False, skip=True).then_inc(sem("down_done"), 1)

            def up_unit(i, k):
                s, c, n = k // 8, k // 2 % 4, k % 2
                if k % 8 == 0:
                    pe.wait_ge(sem("w_sel"), i * 2 + s + 1)
                    pe.wait_ge(sem("w_split"), i * 2 + s + 3)
                pe.wait_ge(sem("sg_done"), i * 16 + k + 1)
                w, cc = slice(n * 128, n * 128 + 128), slice(c * CH, c * CH + CH)
                mm3(bank(6 + n), (W0h[s][:, w], W0l[s][:, w]), (XTh[:, cc], XTl[:, cc])).then_inc(sem("up_ready"), 1)

            for k in range(16):
                up_unit(0, k)
                if k >= 3:
                    down(k, k)
                if k in GATES_PLACED:
                    gates_back(GATES_PLACED.index(k))
            pe.wait_ge(sem("gates_out"), NC_)
            with pe.Fori(1, E0 // 2) as i:
                for k in range(16):
                    s, c, n = k // 8, k // 2 % 4, k % 2
                    up_unit(i, k)
                    down(i * 16 + k, k)
                    if n == 0:
                        pe.matmul(bank(4 + c % 2), esel[s][:, :], SELT[:, c * CH:c * CH + CH], start=True, stop=True).then_inc(sem("gb_ready"), 1)
            for k in range(3):
                down(E0 * 8 + k, k)
            for t in range(T):
                pe.wait_ge(sem("sums_out"), t // 4 + 1)
                last = pe.transpose(bank(4 + t // 4)[:, t % 4 * 128:t % 4 * 128 + 128], OT[:, t * 128:t * 128 + 128], ident[:, :])
                if t % 4 == 3:
                    last.then_inc(sem("sums_T"), 1)
            for c in range(NC_):
                ln_transpose(pe, 2, c)
            pe.wait_ge(sem("l1_split"), 5)
            for t in range(T):
                p, tok = t % 2, slice(t * 128, t * 128 + 128)
                pe.wait_ge(sem("ln_lo"), 2 * NC_ + t // 4 + 1)
                for n, b0, what, free in ((0, 4, "dq_ready", "qs_done"), (2, 6, "dz_ready", "z_pos"), (1, 2, "dk_ready", "pr_done")):
                    if t < 2 and n == 1:
                        pe.wait_ge(sem("ln_lo"), 2 * NC_ + 3 + p)
                    if t >= 2:
                        pe.wait_ge(sem(free), t - 1)
                    w = slice(n * CH, n * CH + CH)
                    if n == 2:
                        pe.matmul(bank(b0 + p), onesr[:, :], abr[:, :], start=True, stop=False)
                    mm3(bank(b0 + p), (XTh[:, tok], XTl[:, tok]), (wdh[:, w], wdl[:, w]), start=n < 2).then_inc(sem(what), 1)
                if t % 4 == 3:
                    c = t // 4
                    cc = slice(c * CH, c * CH + CH)
                    w = slice(3 * CH, 3 * CH + 128)
                    if c >= 2:
                        pe.wait_ge(sem("vp_done"), 2 * c - 2)
                    mm3(bank(c % 2), (wdh[:, w], wdl[:, w]), (XTh[:, cc], XTl[:, cc])).then_inc(sem("dv_ready"), 1)
            pe.wait_ge(sem("l1_in"), 16 * 7)
            pe.wait_ge(sem("qs_done"), T)
            pe.matmul(bank(4), wqe[:, 0, :], ctxT[:, :], start=True, stop=True).then_inc(sem("ctx_pe"), 1)
            pe.wait_ge(sem("z_pos"), T)
            for b in range(B):
                last = pe.matmul(bank(6 + b // 4)[0:64, b % 4 * 128:b % 4 * 128 + 128], ctxT[:, b * SC:b * SC + SC], wqe[:, 0, :],
                                 start=True, stop=True)
            last.then_inc(sem("ctx_pe"), 1)
            pe.wait_ge(sem("ctx_act"), CTX_ACT["ke_done"])
            pe.matmul(bank(5), wqe[:, 1, :], kTe[:, :], start=True, stop=True).then_inc(sem("ctx_pe"), 1)
            for n in (1, 0):
                pe.wait_ge(sem("ab_placed"), 4 - 2 * n)
                for r in range(2):
                    last = pe.transpose(bank(4)[0:64, n * S + r * 128:n * S + r * 128 + 128],
                                        ABt[:, r, n, :, :].rearrange("p h b -> p (h b)"), ident[:, :])
            last.then_inc(sem("ab_T"), 1)
            pe.wait_ge(sem("pr_done"), T)
            pe.wait_ge(sem("vp_done"), 2 * NC_)
            residual()

            def product(base, src, w, done):
                for h in range(H1):
                    last = pe.matmul(PS[:, cols(base, S)], w[:, :], src[:, h * S:h * S + S],
                                     start=False, stop=h == H1 - 1, skip_group_check=True)
                last.then_inc(sem(done), 1)

            def states_product(g, par):
                pe.wait_ge(sem("scan1_done"), g + 1)
                product(g * S - S, r0b[1 - par], wo1, "y0_done")

            def floors_product(g, par):
                pe.wait_ge(sem("scan2_done"), g + 1)
                product(g * S - 2 * S, rb[par], wo1e, "y1_done")

            def weights_out(i, k):
                g = i * 2 + k
                pe.wait_ge(sem("dsel_done"), g + 1)
                for r in range(4):
                    pe.wait_ge(sem("w_copied"), g * 4 + r + 1)
                    for h in range(2):
                        last = pe.matmul(bank(4 + r % 2)[:, h * S:h * S + S], dsel[k][:, 2 * r + h, :], WUr[:, 0, :], start=True, stop=True)
                    last.then_inc(sem("w_bc"), 1)
                    pe.wait_ge(sem("qr_done"), g * 4 + r + 1)
                    for h in range(2):
                        last = pe.matmul(bank(6 + r % 2)[:, h * S:h * S + S], dsel[k][:, 2 * r + h, :], WUr[:, 1, :], start=True, stop=True)
                    last.then_inc(sem("u_bc"), 1)

            def sums_back(c):
                pe.wait_ge(sem("sums_out"), NC_ + c + 1)
                for t in tiles(c):
                    last = pe.transpose(sum_bank(t), OD[:, t * 128:t * 128 + 128], ident[:, :])
                last.then_inc(sem("sums_T"), 1)

            pe.wait_ge(sem("wu_done"), 1)
            pe.wait_ge(sem("ab_in"), 1)
            pe.wait_ge(sem("ctx_act"), CTX_ACT["kk_done"])
            weights_out(0, 0)
            weights_out(0, 1)
            states_product(1, 1)
            with pe.Fori(1, B // 2) as i:
                for k in range(2):
                    weights_out(i, k)
                    states_product(i * 2 + k, k)
                    floors_product(i * 2 + k, k)
            pe.wait_ge(sem("w_copied"), 4 * B + 2)
            pe.wait_ge(sem("qr_done"), 4 * B + 2)
            for c in range(3):
                sums_back(c)
            states_product(B, 0)
            floors_product(B, 0)
            floors_product(B + 1, 1)
            sums_back(3)
            def context_scores(c):
                pe.wait_ge(sem("ln_hi"), 3 * NC_ + c + 1)
                for t in tiles(c):
                    b = t // 2
                    last = pe.matmul(bank(4 + t // 8)[:, t % 8 * SC:t % 8 * SC + SC], XTf[:, t * 128:t * 128 + 128],
                                     KK[:, b * SC:b * SC + SC], start=True, stop=True)
                last.then_inc(sem("es_ready"), 1)

            in_turn(lambda c: ln_transpose(pe, 3, c), context_scores, 1)
            for t in range(T):
                pe.wait_ge(sem("e_prob"), t // 8 + 1)
                last = pe.transpose(bank(t // 4)[0:64, t % 4 * 128:t % 4 * 128 + 128], SE[:, t, :], ident[:, :])
                if t % 4 == 3:
                    last.then_inc(sem("e_T"), 1)
            for t in range(T):
                pe.wait_ge(sem("e_pt"), t // 4 + 1)
                last = pe.matmul(bank(4 + t // 4)[:, t % 4 * 128:t % 4 * 128 + 128], PE_T[:, t * 128:t * 128 + 128], vE[:, t // 2, :],
                                 start=True, stop=True)
                if t % 4 == 3:
                    last.then_inc(sem("e_out"), 1)
            def router_logits(c):
                cc = slice(c * CH, c * CH + CH)
                pe.wait_ge(sem("ln_lo"), 3 * NC_ + c + 1)
                mm3(bank(4 + c), (wr1h[:, :], wr1l[:, :]), (XTh[:, cc], XTl[:, cc])).then_inc(sem("router_T"), 1)

            def logits_by_token(h):
                pe.wait_ge(sem("router_out"), NC_ + 2 * h + 2)
                for t in range(8 * h, 8 * h + 8):
                    last = pe.transpose(bank(4 + h)[:, t % 8 * E1:t % 8 * E1 + E1], FL[:, t * 128:t * 128 + 128], ident[0:64, 0:64])
                last.then_inc(sem("logits_T"), 1)

            def router_step(c):
                router_logits(c)
                if c % 2:
                    logits_by_token(c // 2)

            in_turn(lambda c: ln_transpose(pe, 4, c), router_step, 2)
            residual()
            def shared_down(c):
                pe.wait_ge(sem("sh_hl"), c + 1)
                mm3(bank(c), (wshh[:, 256:384], wshl[:, 256:384]), (FHH[:, c % 2, :], FHL[:, c % 2, :]),
                    start=False, skip=True).then_inc(sem("sh_down"), 1)

            def gate_product(k):
                s, c = k // 4, k % 4
                return (W3h[s][:, 0:128], W3l[s][:, 0:128]), (XTh[:, c * CH:c * CH + CH], XTl[:, c * CH:c * CH + CH])

            def up_product(k):
                s, c = k // 4, k % 4
                return (W3h[s][:, 128:256], W3l[s][:, 128:256]), (XTh[:, c * CH:c * CH + CH], XTl[:, c * CH:c * CH + CH])

            def early_unit(k):
                if k % 4 == 0:
                    pe.wait_ge(sem("f_split"), k // 4 + 3)
                pe.wait_ge(sem("f_exp"), 2)
                pe.wait_ge(sem("fg_done"), k + 2)
                mm3(bank(4), *gate_product(k)).then_inc(sem("g_ready"), 1)
                pe.wait_ge(sem("ft_done"), k + 2)
                mm3(bank(5), *up_product(k)).then_inc(sem("fu_ready"), 1)

            for c in range(NC_):
                cc = slice(c * CH, c * CH + CH)
                if c:
                    pe.wait_ge(sem("sh_sg"), c)
                mm3(bank(6), (wshh[:, 0:128], wshl[:, 0:128]), (XTh[:, cc], XTl[:, cc])).then_inc(sem("sh_g"), 1)
                if c:
                    pe.wait_ge(sem("sh_h"), c)
                mm3(bank(7), (wshh[:, 128:256], wshl[:, 128:256]), (XTh[:, cc], XTl[:, cc])).then_inc(sem("sh_u"), 1)
                for k in EARLY[c]:
                    early_unit(k)
                if c:
                    shared_down(c - 1)
            shared_down(NC_ - 1)
            pe.wait_ge(sem("sh_h"), NC_)
            pe.wait_ge(sem("ft_done"), 8 + 2)
            for t in range(T):
                pe.wait_ge(sem("gates_split"), 2 + t // 8)
                last = pe.transpose(bank(4 + t // 4)[:, t % 4 * 128:t % 4 * 128 + 128], GI1[:, t, :].bitcast(F32), ident[:, :])
                if t % 4 == 3:
                    last.then_inc(sem("gates_T"), 1)
            pe.wait_ge(sem("gates_out"), NC_ + NC_)

            def f_down(U, k):
                s, c = (k - 2) // 4 % 2, (k - 2) % 4
                pe.wait_ge(sem("fhl_done"), U + 1)
                mm3(bank(c), (W3h[s][:, 256:384], W3l[s][:, 256:384]), (FHH[:, (k - 2) % 4, :], FHL[:, (k - 2) % 4, :]),
                    start=False, skip=True).then_inc(sem("fdown_done"), 1)

            def gate_weights(U, k):
                s, c = k // 4, k % 4
                pe.wait_ge(sem("fh_done"), U + 1)
                pe.matmul(bank(7), fsel[s][:, :, :].rearrange("p e i -> p (e i)"), SELT1[:, c * CH:c * CH + CH],
                          start=True, stop=True).then_inc(sem("fgb_ready"), 1)

            for k in range(8):
                if k % 4 == 0:
                    pe.wait_ge(sem("f_sel"), k // 4 + 1)
                gate_weights(k, k)
                if k >= 2:
                    f_down(k, k)
            with pe.Fori(1, E1 // 4) as i:
                for k in range(8):
                    U = i * 8 + k
                    if k % 4 == 0:
                        pe.wait_ge(sem("f_sel"), i * 2 + k // 4 + 1)
                        pe.wait_ge(sem("f_split"), i * 2 + k // 4 + 3)
                    pe.wait_ge(sem("fg_done"), U + 1)
                    mm3(bank(4 + k % 2), *gate_product(k)).then_inc(sem("g_ready"), 1)
                    pe.wait_ge(sem("ft_done"), U + 2)
                    mm3(bank(6), *up_product(k)).then_inc(sem("fu_ready"), 1)
                    f_down(U, k)
                    gate_weights(U, k)
            for k in range(2):
                f_down(E1 * 2 + k, k)
            for t in range(T):
                pe.wait_ge(sem("sums_out"), 2 * NC_ + t // 4 + 1)
                last = pe.transpose(bank(4 + t // 4)[:, t % 4 * 128:t % 4 * 128 + 128], OT1[:, t * 128:t * 128 + 128], ident[:, :])
                if t % 4 == 3:
                    last.then_inc(sem("sums_T"), 1)


def host_layout(v):
    f = np.ascontiguousarray
    x, c = v["x"].reshape(N, D), v["ctx_1024"].reshape(B * SC, D)
    tiles = lambda m: m.reshape(-1, 128, m.shape[-1]).transpose(1, 0, 2)
    lay = lambda *m: np.stack(m, axis=1)
    both = lambda n: np.concatenate([v["L0_ffn_" + n + "_s"], v["L0_ffn_" + n]])
    return {k: f(m) for k, m in {
        "x": tiles(x), "xT": x.T, "ctxT": c.T,
        "w64q": v["L0_attn_W_Q"].transpose(1, 0, 2), "w64k": v["L0_attn_W_K"].transpose(1, 0, 2),
        "w64v": v["L0_attn_W_V"].transpose(1, 0, 2), "w64o": v["L0_attn_W_O"].transpose(2, 0, 1),
        "wx": lay(*(v["L0_xattn_W" + n].T for n in "kvoq")),
        "brow": np.concatenate([v["L0_xattn_b" + n] for n in "kvo"])[None],
        "bq": v["L0_xattn_bq"][:, None],
        "wr0": v["L0_ffn_router_w"], "rw": both("rms_w").T,
        "w12": np.concatenate([both("w1"), both("w2").reshape(E0, 2, 128, D).transpose(0, 2, 1, 3).reshape(E0, 128, HID)], axis=2),
        "wd": np.concatenate([v["L1_attn_W_" + n].T for n in ("q", "k", "alpha_w", "v")], axis=1),
        "abias": v["L1_attn_W_alpha_b"][None], "wo1": v["L1_attn_W_o"].T,
        "wqe": lay(v["L1_xattn_Wq"].T, v["L1_xattn_Wq"]),
        "wr1": v["L1_ffn_router_w"].T, "ebias": np.broadcast_to(v["L1_ffn_e_bias"][None], (128, E1)),
        "wsh": np.concatenate([v["L1_ffn_S" + n] for n in ("Wg", "Wu", "Wd")], axis=1),
        "w3": np.concatenate([v["L1_ffn_" + n].reshape(E1 // 2, 2, D, I1).transpose(0, 2, 1, 3).reshape(E1 // 2, D, 128)
                              for n in ("Wg", "Wu")] + [v["L1_ffn_Wd"].reshape(E1 // 2, 128, D)], axis=2),
    }.items()}


def kernel(**inputs):
    import concourse.bacc as bacc
    from concourse.bass_utils import run_bass_kernel_spmd

    nc = bacc.Bacc("TRN2", target_bir_lowering=False, num_devices=1)
    arrays = host_layout({k: np.asarray(v) for k, v in inputs.items()})
    drams = {k: nc.dram_tensor("in_" + k, m.shape, mybir.dt.from_np(m.dtype), kind="ExternalInput").ap()
             for k, m in arrays.items()}
    out = nc.dram_tensor("out", (128, T, D), F32, kind="ExternalOutput").ap()
    decoder_program(nc, drams, out)
    got = run_bass_kernel_spmd(nc, [{"in_" + k: m for k, m in arrays.items()}], core_ids=[0])
    return got.results[0]["out"].transpose(1, 0, 2).reshape(B, S, D)
```
